# Optimizing a Trainium2 kernel written in Bass

```python
import numpy as np
import jax
import jax.numpy as jnp

def _softmax(x, axis=-1):
    return jax.nn.softmax(x, axis=axis)

def _gelu(x):
    return jax.nn.gelu(x, approximate=True)

def _silu(x):
    return jax.nn.silu(x)

def _sigmoid(x):
    return jax.nn.sigmoid(x)

def _layernorm(x, axis=-1, eps=1e-05):
    m = jnp.mean(x, axis=axis, keepdims=True)
    v = jnp.var(x, axis=axis, keepdims=True)
    return (x - m) / jnp.sqrt(v + eps)

def _scatter_add(tgt, idx, src, axis=0):
    return tgt.at[idx].add(src)

def _segment_sum(src, seg, n):
    return jax.ops.segment_sum(src, seg, n)
kernel_name = 'mk_hybrid_d1_jaxref_r4_c1fb6c'

def setup_inputs(seed: int=0):
    np.random.seed(seed)
    _w = jnp.asarray

    def _L0_attn_a_setup():
        import math
        import jax, jax.numpy as jnp
        import numpy as np
        D_MODEL = 256
        N_HEADS = 16
        HEAD_DIM = D_MODEL // N_HEADS
        B, L = (1, 1024)

        def _slopes(n_heads):
            ratio = 2.0 ** (-8.0 / n_heads)
            return jnp.asarray([ratio ** (i + 1) for i in range(n_heads)], dtype=jnp.float32)
        key = jax.random.key(seed)
        ks = jax.random.split(key, 5)
        scale = 1.0 / math.sqrt(D_MODEL)
        return {'x': jax.random.normal(ks[0], (B, L, D_MODEL), dtype=jnp.float32), 'q_w': jax.random.normal(ks[1], (D_MODEL, D_MODEL), dtype=jnp.float32) * scale, 'k_w': jax.random.normal(ks[2], (D_MODEL, D_MODEL), dtype=jnp.float32) * scale, 'v_w': jax.random.normal(ks[3], (D_MODEL, D_MODEL), dtype=jnp.float32) * scale, 'o_w': jax.random.normal(ks[4], (D_MODEL, D_MODEL), dtype=jnp.float32) * scale}
    _L0_attn_a_in = _L0_attn_a_setup()

    def _L0_attn_b_setup():
        import jax, jax.numpy as jnp
        import numpy as np
        import math
        B, S, D = (4, 512, 256)
        H = 16
        HD = D // H
        DL = 64
        LAMBDA_DECAY = 0.01
        key = jax.random.key(seed)
        ks = jax.random.split(key, 8)
        sc = lambda fan_in: 1.0 / math.sqrt(fan_in)
        return {'x': jax.random.normal(ks[0], (B, S, D), dtype=jnp.float32), 'W_q': jax.random.normal(ks[1], (D, D), dtype=jnp.float32) * sc(D), 'W_k': jax.random.normal(ks[2], (D, D), dtype=jnp.float32) * sc(D), 'W_v': jax.random.normal(ks[3], (D, D), dtype=jnp.float32) * sc(D), 'W_o': jax.random.normal(ks[4], (D, D), dtype=jnp.float32) * sc(D), 'W_down_kv': jax.random.normal(ks[5], (D, DL), dtype=jnp.float32) * sc(D), 'W_up_k': jax.random.normal(ks[6], (DL, D), dtype=jnp.float32) * sc(DL), 'W_up_v': jax.random.normal(ks[7], (DL, D), dtype=jnp.float32) * sc(DL)}
    _L0_attn_b_in = _L0_attn_b_setup()

    def _L0_ffn_setup():
        import jax, jax.numpy as jnp
        import numpy as np
        H = 256
        I = 128
        E = 32
        TOP_K = 6
        N_GROUP = 8
        TOPK_GROUP = 4
        SCALE = 2.5
        N_SHARED = 2
        SI = I * N_SHARED
        B, S = (2, 256)
        key = jax.random.key(seed)
        ks = jax.random.split(key, 8)
        x = jax.random.normal(ks[0], (B, S, H), jnp.float32)
        gate_weight = jax.random.normal(ks[1], (E, H), jnp.float32) * 0.02
        e_score_correction_bias = jax.random.normal(ks[2], (E,), jnp.float32) * 0.01
        experts_gate_up = jax.random.normal(ks[3], (E, 2 * I, H), jnp.float32) * 0.02
        experts_down = jax.random.normal(ks[4], (E, H, I), jnp.float32) * 0.02
        shared_gate_w = jax.random.normal(ks[5], (SI, H), jnp.float32) * 0.02
        shared_up_w = jax.random.normal(ks[6], (SI, H), jnp.float32) * 0.02
        shared_down_w = jax.random.normal(ks[7], (H, SI), jnp.float32) * 0.02
        return {'x': x, 'gate_weight': gate_weight, 'e_score_correction_bias': e_score_correction_bias, 'experts_gate_up': experts_gate_up, 'experts_down': experts_down, 'shared_gate_w': shared_gate_w, 'shared_up_w': shared_up_w, 'shared_down_w': shared_down_w}
    _L0_ffn_in = _L0_ffn_setup()
    _d = {'L0_attn_a_x': _L0_attn_a_in['x'], 'L0_attn_a_q_w': _L0_attn_a_in['q_w'], 'L0_attn_a_k_w': _L0_attn_a_in['k_w'], 'L0_attn_a_v_w': _L0_attn_a_in['v_w'], 'L0_attn_a_o_w': _L0_attn_a_in['o_w'], 'L0_attn_b_W_q': _L0_attn_b_in['W_q'], 'L0_attn_b_W_k': _L0_attn_b_in['W_k'], 'L0_attn_b_W_v': _L0_attn_b_in['W_v'], 'L0_attn_b_W_o': _L0_attn_b_in['W_o'], 'L0_attn_b_W_down_kv': _L0_attn_b_in['W_down_kv'], 'L0_attn_b_W_up_k': _L0_attn_b_in['W_up_k'], 'L0_attn_b_W_up_v': _L0_attn_b_in['W_up_v'], 'L0_ffn_gate_weight': _L0_ffn_in['gate_weight'], 'L0_ffn_e_score_correction_bias': _L0_ffn_in['e_score_correction_bias'], 'L0_ffn_experts_gate_up': _L0_ffn_in['experts_gate_up'], 'L0_ffn_experts_down': _L0_ffn_in['experts_down'], 'L0_ffn_shared_gate_w': _L0_ffn_in['shared_gate_w'], 'L0_ffn_shared_up_w': _L0_ffn_in['shared_up_w'], 'L0_ffn_shared_down_w': _L0_ffn_in['shared_down_w']}
    _x0 = _d['L0_attn_a_x']
    _d['L0_attn_a_x'] = jax.random.normal(jax.random.fold_in(jax.random.key(seed), 1), (8, 512, 256), dtype=_x0.dtype)
    del _x0
    return _d

def reference(L0_attn_a_x, L0_attn_a_q_w, L0_attn_a_k_w, L0_attn_a_v_w, L0_attn_a_o_w, L0_attn_b_W_q, L0_attn_b_W_k, L0_attn_b_W_v, L0_attn_b_W_o, L0_attn_b_W_down_kv, L0_attn_b_W_up_k, L0_attn_b_W_up_v, L0_ffn_gate_weight, L0_ffn_e_score_correction_bias, L0_ffn_experts_gate_up, L0_ffn_experts_down, L0_ffn_shared_gate_w, L0_ffn_shared_up_w, L0_ffn_shared_down_w):

    def _L0_attn_a_ref(x, q_w, k_w, v_w, o_w):
        import math
        import jax, jax.numpy as jnp
        import numpy as np
        D_MODEL = 256
        N_HEADS = 16
        HEAD_DIM = D_MODEL // N_HEADS
        B, L = (1, 1024)

        def _slopes(n_heads):
            ratio = 2.0 ** (-8.0 / n_heads)
            return jnp.asarray([ratio ** (i + 1) for i in range(n_heads)], dtype=jnp.float32)
        b, l, _ = x.shape

        def proj(w):
            return (x @ w).reshape(b, l, N_HEADS, HEAD_DIM).transpose(0, 2, 1, 3)
        q, k, v = (proj(q_w), proj(k_w), proj(v_w))
        scale = math.sqrt(HEAD_DIM)
        scores = jnp.einsum('bhid,bhjd->bhij', q, k) / scale
        pos = jnp.arange(l)
        distance = jnp.abs(pos[None, :] - pos[:, None]).astype(jnp.float32)
        alibi = -distance[None, :, :] * _slopes(N_HEADS)[:, None, None]
        scores = scores + alibi[None]
        causal = pos[None, :] <= pos[:, None]
        scores = jnp.where(causal[None, None], scores, -jnp.inf)
        attn = jax.nn.softmax(scores, axis=-1)
        out = jnp.einsum('bhij,bhjd->bhid', attn, v)
        out = out.transpose(0, 2, 1, 3).reshape(b, l, D_MODEL)
        return out @ o_w

    def _L0_attn_b_ref(x, W_q, W_k, W_v, W_o, W_down_kv, W_up_k, W_up_v):
        import jax, jax.numpy as jnp
        import numpy as np
        import math
        B, S, D = (4, 512, 256)
        H = 16
        HD = D // H
        DL = 64
        LAMBDA_DECAY = 0.01
        b, s, d = x.shape
        q = x @ W_q
        k = x @ W_k
        v = x @ W_v
        latent_kv = (k + v) @ W_down_kv
        k_rec = (latent_kv @ W_up_k).reshape(b, s, H, HD).transpose(0, 2, 1, 3)
        v_rec = (latent_kv @ W_up_v).reshape(b, s, H, HD).transpose(0, 2, 1, 3)
        qh = q.reshape(b, s, H, HD).transpose(0, 2, 1, 3)
        scores = jnp.einsum('bhqd,bhkd->bhqk', qh, k_rec) / math.sqrt(d)
        t = jnp.arange(s, dtype=jnp.float32)
        decay = jnp.exp(-LAMBDA_DECAY * jnp.abs(t[:, None] - t[None, :]))
        scores = scores * decay[None, None, :, :]
        attn = jax.nn.softmax(scores, axis=-1)
        out = jnp.einsum('bhqk,bhkd->bhqd', attn, v_rec)
        out = out.transpose(0, 2, 1, 3).reshape(b, s, d)
        return out @ W_o

    def _L0_ffn_ref(x, gate_weight, e_score_correction_bias, experts_gate_up, experts_down, shared_gate_w, shared_up_w, shared_down_w):
        import jax, jax.numpy as jnp
        import numpy as np
        H = 256
        I = 128
        E = 32
        TOP_K = 6
        N_GROUP = 8
        TOPK_GROUP = 4
        SCALE = 2.5
        N_SHARED = 2
        SI = I * N_SHARED
        B, S = (2, 256)
        b, s, h = x.shape
        xf = x.reshape(-1, h)
        T = xf.shape[0]
        logits = xf.astype(jnp.float32) @ gate_weight.astype(jnp.float32).T
        scores = jax.nn.sigmoid(logits)
        sfc = scores + e_score_correction_bias[None, :]
        gs = E // N_GROUP
        group_scores = sfc.reshape(T, N_GROUP, gs).max(axis=-1)
        _, gidx = jax.lax.top_k(group_scores, TOPK_GROUP)
        gmask = jnp.zeros((T, N_GROUP), bool).at[jnp.arange(T)[:, None], gidx].set(True)
        smask = jnp.repeat(gmask, gs, axis=1)
        masked = jnp.where(smask, sfc, 0.0)
        _, topk_idx = jax.lax.top_k(masked, TOP_K)
        tw = jnp.take_along_axis(scores, topk_idx, axis=1)
        tw = tw / (tw.sum(-1, keepdims=True) + 1e-20)
        tw = (tw * SCALE).astype(xf.dtype)
        combine = jnp.zeros((T, E), xf.dtype).at[jnp.arange(T)[:, None], topk_idx].add(tw)

        def expert_step(acc, inp):
            gu, dn, c = inp
            g = xf @ gu[:I].T
            u = xf @ gu[I:].T
            o = jax.nn.silu(g) * u @ dn.T
            return (acc + c[:, None] * o, None)
        routed, _ = jax.lax.scan(expert_step, jnp.zeros_like(xf), (experts_gate_up, experts_down, combine.T))
        sh = jax.nn.silu(xf @ shared_gate_w.T) * (xf @ shared_up_w.T)
        shared_out = sh @ shared_down_w.T
        return (routed + shared_out).reshape(b, s, h)
    x = L0_attn_a_x
    x = x + _L0_attn_a_ref(_layernorm(x, axis=-1), L0_attn_a_q_w, L0_attn_a_k_w, L0_attn_a_v_w, L0_attn_a_o_w)
    x = x + _L0_ffn_ref(_layernorm(x, axis=-1), L0_ffn_gate_weight, L0_ffn_e_score_correction_bias, L0_ffn_experts_gate_up, L0_ffn_experts_down, L0_ffn_shared_gate_w, L0_ffn_shared_up_w, L0_ffn_shared_down_w)
    x = x + _L0_attn_b_ref(_layernorm(x, axis=-1), L0_attn_b_W_q, L0_attn_b_W_k, L0_attn_b_W_v, L0_attn_b_W_o, L0_attn_b_W_down_kv, L0_attn_b_W_up_k, L0_attn_b_W_up_v)
    x = x + _L0_ffn_ref(_layernorm(x, axis=-1), L0_ffn_gate_weight, L0_ffn_e_score_correction_bias, L0_ffn_experts_gate_up, L0_ffn_experts_down, L0_ffn_shared_gate_w, L0_ffn_shared_up_w, L0_ffn_shared_down_w)
    return x

_drawn_inputs = setup_inputs


def setup_inputs(seed=0):
    import zlib

    import numpy as np

    out = dict(_drawn_inputs(seed))
    spreads = {}
    factors = {'L0_ffn_gate_weight': 24.155, 'L0_ffn_e_score_correction_bias': 104.291}
    for name, (base, spread) in spreads.items():
        noise = np.random.default_rng([zlib.crc32(name.encode()), seed]).standard_normal(out[name].shape)
        drawn = base * np.exp(spread * noise) if base else spread * noise
        out[name] = jnp.asarray(drawn.astype(out[name].dtype))
    for name, factor in factors.items():
        out[name] = (out[name] * factor).astype(out[name].dtype)
    return out
```

```python
from contextlib import ExitStack, contextmanager

import numpy as np

import concourse.bass as bass
from concourse import mybir

F32 = mybir.dt.float32
F32R = mybir.dt.float32r
BF16 = mybir.dt.bfloat16
I32 = mybir.dt.int32
U32 = mybir.dt.uint32
ALU = mybir.AluOpType
ACT = mybir.ActivationFunctionType
AX = mybir.AxisListType

P = 128
B, L, D = 8, 512, 256
T = B * L // P
TB = L // P
DC = D // P
H, HD = 16, 16
G, HG = 4, 4
E, FI = 32, 128
FS = 2 * FI
TOPK, NGROUP, TOPG = 6, 8, 4
EG = E // NGROUP
ROUTE_SCALE = 2.5
LDECAY = 0.01
EPS = 1e-5
NEG = -1e30
LOW, HIGH = -3e38, 3e38
CAP = T * P + P
NSLOT = T * TOPK + E
XROWS = E * CAP + P
YROWS = NSLOT * P


def wait(eng, sem, value):
    if isinstance(value, int) and value <= 0:
        return
    eng.wait_ge(sem, value)


def wait_alone(eng, sem, value):
    if isinstance(value, int) and value <= 0:
        return
    eng.wait_ge(sem, value)
    eng.nop(nofuse=True)


class Ring:

    def __init__(self, banks, plan):
        self.banks, self.plan = banks, plan
        self.at, self.held = 0, [None] * len(banks)

    def __getitem__(self, key):
        return self.banks[self.plan.index(key) % len(self.banks)]

    def take(self, pe, key, freed):
        assert self.plan[self.at] == key, (self.plan[self.at], key)
        i = self.at % len(self.banks)
        if self.held[i] is not None:
            pe.wait_ge(*self.held[i])
        self.held[i] = freed
        self.at += 1
        return self.banks[i]


def attention(nc, sem, decayed, x_res, ident, identb, maskb, w_dram, tab, qk_dram, m_dram):
    tag = "b" if decayed else "a"
    forms = 2 if decayed else 1
    qscale = 1.0 / 16.0 if decayed else 1.0 / 4.0
    NQK = 2 * (forms + 1)
    NHL = 3 if decayed else 4
    UNITS = 2 * TB * forms
    NP1 = H * TB
    NP2 = G * UNITS
    duos = [(kb, f) for kb in range(TB) for f in range(forms)]
    ND = len(duos)
    NMI = 2 * forms * forms

    parts = ([(f, half) for half in range(2) for f in range(forms)] + [(forms, half) for half in range(2)])
    stores = [3 if f == forms else 2 for f, _ in parts]

    def stored(buf, n, j):
        every = sum(c for i, c in enumerate(stores) if i % NHL == buf)
        return every * n + sum(c for i, c in enumerate(stores[:j]) if i % NHL == buf)

    def span(kb, f):
        return (kb * P, L) if f == 0 else (0, (kb + 1) * P)

    def plan_front(n):
        return [("xT", n, 0), ("xT", n, 1), ("q", n, 0), ("q", n, 1), ("k", n, 0), ("k", n, 1)]

    def plan_v(n):
        return [("v", n, 0), ("v", n, 1)]

    def plan_p1(n, g):
        return [("p1", n, g, h, qb) for h in range(HG) for qb in range(TB)]

    def plan_back(n):
        return [("onT", n, 0), ("onT", n, 1), ("y", n, 0), ("y", n, 1)]

    plan_first = plan_front(1) + plan_v(1) + plan_p1(1, 0) + [("mT", 1, 0)]
    plan_last = (plan_p1(0, 1) + [("mT", 0, 1)] + plan_p1(0, 2) + [("oT", 0, 0), ("mT", 0, 2)] + plan_p1(0, 3)
                 + [("oT", 0, 1), ("mT", 0, 3), ("oT", 0, 2), ("oT", 0, 3)] + plan_back(0))
    plan_round = (plan_p1(0, 1) + [("mT", 0, 1)] + plan_front(1) + plan_p1(0, 2) + [("oT", 0, 0), ("mT", 0, 2)]
                  + plan_p1(0, 3) + [("oT", 0, 1), ("mT", 0, 3), ("oT", 0, 2)] + plan_v(1) + [("oT", 0, 3)]
                  + plan_p1(1, 0) + [("mT", 1, 0)] + plan_back(0))

    with ExitStack() as ctx:
        def sb(name, shape, dt=F32):
            return ctx.enter_context(nc.sbuf_tensor(f"{name}_{tag}", shape, dt))

        def ps(name, shape):
            return ctx.enter_context(nc.psum_tensor(f"{name}_{tag}", shape, F32))

        def s(name):
            return sem(f"{name}_{tag}")

        wq, wk, wv, wo = (sb(n, [P, DC, D]) for n in ("wq", "wk", "wv", "wo"))
        qst = [[sb(f"qst{f}_{g}", [P, HG, L], F32R) for g in range(G)] for f in range(forms)]
        kst = [sb(f"kst{g}", [P, HG, L], F32R) for g in range(G)]
        xn = sb("xn", [P, TB, D])
        xT = sb("xT", [P, DC, L])
        hi = [sb(f"hi{i}", [P, L], F32R) for i in range(NHL)]
        lo = [sb(f"lo{i}", [P, L], F32R) for i in range(NHL)]
        v = sb("v", [P, TB, H, 32])
        pt = [[sb(f"pt{i}{j}", [P, 2, L]) for j in range(2)] for i in range(2)]
        oT = sb("oT", [P, L])
        on = sb("on", [P, TB, D])
        onT = sb("onT", [P, DC, L])
        mcol = sb("mcol", [P, HG, TB])
        mhl = sb("mhl", [HG * TB, 2, P], F32R)
        rec = sb("rec", [P, TB, HG])
        stats = sb("stats", [P, TB, 6])
        mv = sb("mv", [P, TB, 2])
        ve = sb("ve", [P, TB])
        rstd = sb("rstd", [P, TB])
        mhalf = sb("mhalf", [P, TB])
        if decayed:
            qf = [sb(f"qf{i}", [P, L]) for i in range(2)]
            efac = sb("efac", [P, 2, L])
            dwin = sb("dwin", [P, 7 * P])
            sfac = sb("sfac", [P, 2, TB])
            mfac = sb("mfac", [P, TB])
            mpost = sb("mpost", [P, HG, TB])
        else:
            cwin = sb("cwin", [P, L])
            mpost = mcol

        rbank = [ps(f"r{i}", [P, 512]) for i in range(3)]
        sbank = [ps(f"s{i}", [P, 2, 512]) for i in range(2)]
        obank = ps("o", [P, 512])
        ring_first, ring_round, ring_last = (Ring(rbank, p) for p in (plan_first, plan_round, plan_last))

        loaded = s("loaded")
        tabs = s("tabs")
        half_set = s("half_set")
        v_set = s("v_set")
        ln = s("ln")
        var_ready = s("var_ready")
        rstd_ready = s("rstd_ready")
        xn_ready = s("xn_ready")
        xT_mm = s("xT_mm")
        xT_a, xT_v = s("xT_a"), s("xT_v")
        qk_mm = s("qk_mm")
        qf_ready = s("qf_ready")
        hi_ready = s("hi_ready")
        lo_ready = s("lo_ready")
        hl_out = [s(f"hl_out{i}") for i in range(NHL)]
        st_ready = [s(f"st_ready{g}") for g in range(G)]
        v_mm = s("v_mm")
        v_ready = s("v_ready")
        p1_mm = s("p1_mm")
        p1_max = s("p1_max")
        m_ready = s("m_ready")
        mT_mm = s("mT_mm")
        mh_ready = s("mh_ready")
        ml_ready = s("ml_ready")
        m_out = s("m_out")
        m_in = s("m_in")
        s_mm = s("s_mm")
        p_ready = s("p_ready")
        pv_done = s("pv_done")
        o_ready = s("o_ready")
        oT_mm = s("oT_mm")
        rec_ready = s("rec_ready")
        on_ready = s("on_ready")
        onT_mm = s("onT_mm")
        onT_ready = s("onT_ready")
        y_mm = s("y_mm")
        x_added = s("x_added")
        maxed = m_ready if decayed else p1_max

        def maxed_at(n, g):
            return G * n + g + 1 if decayed else NP1 * n + HG * TB * (g + 1)

        tables = [(efac, "efac"), (dwin, "dwin"), (sfac, "sfac"), (mfac, "mfac")] if decayed else [(cwin, "cwin")]
        LOADED = 16 * (4 + len(tables))
        TABS = 16 * G * (forms + 1 + (not decayed))

        block = ctx.enter_context(nc.Block())

        @block.sync
        def _(sp):
            for t_, d_ in zip((wq, wk, wv, wo), w_dram):
                sp.dma_start(t_[:], d_.rearrange("(c p) n -> p c n", p=P)).then_inc(loaded, 16)
            for t_, name in tables:
                sp.dma_start(t_[:], tab[name]).then_inc(loaded, 16)
            for g in range(G):
                for st, rows in [(qst[f][g], "qrow_" + tag) for f in range(forms)] + [(kst[g], "krow_" + tag)]:
                    sp.dma_start(st[64:128, :, :].bitcast(F32),
                                 tab[rows].unsqueeze(1).broadcast_to([64, HG, L])).then_inc(tabs, 16)
            if not decayed:
                sp.wait_ge(tabs, 16 * G * (forms + 1))
                for g in range(G):
                    sp.dma_start(kst[g][64:66, :, :].bitcast(F32),
                                 tab["alibi"][:, HG * g:HG * g + HG, :]).then_inc(tabs, 16)

            def store_halves(n):
                for j, (f, half) in enumerate(parts):
                    sp.wait_ge(lo_ready, NQK * n + j + 1)
                    for r, part in enumerate((hi, lo, hi)[:stores[j]]):
                        sp.dma_start(qk_dram[f][8 * half:8 * half + 8, r, :, :],
                                     part[j % NHL][:].bitcast(F32)).then_inc(hl_out[j % NHL], 16)

            def load_stacks(n):
                for i in range(NHL):
                    sp.wait_ge(hl_out[i], 16 * stored(i, n + 1, 0))
                for g in range(G):
                    heads = slice(HG * g, HG * g + HG)
                    wait(sp, pv_done, G * ND * (n - 1) + ND * (g + 1))
                    for d in range(2):
                        for f in range(forms):
                            sp.dma_start(qst[f][g][32 * d:32 * d + 32, :, :].bitcast(F32),
                                         qk_dram[f][heads, 0:2].rearrange("h r d t -> (r d) h t")
                                         ).then_inc(st_ready[g], 16)
                        sp.dma_start(kst[g][32 * d:32 * d + 32, :, :].bitcast(F32),
                                     qk_dram[forms][heads, d:d + 2].rearrange("h r d t -> (r d) h t")
                                     ).then_inc(st_ready[g], 16)

            def load_max(n, g):
                k = G * n + g
                wait_alone(sp, ml_ready, k + 1)
                wait(sp, m_in, 16 * NMI * k)
                sp.dma_start(m_dram, mhl[:].bitcast(F32)).then_inc(m_out, 16)
                sp.wait_ge(m_out, 16 * (k + 1))
                for f in range(forms):
                    for d in range(forms):
                        for r in range(2):
                            row = 96 + 4 * f + 2 * d + r
                            sp.dma_start(qst[f][g][row:row + 1, :, :].bitcast(F32),
                                         m_dram.rearrange("(h q) r t -> r h q t", q=TB)[r:r + 1]
                                         ).then_inc(m_in, 16)

            store_halves(0)
            load_stacks(0)
            load_max(0, 0)

            def round_(b, last):
                load_max(b, 1)
                if not last:
                    store_halves(b + 1)
                load_max(b, 2)
                load_max(b, 3)
                if not last:
                    load_stacks(b + 1)
                    load_max(b + 1, 0)

            with sp.Fori(0, B - 1) as b:
                round_(b, False)
            round_(B - 1, True)
            sp.wait_ge(m_in, 16 * NMI * G * B)

        @block.gpsimd
        def _(pool):
            nc.gpsimd.memset(mhalf[:], -0.5).then_inc(half_set, 1)
            nc.gpsimd.memset(v[:], 0.0).then_inc(v_set, 1)
            pool.wait_ge(v_set, 1)
            nc.gpsimd.memset(v[:, :, :, HD:HD + 1], 1.0).then_inc(v_set, 1)
            pool.wait_ge(half_set, 1)
            with pool.Fori(0, B) as n:
                pool.wait_ge(var_ready, n + 1)
                nc.gpsimd.tensor_tensor(rstd[:], ve[:], mhalf[:], ALU.pow).then_inc(rstd_ready, 1)

        @block.tensor
        def _(pe):
            def front(ring, n):
                pe.wait_ge(xn_ready, n + 1)
                for c in range(DC):
                    bank = ring.take(pe, ("xT", 1, c), ((xT_a, xT_v)[c], n + 1))
                    for i in range(TB):
                        mm = nc.tensor.transpose(bank[:, i * P:(i + 1) * P], xn[:, i, c * P:(c + 1) * P], ident[:])
                    mm.then_inc(xT_mm, 1)
                pe.wait_ge(xT_a, n + 1)
                pe.wait_ge(xT_v, n + 1)
                for w, name in ((wq, "q"), (wk, "k")):
                    for half in range(2):
                        if name == "k":
                            freed = (lo_ready, NQK * n + 2 * forms + half + 1)
                        elif decayed:
                            freed = (qf_ready, 2 * forms * n + forms * (half + 1))
                        else:
                            freed = (lo_ready, NQK * n + half + 1)
                        bank = ring.take(pe, (name, 1, half), freed)
                        for c in range(DC):
                            mm = nc.tensor.matmul(bank[:, :], w[:, c, half * P:(half + 1) * P], xT[:, c, :],
                                                  start=c == 0, stop=c == DC - 1)
                        mm.then_inc(qk_mm, 1)

            def project_v(ring, n):
                for j in range(2):
                    bank = ring.take(pe, ("v", 1, j), (v_ready, 2 * n + j + 1))
                    for i in range(2):
                        for c in range(DC):
                            mm = nc.tensor.matmul(bank[:, i * D:(i + 1) * D],
                                                  xT[:, c, (2 * j + i) * P:(2 * j + i + 1) * P], wv[:, c, :],
                                                  start=c == 0, stop=c == DC - 1)
                    mm.then_inc(v_mm, 1)

            def pass1(ring, n, ahead, g):
                pe.wait_ge(st_ready[g], 32 * (forms + 1) * (n + 1))
                for h in range(HG):
                    for qb in range(TB):
                        bank = ring.take(pe, ("p1", ahead, g, h, qb), (p1_max, NP1 * n + TB * (HG * g + h) + qb + 1))
                        cols = L if decayed else (qb + 1) * P
                        nc.tensor.matmul(bank[:, 0:cols], qst[0][g][0:96, h, qb * P:(qb + 1) * P],
                                         kst[g][0:96, h, 0:cols], start=True, stop=True).then_inc(p1_mm, 1)

            def transpose_max(ring, n, ahead, g):
                pe.wait_ge(maxed, maxed_at(n, g))
                bank = ring.take(pe, ("mT", ahead, g), (ml_ready, G * n + g + 1))
                nc.tensor.transpose(bank[0:HG * TB, 0:P], mpost[:].rearrange("p h q -> p (h q)"),
                                    ident[:]).then_inc(mT_mm, 1)

            def scores(n, g, d):
                kb, f = duos[d]
                q0, q1 = span(kb, f)
                for pair in range(2):
                    pe.wait_ge(p_ready, NP2 * n + UNITS * g + 2 * d + pair + 1)
                    for hh in range(2):
                        h = 2 * pair + hh
                        nc.tensor.matmul(sbank[pair][:, hh, q0:q1], kst[g][:, h, kb * P:(kb + 1) * P],
                                         qst[f][g][:, h, q0:q1], start=True, stop=False)
                        mm = nc.tensor.matmul(sbank[pair][:, hh, kb * P:(kb + 1) * P], identb[:],
                                              maskb[:, f, :], start=False, stop=True)
                    mm.then_inc(s_mm, 1)

            def weigh(n, g, d):
                kb, f = duos[d]
                q0, q1 = span(kb, f)
                if d == 0:
                    pe.wait_ge(o_ready, G * n + g + 1)
                pe.wait_ge(p_ready, NP2 * n + UNITS * g + 2 * d + 2 + 2)
                for h in range(HG):
                    mm = nc.tensor.matmul(obank[32 * h:32 * h + 32, q0:q1], v[:, kb, HG * g + h, :],
                                          pt[d % 2][h // 2][:, h % 2, q0:q1],
                                          start=d == 0, stop=d == ND - 1)
                mm.then_inc(pv_done, 1)

            def pass2(ring, n, g):
                pe.wait_ge(m_in, 16 * NMI * (G * n + g + 1))
                if g == 0:
                    pe.wait_ge(v_ready, 2 * (n + 1))
                for d in range(ND):
                    scores(n, g, d)
                    if d == 0 and g < G - 1:
                        transpose_max(ring, n, 0, g + 1)
                    if d:
                        weigh(n, g, d - 1)
                weigh(n, g, ND - 1)

            def untranspose(ring, n, g):
                k = G * n + g
                pe.wait_ge(o_ready, k + 2)
                bank = ring.take(pe, ("oT", 0, g), (on_ready, k + 1))
                for qb in range(TB):
                    mm = nc.tensor.transpose(bank[:, qb * P:(qb + 1) * P], oT[:, qb * P:(qb + 1) * P], ident[:])
                mm.then_inc(oT_mm, 1)

            def back(ring, n):
                pe.wait_ge(on_ready, G * (n + 1))
                for c in range(DC):
                    bank = ring.take(pe, ("onT", 0, c), (onT_ready, 2 * n + c + 1))
                    for i in range(TB):
                        mm = nc.tensor.transpose(bank[:, i * P:(i + 1) * P], on[:, i, c * P:(c + 1) * P], ident[:])
                    mm.then_inc(onT_mm, 1)
                pe.wait_ge(onT_ready, 2 * n + 2)
                for j in range(2):
                    bank = ring.take(pe, ("y", 0, j), (x_added, 2 * n + j + 2))
                    for i in range(2):
                        for c in range(DC):
                            mm = nc.tensor.matmul(bank[:, i * D:(i + 1) * D],
                                                  onT[:, c, (2 * j + i) * P:(2 * j + i + 1) * P], wo[:, c, :],
                                                  start=c == 0, stop=c == DC - 1)
                    mm.then_inc(y_mm, 1)

            pe.wait_ge(loaded, LOADED)
            pe.wait_ge(tabs, TABS)
            front(ring_first, 0)
            project_v(ring_first, 0)
            pass1(ring_first, 0, 1, 0)
            transpose_max(ring_first, 0, 1, 0)

            def round_(ring, b, last):
                pe.wait_ge(ml_ready, G * b + 1)
                pe.wait_ge(x_added, 2 * b + 1)
                pass1(ring, b, 0, 1)
                pass2(ring, b, 0)
                if not last:
                    front(ring, b + 1)
                pass1(ring, b, 0, 2)
                untranspose(ring, b, 0)
                pass2(ring, b, 1)
                pass1(ring, b, 0, 3)
                untranspose(ring, b, 1)
                pass2(ring, b, 2)
                untranspose(ring, b, 2)
                pass2(ring, b, 3)
                if not last:
                    project_v(ring, b + 1)
                untranspose(ring, b, 3)
                if not last:
                    pass1(ring, b + 1, 1, 0)
                    transpose_max(ring, b + 1, 1, 0)
                back(ring, b)

            with pe.Fori(0, B - 1) as b:
                round_(ring_round, b, False)
            round_(ring_last, B - 1, True)

        @block.scalar
        def _(act):
            nc.scalar.nop().then_inc(p_ready, 2)
            act.wait_ge(v_set, 2)
            act.wait_ge(loaded, LOADED)

            def front(ring, n):
                act.wait_ge(xT_mm, 2 * n + 1)
                nc.scalar.copy(xT[:, 0, :], ring["xT", 1, 0][:, :]).then_inc(xT_a, 1)
                for j, (f, half) in enumerate(parts):
                    if j >= NHL:
                        act.wait_ge(hl_out[j % NHL], 16 * stored(j % NHL, n, j))
                    else:
                        wait(act, hl_out[j % NHL], 16 * stored(j % NHL, n, 0))
                    if decayed and f < forms:
                        act.wait_ge(qf_ready, 2 * forms * n + j + 1)
                        nc.scalar.copy(hi[j % NHL][:], qf[j % 2][:]).then_inc(hi_ready, 1)
                    else:
                        act.wait_ge(qk_mm, 4 * n + (2 if f == forms else 0) + half + 1)
                        nc.scalar.activation(hi[j % NHL][:], ring["k" if f == forms else "q", 1, half][:, :],
                                             ACT.Copy, scale=1.0 if f == forms else qscale).then_inc(hi_ready, 1)

            def copy_v(ring, n):
                for j in range(2):
                    act.wait_ge(v_mm, 2 * n + j + 1)
                    nc.scalar.copy(v[:, 2 * j:2 * j + 2, :, 0:HD],
                                   ring["v", 1, j][:, :].rearrange("p (t h d) -> p t h d", t=2, h=H)).then_inc(v_ready, 1)

            def split_max(ring, n, ahead, g):
                k = G * n + g
                act.wait_ge(mT_mm, k + 1)
                wait(act, m_out, 16 * k)
                nc.scalar.mul(mhl[:, 0, :], ring["mT", ahead, g][0:HG * TB, 0:P], -1.0).then_inc(mh_ready, 1)

            def exps(ring, n, g):
                for d, (kb, f) in enumerate(duos):
                    q0, q1 = span(kb, f)
                    for pair in range(2):
                        act.wait_ge(s_mm, NP2 * n + UNITS * g + 2 * d + pair + 1)
                        nc.scalar.activation(pt[d % 2][pair][:, :, q0:q1], sbank[pair][:, :, q0:q1], ACT.Exp,
                                             scale=sfac[:, f, kb:kb + 1] if decayed else 1.0).then_inc(p_ready, 1)
                    if d == 0 and g < G - 1:
                        split_max(ring, n, 0, g + 1)

            def back(ring, n):
                for c in range(DC):
                    act.wait_ge(onT_mm, 2 * n + c + 1)
                    nc.scalar.copy(onT[:, c, :], ring["onT", 0, c][:, :]).then_inc(onT_ready, 1)

            front(ring_first, 0)
            copy_v(ring_first, 0)
            split_max(ring_first, 0, 1, 0)

            def round_(ring, b, last):
                exps(ring, b, 0)
                if not last:
                    front(ring, b + 1)
                exps(ring, b, 1)
                exps(ring, b, 2)
                exps(ring, b, 3)
                if not last:
                    copy_v(ring, b + 1)
                    split_max(ring, b + 1, 1, 0)
                back(ring, b)

            with act.Fori(0, B - 1) as b:
                round_(ring_round, b, False)
            round_(ring_last, B - 1, True)

        @block.vector
        def _(dve):
            nc.vector.nop().then_inc(o_ready, 1)
            nc.vector.nop().then_inc(x_added, 1)
            dve.wait_ge(loaded, LOADED)

            def layernorm(n):
                for i in range(TB):
                    st = nc.vector.bn_stats(stats[:, i, :], x_res[:, bass.ds(n * TB + i, 1), :].rearrange("p a d -> p (a d)"))
                st.then_inc(ln, 1)
                wait_alone(dve, ln, 2 * n + 1)
                for i in range(TB):
                    st = nc.vector.bn_aggr(mv[:, i, :], stats[:, i, :])
                st.then_inc(ln, 1)
                dve.wait_ge(ln, 2 * n + 2)
                nc.vector.tensor_scalar_add(ve[:], mv[:, :, 1], EPS).then_inc(var_ready, 1)
                dve.wait_ge(rstd_ready, n + 1)
                for i in range(TB):
                    st = nc.vector.tensor_scalar(xn[:, i, :], x_res[:, bass.ds(n * TB + i, 1), :].rearrange("p a d -> p (a d)"),
                                                 mv[:, i, 0:1], rstd[:, i:i + 1], ALU.subtract, ALU.mult)
                st.then_inc(xn_ready, 1)

            def front(ring, n):
                dve.wait_ge(xT_mm, 2 * n + 2)
                nc.vector.tensor_copy(xT[:, 1, :], ring["xT", 1, 1][:, :]).then_inc(xT_v, 1)

                def low(j):
                    f, half = parts[j]
                    dve.wait_ge(hi_ready, NQK * n + j + 1)
                    high = hi[j % NHL][:].bitcast(F32)
                    if decayed and f < forms:
                        nc.vector.tensor_tensor(lo[j % NHL][:], qf[j % 2][:], high, ALU.subtract).then_inc(lo_ready, 1)
                    else:
                        nc.vector.scalar_tensor_tensor(out=lo[j % NHL][:], in0=ring["k" if f == forms else "q", 1, half][:, :],
                                                       scalar=1.0 if f == forms else qscale, in1=high,
                                                       op0=ALU.mult, op1=ALU.subtract).then_inc(lo_ready, 1)

                if decayed:
                    for j in range(2 * forms):
                        f, half = parts[j]
                        dve.wait_ge(qk_mm, 4 * n + half + 1)
                        wait(dve, lo_ready, NQK * n + max(j - 1, 0))
                        nc.vector.tensor_tensor(qf[j % 2][:], ring["q", 1, half][:, :], efac[:, f, :],
                                                ALU.mult).then_inc(qf_ready, 1)
                        dve.wait_ge(qf_ready, 2 * forms * n + j + 1)
                        if j:
                            low(j - 1)
                    for j in range(2 * forms - 1, NQK):
                        low(j)
                else:
                    for j in range(NQK):
                        low(j)

            def maxima(ring, n, ahead, g):
                for h in range(HG):
                    for qb in range(TB):
                        wait_alone(dve, p1_mm, NP1 * n + TB * (HG * g + h) + qb + 1)
                        bank = ring["p1", ahead, g, h, qb]
                        cols = L if decayed else (qb + 1) * P
                        other = dwin[:, (TB - 1 - qb) * P:(TB - 1 - qb) * P + L] if decayed else cwin[:, L - cols:L]
                        nc.vector.tensor_tensor_reduce(out=bank[:, 0:cols], in0=bank[:, 0:cols], in1=other, scale=1.0,
                                                       scalar=LOW, op0=ALU.mult if decayed else ALU.add, op1=ALU.max,
                                                       accum_out=mcol[:, h, qb:qb + 1]).then_inc(p1_max, 1)
                if decayed:
                    dve.wait_ge(p1_max, NP1 * n + HG * TB * (g + 1))
                    nc.vector.tensor_tensor(mpost[:], mcol[:], mfac[:].unsqueeze(1).broadcast_to([P, HG, TB]),
                                            ALU.mult).then_inc(m_ready, 1)

            def split_max(ring, n, ahead, g):
                dve.wait_ge(mh_ready, G * n + g + 1)
                nc.vector.scalar_tensor_tensor(out=mhl[:, 1, :], in0=ring["mT", ahead, g][0:HG * TB, 0:P], scalar=-1.0,
                                               in1=mhl[:, 0, :].bitcast(F32), op0=ALU.mult,
                                               op1=ALU.subtract).then_inc(ml_ready, 1)

            def copy_o(n, g):
                dve.wait_ge(pv_done, ND * (G * n + g + 1))
                nc.vector.tensor_copy(oT[:], obank[:, :]).then_inc(o_ready, 1)

            def normalise(ring, n, g):
                k = G * n + g
                dve.wait_ge(oT_mm, k + 1)
                o4 = ring["oT", 0, g][:, :].rearrange("p (q h x) -> p q h x", q=TB, h=HG)
                nc.vector.reciprocal(rec[:], o4[:, :, :, HD]).then_inc(rec_ready, 1)
                dve.wait_ge(rec_ready, k + 1)
                nc.vector.tensor_tensor(on[:, :, HG * HD * g:HG * HD * (g + 1)].rearrange("p q (h d) -> p q h d", h=HG),
                                        o4[:, :, :, 0:HD], rec[:].unsqueeze(3).broadcast_to([P, TB, HG, HD]),
                                        ALU.mult).then_inc(on_ready, 1)

            def add(ring, n):
                for j in range(2):
                    dve.wait_ge(y_mm, 2 * n + j + 1)
                    xr = x_res[:, bass.ds(n * TB + 2 * j, 2), :].rearrange("p a d -> p (a d)")
                    nc.vector.tensor_tensor(xr, ring["y", 0, j][:, :], xr, ALU.add).then_inc(x_added, 1)

            layernorm(0)
            front(ring_first, 0)
            maxima(ring_first, 0, 1, 0)
            split_max(ring_first, 0, 1, 0)

            def round_(ring, b, last):
                maxima(ring, b, 0, 1)
                if not last:
                    layernorm(b + 1)
                split_max(ring, b, 0, 1)
                copy_o(b, 0)
                if not last:
                    front(ring, b + 1)
                maxima(ring, b, 0, 2)
                normalise(ring, b, 0)
                split_max(ring, b, 0, 2)
                copy_o(b, 1)
                maxima(ring, b, 0, 3)
                normalise(ring, b, 1)
                split_max(ring, b, 0, 3)
                copy_o(b, 2)
                normalise(ring, b, 2)
                copy_o(b, 3)
                normalise(ring, b, 3)
                if not last:
                    maxima(ring, b + 1, 1, 0)
                    split_max(ring, b + 1, 1, 0)
                add(ring, b)

            with dve.Fori(0, B - 1) as b:
                round_(ring_round, b, False)
            round_(ring_last, B - 1, True)


def route(nc, sem, tag, x_res, ident, gate_w, gate_b, tab, xs_dram, xn_dram, run, row_all, w_all,
          wgu, wd, gu_dram, dn_dram):
    with ExitStack() as ctx:
        def sb(name, shape, dt=F32):
            return ctx.enter_context(nc.sbuf_tensor(f"{name}_{tag}", shape, dt))

        def ps(name, shape):
            return ctx.enter_context(nc.psum_tensor(f"{name}_{tag}", shape, F32))

        def s(name):
            return sem(f"{name}_{tag}")

        gw = sb("gw", [P, DC, E])
        gb = sb("gb", [P, E])
        base = sb("base", [P, E])
        before_f, ones_f = sb("before_f", [P, P]), sb("ones_f", [P, P])
        before, ones = sb("before", [P, P], BF16), sb("ones", [P, P], BF16)
        stats, mv = sb("rstats", [P, TB, 6]), sb("rmv", [P, TB, 2])
        ve, rstd, mhalf = sb("rve", [P, TB]), sb("rrstd", [P, TB]), sb("rmhalf", [P, TB])
        xn = [sb(f"rxn{i}", [P, TB, D]) for i in range(2)]
        xT = sb("rxT", [P, DC, L])
        th = sb("rth", [P, TB, E])
        score = sb("score", [P, TB, E])
        vals, valr = sb("vals", [P, TB, E + 2]), sb("valr", [P, TB, E + 2])
        top, topr = sb("top", [P, TB, 8]), sb("topr", [P, TB, 8])
        gval, gvalr = sb("gval", [P, TB, NGROUP + 4]), sb("gvalr", [P, TB, NGROUP + 4])
        gtop, gtopr = sb("gtop", [P, TB, 8]), sb("gtopr", [P, TB, 8])
        gmask = sb("gmask", [P, TB, NGROUP])
        mask, maskb = sb("rmask", [P, TB, E]), sb("rmaskb", [P, TB, E], BF16)
        wsel = sb("wsel", [P, TB, E])
        wsum = sb("wsum", [P, TB])
        slot = sb("slot", [P, TB, E])
        stop_, same = sb("stop", [P, TB, 8]), sb("same", [P, TOPK, E])
        w6 = sb("w6", [P, TB, TOPK])
        idx = [sb(f"idx{i}", [P, TB, TOPK], U32) for i in range(2)]

        bank_x = [ps(f"rx{i}", [P, 512]) for i in range(2)]
        bank_l = ps("rl", [P, TB, E])
        bank_r = ps("rr", [P, TB + 1, E])

        loaded, cast = s("rloaded"), s("rcast")
        w_in = s("rw_in")
        half_set = s("rhalf")
        step = s("rstep")
        var_ready = s("rvar")
        rstd_ready = s("rrstd_ready")
        xn_ready = s("rxn_ready")
        xT_mm = s("rxT_mm")
        xT_ready = s("rxT_ready")
        l_mm = s("rl_mm")
        th_ready = s("rth_ready")
        mask_ready = s("rmask_ready")
        rank_mm = s("rrank_mm")
        idx_ready = s("ridx_ready")
        sent = [s(f"rsent{i}") for i in range(2)]
        kept = [s(f"rkept{i}") for i in range(2)]

        NSTEP = 29

        block = ctx.enter_context(nc.Block())

        @block.sync
        def _(sp):
            sp.dma_start(gw[:], gate_w.rearrange("(c p) e -> p c e", p=P)).then_inc(loaded, 16)
            sp.dma_start(gb[:], gate_b.unsqueeze(0).broadcast_to([P, E])).then_inc(loaded, 16)
            sp.dma_start(base[:], tab["base"]).then_inc(loaded, 16)
            sp.dma_start(before_f[:], tab["before"]).then_inc(loaded, 16)
            sp.dma_start(wgu[:], gu_dram.rearrange("e (c p) n -> p (e c) n", p=P)).then_inc(w_in, 16)
            sp.dma_start(wd[:], dn_dram.rearrange("e p n -> p e n")).then_inc(w_in, 16)
            with sp.Fori(0, B // 2) as j:
                for p in range(2):
                    wait_alone(sp, xn_ready, 2 * j + p + 1)
                    sp.dma_start(xn_dram[bass.ds(j * 2 * L + p * L, L), :].rearrange("(t q) d -> q t d", q=P),
                                 xn[p][:]).then_inc(kept[p], 16)
            for p in range(2):
                sp.wait_ge(kept[p], 16 * (B // 2))
            sp.wait_ge(w_in, 32)

        @block.gpsimd
        def _(pool):
            nc.gpsimd.memset(mhalf[:], -0.5).then_inc(half_set, 1)
            pool.wait_ge(half_set, 1)

            def scatter(n, p):
                wait_alone(pool, idx_ready, n + 1)
                for i in range(TB):
                    for k in range(TOPK):
                        nc.gpsimd.indirect_dma_start(
                            xs_dram, bass.IndirectOffsetOnAxis(ap=idx[p][:, i, k:k + 1], axis=0),
                            xn[p][:, i, :], None).then_inc(sent[p], 16)

            def roots(n):
                pool.wait_ge(var_ready, n + 1)
                nc.gpsimd.tensor_tensor(rstd[:], ve[:], mhalf[:], ALU.pow).then_inc(rstd_ready, 1)

            roots(0)
            with pool.Fori(0, B // 2 - 1) as j:
                for p in range(2):
                    roots(2 * j + p + 1)
                    scatter(2 * j + p, p)
            roots(B - 1)
            scatter(B - 2, 0)
            scatter(B - 1, 1)
            for p in range(2):
                pool.wait_ge(sent[p], 16 * TB * TOPK * (B // 2))

        @block.tensor
        def _(pe):
            pe.wait_ge(loaded, 64)
            pe.wait_ge(cast, 1)
            with pe.Fori(0, B // 2) as j:
                for p in range(2):
                    n = 2 * j + p
                    pe.wait_ge(xn_ready, n + 1)
                    for c in range(DC):
                        for i in range(TB):
                            mm = nc.tensor.transpose(bank_x[c][:, i * P:(i + 1) * P], xn[p][:, i, c * P:(c + 1) * P],
                                                     ident[:])
                        mm.then_inc(xT_mm, 1)
                    pe.wait_ge(xT_ready, 2 * n + 2)
                    for i in range(TB):
                        for c in range(DC):
                            mm = nc.tensor.matmul(bank_l[:, i, :], xT[:, c, i * P:(i + 1) * P], gw[:, c, :],
                                                  start=c == 0, stop=c == DC - 1)
                    mm.then_inc(l_mm, 1)
                    pe.wait_ge(mask_ready, n + 1)
                    for i in range(TB + 1):
                        for k in range(min(i + 1, TB)):
                            mm = nc.tensor.matmul(bank_r[:, i, :], (before if k == i else ones)[:], maskb[:, k, :],
                                                  start=k == 0, stop=k == min(i, TB - 1))
                    mm.then_inc(rank_mm, 1)

        @block.scalar
        def _(act):
            with act.Fori(0, B) as n:
                for c in range(DC):
                    act.wait_ge(xT_mm, 2 * n + c + 1)
                    nc.scalar.copy(xT[:, c, :], bank_x[c][:, :]).then_inc(xT_ready, 1)
                act.wait_ge(l_mm, n + 1)
                nc.scalar.activation(th[:], bank_l[:], ACT.Tanh, scale=0.5).then_inc(th_ready, 1)

        @block.vector
        def _(dve):
            dve.wait_ge(loaded, 64)
            nc.vector.memset(ones_f[:], 1.0)
            for marks in (vals, gval, gtopr, topr):
                nc.vector.memset(marks[:], LOW)
            nc.vector.tensor_copy(run[:], base[:])
            nc.vector.tensor_copy(before[:], before_f[:])
            nc.vector.memset(ones[:], 1.0).then_inc(cast, 1)
            dve.wait_ge(cast, 1)

            def layernorm(n, p, free):
                def x(i):
                    return x_res[:, bass.ds(n * TB + i, 1), :].rearrange("p a d -> p (a d)")
                for i in range(TB):
                    st = nc.vector.bn_stats(stats[:, i, :], x(i))
                at = tick(n)
                at(st)
                for i in range(TB):
                    st = nc.vector.bn_aggr(mv[:, i, :], stats[:, i, :])
                at(st)
                nc.vector.tensor_scalar_add(ve[:], mv[:, :, 1], EPS).then_inc(var_ready, 1)
                dve.wait_ge(rstd_ready, n + 1)
                if free is not None:
                    dve.wait_ge(kept[p], 16 * free)
                    dve.wait_ge(sent[p], 16 * TB * TOPK * free)
                for i in range(TB):
                    st = nc.vector.tensor_scalar(xn[p][:, i, :], x(i), mv[:, i, 0:1], rstd[:, i:i + 1],
                                                 ALU.subtract, ALU.mult)
                st.then_inc(xn_ready, 1)
                return at

            class tick:

                def __init__(self, n):
                    self.n, self.k = n, 0

                def __call__(self, ins):
                    self.k += 1
                    ins.then_inc(step, 1)
                    wait_alone(dve, step, NSTEP * self.n + self.k)

            def choose(n, p, at):
                dve.wait_ge(th_ready, n + 1)
                at(nc.vector.tensor_scalar(score[:], th[:], 0.5, 0.5, ALU.mult, ALU.add))
                biased = vals[:, :, 0:E]
                at(nc.vector.tensor_tensor(biased, score[:], gb[:].unsqueeze(1).broadcast_to([P, TB, E]), ALU.add))
                groups = biased.rearrange("p t (g e) -> p t g e", g=NGROUP)
                at(nc.vector.tensor_reduce(gval[:, :, 0:NGROUP], groups, AX.X, ALU.max))
                for i in range(TB):
                    st = nc.vector.max(gtop[:, i, :], gval[:, i, :])
                at(st)
                at(nc.vector.tensor_copy(gtopr[:, :, 0:TOPG], gtop[:, :, 0:TOPG]))
                for i in range(TB):
                    st = nc.vector.match_replace(gvalr[:, i, :], gtopr[:, i, :], gval[:, i, :], HIGH)
                at(st)
                at(nc.vector.tensor_scalar(gmask[:], gvalr[:, :, 0:NGROUP], HIGH, None, ALU.is_ge))
                at(nc.vector.tensor_tensor(groups, groups, gmask[:].unsqueeze(3).broadcast_to([P, TB, NGROUP, EG]),
                                           ALU.mult))
                at(nc.vector.tensor_scalar_add(biased, biased, 0.0))
                for i in range(TB):
                    st = nc.vector.max(top[:, i, :], vals[:, i, :])
                at(st)
                at(nc.vector.tensor_copy(topr[:, :, 0:TOPK], top[:, :, 0:TOPK]))
                for i in range(TB):
                    st = nc.vector.match_replace(valr[:, i, :], topr[:, i, :], vals[:, i, :], HIGH)
                at(st)
                nc.vector.tensor_scalar(maskb[:], valr[:, :, 0:E], HIGH, None, ALU.is_ge).then_inc(mask_ready, 1)
                at(nc.vector.tensor_scalar(mask[:], valr[:, :, 0:E], HIGH, None, ALU.is_ge))
                return at

            def place(n, p, at, free):
                at(nc.vector.tensor_tensor(wsel[:], mask[:], score[:], ALU.mult))
                at(nc.vector.tensor_reduce(wsum[:], wsel[:], AX.X, ALU.add))
                at(nc.vector.tensor_scalar_add(wsum[:], wsum[:], 1e-20))
                at(nc.vector.reciprocal(wsum[:], wsum[:]))
                at(nc.vector.tensor_scalar_mul(wsum[:], wsum[:], ROUTE_SCALE))
                at(nc.vector.tensor_tensor(wsel[:], wsel[:], wsum[:].unsqueeze(2).broadcast_to([P, TB, E]), ALU.mult))
                dve.wait_ge(rank_mm, n + 1)
                at(nc.vector.tensor_tensor(slot[:], bank_r[:, 0:TB, :], run[:].unsqueeze(1).broadcast_to([P, TB, E]),
                                           ALU.add))
                nc.vector.tensor_tensor(run[:], bank_r[:, TB, :], run[:], ALU.add)
                at(nc.vector.tensor_tensor(slot[:], slot[:], mask[:], ALU.mult))
                for i in range(TB):
                    st = nc.vector.max(stop_[:, i, :], slot[:, i, :])
                at(st)
                if free is not None:
                    dve.wait_ge(sent[p], 16 * TB * TOPK * free)
                nc.vector.tensor_scalar_add(row_all[:, bass.ds(n * TB, TB), :], stop_[:, :, 0:TOPK], -1.0)
                nc.vector.tensor_scalar_add(idx[p][:], stop_[:, :, 0:TOPK], -1.0).then_inc(idx_ready, 1)
                for i in range(TB):
                    for k in range(TOPK):
                        st = nc.vector.scalar_tensor_tensor(out=same[:, k, :], in0=slot[:, i, :],
                                                            scalar=stop_[:, i, k:k + 1], in1=wsel[:, i, :],
                                                            op0=ALU.is_equal, op1=ALU.mult,
                                                            accum_out=w6[:, i, k:k + 1])
                    at(st)
                at(nc.vector.tensor_copy(w_all[:, bass.ds(n * TB, TB), :], w6[:]))
                assert at.k == NSTEP, at.k

            def whole(n, p, free):
                at = layernorm(n, p, free)
                choose(n, p, at)
                place(n, p, at, free)

            whole(0, 0, None)
            whole(1, 1, None)
            with dve.Fori(1, B // 2) as j:
                for p in range(2):
                    whole(2 * j + p, p, j)


def experts(nc, sem, tag, ident, wgu, wd, tab, run, row_all, idx_all, xs_dram, ys_dram, zrow):
    U = 4
    J = NSLOT // U
    with ExitStack() as ctx:
        def sb(name, shape, dt=F32):
            return ctx.enter_context(nc.sbuf_tensor(f"{name}_{tag}", shape, dt))

        def ps(name, shape):
            return ctx.enter_context(nc.psum_tensor(f"{name}_{tag}", shape, F32))

        def s(name):
            return sem(f"{name}_{tag}")

        sidx, ebase = sb("sidx", [P, U]), sb("ebase", [P, E])
        padf, padu = sb("padf", [P, E]), sb("padu", [P, E], U32)
        cnt_i, nt_i = sb("cnt_i", [P, E], I32), sb("nt_i", [P, E], I32)
        nt, ct, one = sb("nt", [P, E]), sb("ct", [P, E]), sb("one", [P, E])
        le, ln = sb("le", [P, U, E]), sb("len", [P, U, E])
        ex, st0 = sb("ex", [P, U]), sb("st0", [P, U])
        cols = sb("cols", [P, 2, U])
        rows = sb("rows", [1, 2, U, J], U32)
        shift, moved = sb("shift", [P, E]), [sb(f"moved{i}", [P, T * TOPK]) for i in range(2)]
        acc = [sb(f"acc{i}", [P, T * TOPK]) for i in range(2)]
        xt = [sb(f"ext{i}", [P, D]) for i in range(U)]
        xT = [sb(f"exT{i}", [P, DC, P]) for i in range(2)]
        th = [sb(f"eth{i}", [P, FI]) for i in range(2)]
        a = [sb(f"ea{i}", [P, FI]) for i in range(2)]
        h = [sb(f"eh{i}", [P, FI]) for i in range(2)]
        hT = [sb(f"ehT{i}", [P, P]) for i in range(2)]
        y = [sb(f"ey{i}", [P, D]) for i in range(U)]
        bx = [ps(f"ebx{i}", [P, DC, P]) for i in range(2)]
        bg = [ps(f"ebg{i}", [P, 2 * FI]) for i in range(2)]
        bh = [ps(f"ebh{i}", [P, P]) for i in range(2)]
        by = [ps(f"eby{i}", [P, D]) for i in range(2)]

        loaded, zeroed = s("eloaded"), s("ezeroed")
        step = s("estep")
        pad_ready = s("epad_ready")
        padded = s("epadded")
        shift_ready = s("eshift")
        move = s("emove")
        cols_ready = s("ecols")
        rows_mm, rows_ready = s("erows_mm"), s("erows")
        x_in = [s(f"ex_in{i}") for i in range(U)]
        y_out = [s(f"ey_out{i}") for i in range(U)]
        xT_mm, xT_ready = s("exT_mm"), s("exT_ready")
        g_mm = s("eg_mm")
        th_ready = s("eth_ready")
        a_ready = s("ea_ready")
        h_ready = s("eh_ready")
        hT_mm, hT_ready = s("ehT_mm"), s("ehT_ready")
        y_mm, y_ready = s("ey_mm"), s("ey_ready")

        block = ctx.enter_context(nc.Block())

        @block.sync
        def _(sp):
            sp.dma_start(sidx[:], tab["sidx"]).then_inc(loaded, 16)
            sp.dma_start(ebase[:], tab["base"]).then_inc(loaded, 16)
            sp.dma_start(xs_dram[E * CAP:E * CAP + P, :], zrow[:]).then_inc(padded, 16)
            sp.wait_ge(pad_ready, 1)
            with sp.Fori(0, E) as e:
                r = sp.value_load(padu[0:1, bass.ds(e, 1)], min_val=0, max_val=E * CAP - P)
                sp.dma_start(xs_dram[bass.ds(r, P), :], zrow[:]).then_inc(padded, 16)
            sp.wait_ge(padded, 16 * (E + 1))
            sp.wait_ge(rows_ready, 1)

            def load(s_, q, j):
                wait_alone(sp, xT_mm, s_ - U + 1)
                r = sp.value_load(rows[0:1, 1, q, bass.ds(j, 1)], min_val=0, max_val=XROWS - P)
                sp.dma_start(xt[q][:], xs_dram[bass.ds(r, P), :]).then_inc(x_in[q], 16)

            def store(s_, q, j):
                wait_alone(sp, y_ready, s_ + 1)
                sp.dma_start(ys_dram[bass.ds(s_ * P, P), :], y[q][:]).then_inc(y_out[q], 16)

            LAG = 6
            for s_ in range(2 * U):
                load(s_, s_ % U, s_ // U)
                if s_ >= LAG:
                    store(s_ - LAG, (s_ - LAG) % U, (s_ - LAG) // U)
            with sp.Fori(2, J) as j:
                for q in range(U):
                    load(U * j + q, q, j)
                    store(U * j + q - LAG, (q - LAG) % U, j + (q - LAG) // U)
            for s_ in range(NSLOT - LAG, NSLOT):
                store(s_, s_ % U, s_ // U)
            for q in range(U):
                sp.wait_ge(y_out[q], 16 * J)

        @block.gpsimd
        def _(pool):
            pool.wait_ge(shift_ready, 1)
            rows_f = row_all[:].rearrange("p t k -> p (t k)")
            for e in range(1, E):
                nc.gpsimd.tensor_scalar(moved[e % 2][:], rows_f, float(e * CAP), shift[:, e - 1:e],
                                        ALU.is_ge, ALU.mult).then_inc(move, 1)
                pool.wait_ge(move, 2 * e - 1)
                nc.gpsimd.tensor_tensor(acc[e % 2][:], moved[e % 2][:], rows_f if e == 1 else acc[(e - 1) % 2][:],
                                        ALU.add).then_inc(move, 1)
                pool.wait_ge(move, 2 * e)
            nc.gpsimd.tensor_copy(idx_all[:].rearrange("p t k -> p (t k)"), acc[(E - 1) % 2][:]).then_inc(move, 1)
            pool.wait_ge(move, 2 * E - 1)

        @block.tensor
        def _(pe):
            pe.wait_ge(cols_ready, 1)
            for w in range(2):
                for q in range(U):
                    mm = nc.tensor.transpose(by[w][0:1, q * J:(q + 1) * J], cols[0:J, w, q:q + 1], ident[0:J, 0:J])
            mm.then_inc(rows_mm, 1)
            pe.wait_ge(rows_ready, 1)

            def up_t(s_, q, j):
                pe.wait_ge(x_in[q], 16 * (j + 1))
                wait(pe, xT_ready, s_ - 1)
                for c in range(DC):
                    mm = nc.tensor.transpose(bx[q % 2][:, c, :], xt[q][:, c * P:(c + 1) * P], ident[:])
                mm.then_inc(xT_mm, 1)

            def up(s_, q, j):
                e = pe.value_load(rows[0:1, 0, q, bass.ds(j, 1)], min_val=0, max_val=E - 1)
                pe.wait_ge(xT_ready, s_ + 1)
                wait(pe, h_ready, s_ - 1)
                for c in range(DC):
                    mm = nc.tensor.matmul(bg[q % 2][:, :], xT[q % 2][:, c, :],
                                          wgu[:, bass.ds(e * DC + c, 1), :].rearrange("p a n -> p (a n)"),
                                          start=c == 0, stop=c == DC - 1)
                mm.then_inc(g_mm, 1)

            def down_t(s_, q, j):
                pe.wait_ge(h_ready, s_ + 1)
                wait(pe, hT_ready, s_ - 1)
                nc.tensor.transpose(bh[q % 2][:, :], h[q % 2][:], ident[:]).then_inc(hT_mm, 1)

            def down(s_, q, j):
                e = pe.value_load(rows[0:1, 0, q, bass.ds(j, 1)], min_val=0, max_val=E - 1)
                pe.wait_ge(hT_ready, s_ + 1)
                wait(pe, y_ready, s_ - 1)
                nc.tensor.matmul(by[q % 2][:, :], hT[q % 2][:],
                                 wd[:, bass.ds(e, 1), :].rearrange("p a n -> p (a n)"),
                                 start=True, stop=True).then_inc(y_mm, 1)

            def at(f, s_, q, j, back_):
                f(s_ - back_, (q - back_) % U, j + (q - back_) // U)

            up_t(0, 0, 0)
            for s_ in range(U):
                q = s_
                up(s_, q, 0)
                if s_ >= 1:
                    at(down_t, s_, q, 0, 1)
                if s_ >= 2:
                    at(down, s_, q, 0, 2)
                at(up_t, s_, q, 0, -1)
            with pe.Fori(1, J - 1) as j:
                for q in range(U):
                    up(U * j + q, q, j)
                    at(down_t, U * j + q, q, j, 1)
                    at(down, U * j + q, q, j, 2)
                    at(up_t, U * j + q, q, j, -1)
            for s_ in range(NSLOT - U, NSLOT + 2):
                q, j = s_ % U, s_ // U
                if s_ < NSLOT:
                    up(s_, q, j)
                if s_ <= NSLOT:
                    at(down_t, s_, q, j, 1)
                at(down, s_, q, j, 2)
                if s_ < NSLOT - 1:
                    at(up_t, s_, q, j, -1)

        @block.scalar
        def _(act):
            act.wait_ge(rows_mm, 1)
            for w in range(2):
                cp = nc.scalar.copy(rows[0:1, w, :, :], by[w][0:1, 0:U * J].rearrange("p (q j) -> p q j", q=U))
            cp.then_inc(rows_ready, 1)

            def tokens(s_, q, j):
                act.wait_ge(xT_mm, s_ + 1)
                nc.scalar.copy(xT[q % 2][:], bx[q % 2][:]).then_inc(xT_ready, 1)

            def squash(s_, q, j):
                act.wait_ge(g_mm, s_ + 1)
                nc.scalar.activation(th[q % 2][:], bg[q % 2][:, 0:FI], ACT.Tanh, scale=0.5).then_inc(th_ready, 1)

            def output(s_, q, j):
                act.wait_ge(y_mm, s_ + 1)
                wait(act, y_out[q], 16 * j)
                nc.scalar.copy(y[q][:], by[q % 2][:]).then_inc(y_ready, 1)

            def at(f, s_, q, j, back_):
                f(s_ - back_, (q - back_) % U, j + (q - back_) // U)

            tokens(0, 0, 0)
            for s_ in range(U):
                squash(s_, s_, 0)
                if s_ >= 2:
                    at(output, s_, s_, 0, 2)
                at(tokens, s_, s_, 0, -1)
            for q in range(2):
                squash(U + q, q, 1)
                at(output, U + q, q, 1, 2)
                at(tokens, U + q, q, 1, -1)
            with act.Fori(1, J - 1) as j:
                for q_ in range(U):
                    q, jj = (q_ + 2) % U, j + (q_ + 2) // U
                    squash(U * j + q_ + 2, q, jj)
                    at(output, U * j + q_ + 2, q, jj, 2)
                    at(tokens, U * j + q_ + 2, q, jj, -1)
            for s_ in range(NSLOT - 2, NSLOT + 2):
                q, j = s_ % U, s_ // U
                if s_ < NSLOT:
                    squash(s_, q, j)
                at(output, s_, q, j, 2)
                if s_ < NSLOT - 1:
                    at(tokens, s_, q, j, -1)

        @block.vector
        def _(dve):
            k = [0]

            def done(ins):
                k[0] += 1
                ins.then_inc(step, 1)
                dve.wait_ge(step, k[0])

            dve.wait_ge(loaded, 32)
            done(nc.vector.tensor_scalar_add(padf[:], run[:], -1.0))
            nc.vector.tensor_copy(padu[:], padf[:]).then_inc(pad_ready, 1)
            nc.vector.memset(one[:], 1.0)
            done(nc.vector.tensor_tensor(nt[:], run[:], ebase[:], ALU.subtract))
            done(nc.vector.tensor_scalar_add(cnt_i[:], nt[:], float(P - 1)))
            done(nc.vector.tensor_single_scalar(nt_i[:], cnt_i[:], P.bit_length() - 1, ALU.arith_shift_right))
            done(nc.vector.tensor_copy(nt[:], nt_i[:]))
            done(nc.vector.tensor_tensor_scan(ct[:], one[:], nt[:], 0.0, ALU.mult, ALU.add))
            done(nc.vector.tensor_tensor(le[:], ct[:].unsqueeze(1).broadcast_to([P, U, E]),
                                         sidx[:].unsqueeze(2).broadcast_to([P, U, E]), ALU.is_le))
            done(nc.vector.tensor_tensor(ln[:], le[:], nt[:].unsqueeze(1).broadcast_to([P, U, E]), ALU.mult))
            nc.vector.tensor_reduce(ex[:], le[:], AX.X, ALU.add)
            done(nc.vector.tensor_reduce(st0[:], ln[:], AX.X, ALU.add))
            done(nc.vector.tensor_tensor(st0[:], sidx[:], st0[:], ALU.subtract))
            done(nc.vector.tensor_scalar_mul(st0[:], st0[:], float(P)))
            done(nc.vector.scalar_tensor_tensor(out=st0[:], in0=ex[:], scalar=float(CAP), in1=st0[:],
                                                op0=ALU.mult, op1=ALU.add))
            nc.vector.tensor_scalar_min(cols[:, 1, :], st0[:], float(E * CAP))
            nc.vector.tensor_scalar_min(cols[:, 0, :], ex[:], float(E - 1)).then_inc(cols_ready, 1)
            nc.vector.tensor_scalar(shift[:], nt[:], float(P), float(-CAP), ALU.mult, ALU.add).then_inc(shift_ready, 1)
            dve.wait_ge(rows_ready, 1)

            def inner(s_, q, j):
                dve.wait_ge(th_ready, s_ + 1)
                nc.vector.scalar_tensor_tensor(out=a[q % 2][:], in0=th[q % 2][:], scalar=1.0, in1=bg[q % 2][:, 0:FI],
                                               op0=ALU.add, op1=ALU.mult).then_inc(a_ready, 1)
                dve.wait_ge(a_ready, s_ + 1)
                nc.vector.scalar_tensor_tensor(out=h[q % 2][:], in0=a[q % 2][:], scalar=0.5,
                                               in1=bg[q % 2][:, FI:2 * FI], op0=ALU.mult,
                                               op1=ALU.mult).then_inc(h_ready, 1)

            def turned(s_, q, j):
                dve.wait_ge(hT_mm, s_ + 1)
                nc.vector.tensor_copy(hT[q % 2][:], bh[q % 2][:]).then_inc(hT_ready, 1)

            inner(0, 0, 0)
            for s_ in range(1, U):
                turned(s_ - 1, s_ - 1, 0)
                inner(s_, s_, 0)
            with dve.Fori(1, J) as j:
                for q in range(U):
                    turned(U * j + q - 1, (q - 1) % U, j)
                    inner(U * j + q, q, j)
            turned(NSLOT - 1, U - 1, J - 1)


def combine(nc, sem, tag, x_res, ident, wsg, wsd, xn_dram, ys_dram, idx_all, w_all, out_dram):
    NB = 2
    with ExitStack() as ctx:
        def sb(name, shape, dt=F32):
            return ctx.enter_context(nc.sbuf_tensor(f"{name}_{tag}", shape, dt))

        def ps(name, shape):
            return ctx.enter_context(nc.psum_tensor(f"{name}_{tag}", shape, F32))

        def s(name):
            return sem(f"{name}_{tag}")

        wg = sb("cwg", [P, DC, 2 * FS])
        wd = sb("cwd", [P, FS // P, D])
        yg = [sb(f"cyg{i}", [P, TOPK, D]) for i in range(NB)]
        idx = [sb(f"cidx{i}", [P, TOPK], U32) for i in range(NB)]
        xt = [sb(f"cxt{i}", [P, D]) for i in range(NB)]
        xT = sb("cxT", [P, DC, P])
        th, a, h = sb("cth", [P, FS]), sb("ca", [P, FS]), sb("ch", [P, FS])
        hT = sb("chT", [P, FS // P, P])
        bx, bg, bh, by = ps("cbx", [P, DC, P]), ps("cbg", [P, 2 * FS]), ps("cbh", [P, FS // P, P]), ps("cby", [P, D])

        loaded = s("cloaded")
        x_in = [s(f"cx_in{i}") for i in range(NB)]
        idx_ready = s("cidx_ready")
        got = [s(f"cgot{i}") for i in range(NB)]
        xT_mm, xT_ready = s("cxT_mm"), s("cxT_ready")
        g_mm = s("cg_mm")
        th_ready = s("cth_ready")
        a_ready, h_ready = s("ca_ready"), s("ch_ready")
        hT_mm, hT_ready = s("chT_mm"), s("chT_ready")
        y_mm = s("cy_mm")
        added = s("cadded")
        stored = s("cstored")
        NA = TOPK + 1

        block = ctx.enter_context(nc.Block())

        @block.sync
        def _(sp):
            sp.dma_start(wg[:], wsg.rearrange("(c p) n -> p c n", p=P)).then_inc(loaded, 16)
            sp.dma_start(wd[:], wsd.rearrange("(c p) n -> p c n", p=P)).then_inc(loaded, 16)

            def load(t, p, j):
                wait_alone(sp, xT_mm, t - NB + 1)
                sp.dma_start(xt[p][:], xn_dram[bass.ds(t * P, P), :]).then_inc(x_in[p], 16)

            def store(t):
                if out_dram is not None:
                    wait_alone(sp, added, NA * (t + 1))
                    sp.dma_start(out_dram[bass.ds(t * P, P), :],
                                 x_res[:, bass.ds(t, 1), :].rearrange("p a d -> p (a d)")).then_inc(stored, 16)

            for p in range(NB):
                load(p, p, 0)
            with sp.Fori(1, T // NB) as j:
                for p in range(NB):
                    load(NB * j + p, p, j)
                    store(NB * j + p - NB)
            for t in range(T - NB, T):
                store(t)
            if out_dram is not None:
                sp.wait_ge(stored, 16 * T)

        @block.gpsimd
        def _(pool):
            with pool.Fori(0, T // NB) as j:
                for p in range(NB):
                    wait_alone(pool, idx_ready, NB * j + p + 1)
                    for k in range(TOPK):
                        nc.gpsimd.indirect_dma_start(yg[p][:, k, :], None, ys_dram,
                                                     bass.IndirectOffsetOnAxis(ap=idx[p][:, k:k + 1], axis=0)
                                                     ).then_inc(got[p], 16)

        @block.tensor
        def _(pe):
            pe.wait_ge(loaded, 32)
            with pe.Fori(0, T // NB) as j:
                for p in range(NB):
                    t = NB * j + p
                    pe.wait_ge(x_in[p], 16 * (j + 1))
                    for c in range(DC):
                        mm = nc.tensor.transpose(bx[:, c, :], xt[p][:, c * P:(c + 1) * P], ident[:])
                    mm.then_inc(xT_mm, 1)
                    pe.wait_ge(xT_ready, t + 1)
                    for c in range(DC):
                        mm = nc.tensor.matmul(bg[:, :], xT[:, c, :], wg[:, c, :], start=c == 0, stop=c == DC - 1)
                    mm.then_inc(g_mm, 1)
                    pe.wait_ge(h_ready, t + 1)
                    for c in range(FS // P):
                        mm = nc.tensor.transpose(bh[:, c, :], h[:, c * P:(c + 1) * P], ident[:])
                    mm.then_inc(hT_mm, 1)
                    pe.wait_ge(hT_ready, t + 1)
                    for c in range(FS // P):
                        mm = nc.tensor.matmul(by[:, :], hT[:, c, :], wd[:, c, :], start=c == 0, stop=c == FS // P - 1)
                    mm.then_inc(y_mm, 1)
                    pe.wait_ge(added, NA * t + 1)

        @block.scalar
        def _(act):
            with act.Fori(0, T) as t:
                act.wait_ge(xT_mm, t + 1)
                nc.scalar.copy(xT[:], bx[:]).then_inc(xT_ready, 1)
                act.wait_ge(g_mm, t + 1)
                nc.scalar.activation(th[:], bg[:, 0:FS], ACT.Tanh, scale=0.5).then_inc(th_ready, 1)
                act.wait_ge(hT_mm, t + 1)
                nc.scalar.copy(hT[:], bh[:]).then_inc(hT_ready, 1)

        @block.vector
        def _(dve):
            def rows(t, p, j):
                nc.vector.tensor_copy(idx[p][:], idx_all[:, bass.ds(t, 1), :].rearrange("p a k -> p (a k)")
                                      ).then_inc(idx_ready, 1)

            def tile(t, p, j):
                x = x_res[:, bass.ds(t, 1), :].rearrange("p a d -> p (a d)")
                dve.wait_ge(th_ready, t + 1)
                nc.vector.scalar_tensor_tensor(out=a[:], in0=th[:], scalar=1.0, in1=bg[:, 0:FS],
                                               op0=ALU.add, op1=ALU.mult).then_inc(a_ready, 1)
                dve.wait_ge(a_ready, t + 1)
                nc.vector.scalar_tensor_tensor(out=h[:], in0=a[:], scalar=0.5, in1=bg[:, FS:2 * FS],
                                               op0=ALU.mult, op1=ALU.mult).then_inc(h_ready, 1)
                dve.wait_ge(y_mm, t + 1)
                nc.vector.tensor_tensor(x, by[:], x, ALU.add).then_inc(added, 1)
                dve.wait_ge(got[p], 16 * TOPK * (j + 1))
                for k in range(TOPK):
                    dve.wait_ge(added, NA * t + k + 1)
                    nc.vector.scalar_tensor_tensor(out=x, in0=yg[p][:, k, :],
                                                   scalar=w_all[:, bass.ds(t, 1), k:k + 1].rearrange("p a k -> p (a k)"),
                                                   in1=x, op0=ALU.mult, op1=ALU.add).then_inc(added, 1)
                dve.wait_ge(added, NA * (t + 1))

            for p in range(NB):
                rows(p, p, 0)
            with dve.Fori(0, T // NB - 1) as j:
                for p in range(NB):
                    tile(NB * j + p, p, j)
                    rows(NB * j + p + NB, p, j + 1)
            for p in range(NB):
                tile(T - NB + p, p, T // NB - 1)


def setup(nc, sem, x_dram, x_res, ident, identb, maskb, zrow, tab, wkT_dram, wvT_dram, wdown_dram, wup_dram, kv_dram,
          row_tables):
    DL = wdown_dram.shape[1]
    with ExitStack() as ctx:
        def sb(name, shape, dt=F32):
            return ctx.enter_context(nc.sbuf_tensor(f"{name}_0", shape, dt))

        def ps(name, shape):
            return ctx.enter_context(nc.psum_tensor(f"{name}_0", shape, F32))

        maskf = sb("maskf", [P, 2, P])
        wkT, wvT, wkvT = (sb(n, [P, DC, D]) for n in ("wkT", "wvT", "wkvT"))
        wdown, wup = sb("wdown", [P, DC, DL]), sb("wup", [DL, 2, D])
        foldT = sb("foldT", [DL, D])
        kv = sb("kv", [P, 2, DC, D])
        bank_f, bank_kv = ps("bank_f", [DL, D]), [ps(f"bank_kv{i}", [P, DC, D]) for i in range(2)]
        x_in, c_in, w_in = sem("x_in"), sem("c_in"), sem("w_in")
        summed = sem("summed")
        cast = sem("cast")
        f_mm, f_ready = sem("f_mm"), sem("f_ready")
        kv_mm, kv_ready = sem("kv_mm"), sem("kv_ready")
        kv_out = sem("kv_out")
        rows_out = sem("rows_out")

        block = ctx.enter_context(nc.Block())

        @block.sync
        def _(sp):
            sp.dma_start(x_res[:], x_dram.rearrange("b (t p) d -> p (b t) d", p=P)).then_inc(x_in, 16)
            sp.dma_start(ident[:], tab["ident"]).then_inc(c_in, 16)
            sp.dma_start(maskf[:], tab["mask"]).then_inc(c_in, 16)
            sp.dma_start(wkT[:], wkT_dram.rearrange("(c p) n -> p c n", p=P)).then_inc(w_in, 16)
            sp.dma_start(wvT[:], wvT_dram.rearrange("(c p) n -> p c n", p=P)).then_inc(w_in, 16)
            sp.dma_start(wdown[:], wdown_dram.rearrange("(c p) n -> p c n", p=P)).then_inc(w_in, 16)
            for i in range(2):
                sp.dma_start(wup[:, i, :], wup_dram[i]).then_inc(w_in, 16)
            for name, rows in row_tables.items():
                sp.dma_start(rows, tab[name]).then_inc(rows_out, 16)
            sp.wait_ge(kv_ready, 2)
            for i in range(2):
                sp.dma_start(kv_dram[i].rearrange("(c p) n -> p c n", p=P), kv[:, i, :, :]).then_inc(kv_out, 16)
            sp.wait_ge(kv_out, 32)
            sp.wait_ge(x_in, 16)
            sp.wait_ge(rows_out, 16 * len(row_tables))

        @block.vector
        def _(dve):
            nc.vector.memset(zrow[:], 0.0)
            dve.wait_ge(c_in, 32)
            nc.vector.tensor_copy(identb[:], ident[:])
            nc.vector.tensor_copy(maskb[:], maskf[:]).then_inc(cast, 1)
            dve.wait_ge(w_in, 80)
            nc.vector.tensor_tensor(wkvT[:], wkT[:], wvT[:], ALU.add).then_inc(summed, 1)
            dve.wait_ge(cast, 1)

        @block.tensor
        def _(pe):
            pe.wait_ge(summed, 1)
            for c in range(DC):
                mm = nc.tensor.matmul(bank_f[:, :], wdown[:, c, :], wkvT[:, c, :], start=c == 0, stop=c == DC - 1)
            mm.then_inc(f_mm, 1)
            pe.wait_ge(f_ready, 1)
            for i in range(2):
                for c in range(DC):
                    mm = nc.tensor.matmul(bank_kv[i][:, c, :], foldT[:, c * P:(c + 1) * P], wup[:, i, :],
                                          start=True, stop=True)
                mm.then_inc(kv_mm, 1)

        @block.scalar
        def _(act):
            act.wait_ge(f_mm, 1)
            nc.scalar.copy(foldT[:], bank_f[:, :]).then_inc(f_ready, 1)
            for i in range(2):
                act.wait_ge(kv_mm, i + 1)
                nc.scalar.copy(kv[:, i, :, :], bank_kv[i][:]).then_inc(kv_ready, 1)


@contextmanager
def phase(nc):
    sems = []

    def sem(name):
        sems.append(nc.alloc_semaphore(name=name))
        return sems[-1]

    yield sem
    nc.clear_and_free_semaphores(sems)
    nc.all_engine_barrier()


def hybrid_kernel(nc, ins, out):
    with ExitStack() as ctx:
        def sb(name, shape, dt=F32):
            return ctx.enter_context(nc.sbuf_tensor(name, shape, dt))

        def dram(name, shape):
            return nc.dram_tensor(name, shape, F32, kind="Internal").ap()

        x_res = sb("x_res", [P, T, D])
        ident = sb("ident", [P, P])
        identb = sb("identb", [P, P], BF16)
        maskb = sb("maskb", [P, 2, P], BF16)
        zrow = sb("zrow", [P, D])
        qk_dram = [dram(f"qk{i}", [H, 3, HD, L]) for i in range(3)]
        m_dram = dram("m", [HG * TB, 2, P])
        kv_dram = [dram(f"kv{i}", [D, D]) for i in range(2)]
        row_tables = {n: dram(n, ins[n].shape) for n in ("qrow_a", "krow_a", "qrow_b", "krow_b", "alibi")}
        xs_dram = dram("xs", [XROWS, D])
        ys_dram = dram("ys", [YROWS, D])
        xn_dram = dram("xn", [T * P, D])

        with phase(nc) as sem:
            setup(nc, sem, ins["x"], x_res, ident, identb, maskb, zrow, ins, ins["wkT"], ins["wvT"], ins["wdown"],
                  [ins["wupk"], ins["wupv"]], kv_dram, row_tables)

        def ffn(tag, out_dram):
            with ExitStack() as tables:
                def tsb(name, shape, dt=F32):
                    return tables.enter_context(nc.sbuf_tensor(f"{name}_{tag}", shape, dt))

                run, row_all = tsb("run", [P, E]), tsb("row_all", [P, T, TOPK])
                idx_all, w_all = tsb("idx_all", [P, T, TOPK], U32), tsb("w_all", [P, T, TOPK])
                with ExitStack() as weights:
                    wgu = weights.enter_context(nc.sbuf_tensor(f"wgu_{tag}", [P, E * DC, 2 * FI], F32))
                    wd = weights.enter_context(nc.sbuf_tensor(f"wd_{tag}", [P, E, D], F32))
                    with phase(nc) as sem:
                        route(nc, sem, tag, x_res, ident, ins["gate"], ins["bias"], ins, xs_dram, xn_dram, run,
                              row_all, w_all, wgu, wd, ins["gu"], ins["dn"])
                    with phase(nc) as sem:
                        experts(nc, sem, tag, ident, wgu, wd, ins, run, row_all, idx_all, xs_dram, ys_dram, zrow)
                with phase(nc) as sem:
                    combine(nc, sem, tag, x_res, ident, ins["wsg"], ins["wsd"], xn_dram, ys_dram, idx_all, w_all,
                            out_dram)

        tables = {**ins, **row_tables}
        with phase(nc) as sem:
            attention(nc, sem, False, x_res, ident, identb, maskb, [ins[n] for n in ("a_wq", "a_wk", "a_wv", "a_wo")],
                      tables, [qk_dram[0], qk_dram[2]], m_dram)
        ffn("1", None)
        with phase(nc) as sem:
            attention(nc, sem, True, x_res, ident, identb, maskb, [ins["b_wq"], kv_dram[0], kv_dram[1], ins["b_wo"]],
                      tables, qk_dram, m_dram)
        ffn("2", out.rearrange("b l d -> (b l) d"))


def split12(a):
    high = (a.astype(np.float32).view(np.uint32) & np.uint32(0xFFFFF000)).view(np.float32)
    return high, (a - high).astype(np.float32)


def constants():
    j, p = np.arange(L), np.arange(P)
    mid = L / 2
    slope = (2.0 ** (-8.0 / H)) ** (np.arange(H) + 1)
    t = {"ident": np.eye(P), "alibi": np.stack(split12(slope[:, None] * (j[None, :] - mid)))}
    for name in ("qrow_a", "krow_a", "qrow_b", "krow_b"):
        t[name] = np.zeros((64, L))
    t["qrow_a"][0:2] = 1.0
    t["krow_a"][32:34] = 1.0
    for f, sign in ((0, -1.0), (1, 1.0)):
        high, low = split12(np.exp(sign * LDECAY * (j - mid)))
        t["krow_b"][32 + 4 * f:36 + 4 * f] = [high, low, low, high]
    t["cwin"] = np.zeros((P, L))
    t["cwin"][:, L - P:] = np.where(p[None, :] <= p[:, None], 0.0, NEG)
    t["efac"] = np.broadcast_to(np.stack([np.exp(-LDECAY * (j - mid)), np.exp(LDECAY * (j - mid))]) / 16.0, (P, 2, L))
    t["dwin"] = np.exp(-LDECAY * np.abs(p[:, None] - (np.arange(7 * P) - 3 * P)[None, :]))
    at = p[:, None] + P * np.arange(TB)[None, :] - mid
    t["sfac"] = np.stack([np.exp(LDECAY * at), np.exp(-LDECAY * at)], 1)
    t["mfac"] = np.exp(LDECAY * at)
    t["mask"] = np.stack([np.where(p[None, :] >= p[:, None], 0.0, NEG), np.where(p[None, :] < p[:, None], 0.0, NEG)], 1)
    t["base"] = np.broadcast_to(np.arange(E) * CAP + 1.0, (P, E))
    t["before"] = p[:, None] < p[None, :]
    t["sidx"] = 4.0 * p[:, None] + np.arange(4)[None, :]
    return {k: np.ascontiguousarray(a, np.float32) for k, a in t.items()}


def kernel(**inputs):
    import concourse.bacc as bacc
    from concourse.bass_utils import run_bass_kernel_spmd

    def turned(a, *axes):
        return np.ascontiguousarray(np.transpose(a, axes))

    i = {k: np.asarray(a) for k, a in inputs.items()}
    arrays = {
        "x": i["L0_attn_a_x"],
        "a_wq": i["L0_attn_a_q_w"], "a_wk": i["L0_attn_a_k_w"], "a_wv": i["L0_attn_a_v_w"], "a_wo": i["L0_attn_a_o_w"],
        "b_wq": i["L0_attn_b_W_q"], "b_wo": i["L0_attn_b_W_o"],
        "wkT": turned(i["L0_attn_b_W_k"], 1, 0), "wvT": turned(i["L0_attn_b_W_v"], 1, 0),
        "wdown": i["L0_attn_b_W_down_kv"], "wupk": i["L0_attn_b_W_up_k"], "wupv": i["L0_attn_b_W_up_v"],
        "gate": turned(i["L0_ffn_gate_weight"], 1, 0), "bias": i["L0_ffn_e_score_correction_bias"],
        "gu": turned(i["L0_ffn_experts_gate_up"], 0, 2, 1), "dn": turned(i["L0_ffn_experts_down"], 0, 2, 1),
        "wsg": np.concatenate([turned(i["L0_ffn_shared_gate_w"], 1, 0), turned(i["L0_ffn_shared_up_w"], 1, 0)], 1),
        "wsd": turned(i["L0_ffn_shared_down_w"], 1, 0),
        **constants(),
    }
    nc = bacc.Bacc("TRN2", target_bir_lowering=False, num_devices=1)
    ins = {k: nc.dram_tensor(f"in_{k}", a.shape, mybir.dt.from_np(a.dtype), kind="ExternalInput").ap()
           for k, a in arrays.items()}
    out = nc.dram_tensor("out", (B, L, D), F32, kind="ExternalOutput").ap()
    hybrid_kernel(nc, ins, out)
    r = run_bass_kernel_spmd(nc, [{f"in_{k}": np.ascontiguousarray(a) for k, a in arrays.items()}], core_ids=[0])
    return r.results[0]["out"]
```

```python
from contextlib import ExitStack, contextmanager

import numpy as np

import concourse.bass as bass
from concourse import mybir

F32 = mybir.dt.float32
F32R = mybir.dt.float32r
BF16 = mybir.dt.bfloat16
I32 = mybir.dt.int32
U32 = mybir.dt.uint32
ALU = mybir.AluOpType
ACT = mybir.ActivationFunctionType
AX = mybir.AxisListType

P = 128
B, L, D = 8, 512, 256
T = B * L // P
TB = L // P
DC = D // P
H, HD = 16, 16
G, HG = 4, 4
E, FI = 32, 128
FS = 2 * FI
TOPK, NGROUP, TOPG = 6, 8, 4
EG = E // NGROUP
ROUTE_SCALE = 2.5
LDECAY = 0.01
EPS = 1e-5
NEG = -1e30
LOW, HIGH = -3e38, 3e38
CAP = T * P + P
NSLOT = T * TOPK + E
XROWS = E * CAP + P
YROWS = NSLOT * P


def wait(eng, sem, value):
    if isinstance(value, int) and value <= 0:
        return
    eng.wait_ge(sem, value)


def wait_alone(eng, sem, value):
    if isinstance(value, int) and value <= 0:
        return
    eng.wait_ge(sem, value)
    eng.nop(nofuse=True)


class Ring:

    def __init__(self, banks, plan):
        self.banks, self.plan = banks, plan
        self.at, self.held = 0, [None] * len(banks)

    def __getitem__(self, key):
        return self.banks[self.plan.index(key) % len(self.banks)]

    def take(self, pe, key, freed):
        assert self.plan[self.at] == key, (self.plan[self.at], key)
        i = self.at % len(self.banks)
        if self.held[i] is not None:
            pe.wait_ge(*self.held[i])
        self.held[i] = freed
        self.at += 1
        return self.banks[i]


def attention(nc, sem, decayed, x_res, ident, identb, maskb, w_dram, tab, qk_dram, m_dram,
              chosen=None):
    tag = "b" if decayed else "a"
    forms = 2 if decayed else 1
    qscale = 1.0 / 16.0 if decayed else 1.0 / 4.0
    NQK = 2 * (forms + 1)
    NHL = 3 if decayed else 4
    UNITS = 2 * TB * forms
    ROWS = 104 if decayed else 98
    NP1 = H * TB
    NP2 = G * UNITS
    duos = [(kb, f) for kb in range(TB) for f in range(forms)]
    ND = len(duos)
    NMI = 2 * forms * forms

    parts = ([(f, half) for half in range(2) for f in range(forms)] + [(forms, half) for half in range(2)])
    stores = [3 if f == forms else 2 for f, _ in parts]

    def stored(buf, n, j):
        every = sum(c for i, c in enumerate(stores) if i % NHL == buf)
        return every * n + sum(c for i, c in enumerate(stores[:j]) if i % NHL == buf)

    def span(kb, f):
        return (kb * P, L) if f == 0 else (0, (kb + 1) * P)

    QUARTER = ND // 4

    def stages(g, d, first, last):
        if d % QUARTER:
            return []
        before, now, after = {
            (0, 0): ([], [], [("ln", 0)]),
            (0, 1): ([("oT", -1)], [], [("scale", 0)]),
            (0, 2): ([], [], [("xT", 0)]),
            (0, 3): ([], [], [("q", 0)]),
            (1, 0): ([("onT", 0)], [], [("k", 0)]),
            (1, 1): ([], [("oT", 0)], []),
            (1, 2): ([("y", 0)], [], []),
            (1, 3): ([], [], [("v", 0)]),
            (2, 1): ([], [("oT", 1)], []),
            (3, 1): ([], [("oT", 2)], []),
        }.get((g, d // QUARTER), ([], [], []))
        return before * (not first) + now + after * (not last)

    def tiles(g, d, last):
        each = HG * TB // ND
        return [(g + 2, i) for i in range(d * each, d * each + each) if not (last and g + 2 >= G)]

    def moves_max(g, d, last):
        return d == 0 and not (last and g == G - 1)

    def banks_of(stage, r):
        return {"ln": [], "scale": [], "oT": [("oT", r)]}.get(stage, [(stage, i) for i in range(2)])

    def plan_round(first, last):
        plan = []
        for g in range(G):
            for d in range(ND):
                plan += [("p1", r, i) for r, i in tiles(g, d, last)]
                if moves_max(g, d, last):
                    plan.append(("mT", g + 1))
                for stage, r in stages(g, d, first, last):
                    plan += banks_of(stage, r)
        return plan

    plan_start = ([k for stage in ("xT", "q", "k", "v") for k in banks_of(stage, 0)]
                  + [("p1", 4, i) for i in range(HG * TB)] + [("mT", 4)] + [("p1", 5, i) for i in range(HG * TB)])
    plan_end = [("oT", -1), ("onT", 0), ("onT", 1), ("y", 0), ("y", 1)]

    with ExitStack() as ctx:
        def sb(name, shape, dt=F32):
            return ctx.enter_context(nc.sbuf_tensor(f"{name}_{tag}", shape, dt))

        def ps(name, shape):
            return ctx.enter_context(nc.psum_tensor(f"{name}_{tag}", shape, F32))

        def s(name):
            return sem(f"{name}_{tag}")

        wq, wk, wv, wo = (sb(n, [P, DC, D]) for n in ("wq", "wk", "wv", "wo"))
        qst = [[sb(f"qst{f}_{g}", [ROWS, HG, L], F32R) for g in range(G)] for f in range(forms)]
        kst = [sb(f"kst{g}", [ROWS, HG, L], F32R) for g in range(G)]
        xn_onT = sb("xn_onT", [P, TB * D])
        xn = xn_onT[:].rearrange("p (t d) -> p t d", t=TB)
        onT = xn_onT[:].rearrange("p (c l) -> p c l", c=DC)
        xT = sb("xT", [P, DC, L])
        hi = [sb(f"hi{i}", [P, L], F32R) for i in range(NHL)]
        lo = [sb(f"lo{i}", [P, L], F32R) for i in range(NHL)]
        v_all = sb("v_all", [P, TB, D])
        v = sb("v", [P, TB, H * (HD + 1) + 32 - (HD + 1)])
        pt = [[sb(f"pt{i}{j}", [P, 2, L]) for j in range(2)] for i in range(2)]
        oT = sb("oT", [P, L])
        on = sb("on", [P, TB, D])
        mcol = [sb(f"mcol{i}", [P, HG, TB]) for i in range(2)]
        mhl = sb("mhl", [HG * TB, 2, P], F32R)
        rec = sb("rec", [P, TB, HG])
        stats = sb("stats", [P, TB, 6])
        mv = sb("mv", [P, TB, 2])
        ve = sb("ve", [P, TB])
        rstd = sb("rstd", [P, TB])
        mhalf = sb("mhalf", [P, TB])
        if decayed:
            qf = [sb(f"qf{i}", [P, L]) for i in range(2)]
            efac = sb("efac", [P, 2, L])
            dwin = sb("dwin", [P, 7 * P])
            sfac = sb("sfac", [P, 2, TB])
            mfac = sb("mfac", [P, TB])
            mpost = [sb("mpost", [P, HG, TB])] * 2
        else:
            cwin = sb("cwin", [P, L])
            mpost = mcol

        rbank = [ps(f"r{i}", [P, 512]) for i in range(3)]
        sbank = [ps(f"s{i}", [P, 2, 512]) for i in range(2)]
        obank = ps("o", [P, 512])
        ring_start, ring_end = Ring(rbank, plan_start), Ring(rbank, plan_end)
        rings = {(first, last): Ring(rbank, plan_round(first, last))
                 for first, last in ((True, False), (False, False), (False, True))}

        loaded = s("loaded")
        tabs = s("tabs")
        half_set = s("half_set")
        v_set = s("v_set")
        ln = s("ln")
        var_ready = s("var_ready")
        rstd_ready = s("rstd_ready")
        xn_ready = s("xn_ready")
        xT_mm = s("xT_mm")
        xT_a, xT_v = s("xT_a"), s("xT_v")
        qk_mm = s("qk_mm")
        qf_ready = s("qf_ready")
        hi_ready = s("hi_ready")
        lo_ready = s("lo_ready")
        hl_out = [s(f"hl_out{i}") for i in range(NHL)]
        st_ready = [s(f"st_ready{g}") for g in range(G)]
        v_mm = s("v_mm")
        v_out = s("v_out")
        v_ready = s("v_ready")
        p1_mm = s("p1_mm")
        p1_max = s("p1_max")
        m_ready = s("m_ready")
        mT_mm = s("mT_mm")
        mh_ready = s("mh_ready")
        ml_ready = s("ml_ready")
        m_out = s("m_out")
        m_in = s("m_in")
        s_mm = s("s_mm")
        p_ready = s("p_ready")
        pv_done = s("pv_done")
        o_ready = s("o_ready")
        oT_mm = s("oT_mm")
        rec_ready = s("rec_ready")
        on_ready = s("on_ready")
        onT_mm = s("onT_mm")
        onT_ready = s("onT_ready")
        y_mm = s("y_mm")
        x_added = s("x_added")
        maxed = m_ready if decayed else p1_max
        if chosen:
            ys_dram, idx_all, w_all = chosen
            NY = 4
            yg = [sb(f"yg{i}", [P, D]) for i in range(NY)]
            idx = sb("cidx", [P, TB, TOPK], U32)
            idx_ready = s("cidx_ready")
            got = [s(f"cgot{i}") for i in range(NY)]
            y_added = s("cadded")
        NADD = TB * TOPK

        def maxed_at(n, g):
            return G * n + g + 1 if decayed else NP1 * n + HG * TB * (g + 1)

        tables = [(efac, "efac"), (dwin, "dwin"), (sfac, "sfac"), (mfac, "mfac")] if decayed else [(cwin, "cwin")]
        LOADED = 16 * (4 + len(tables))
        TABS = 16 * G * (forms + 1 + (not decayed))

        block = ctx.enter_context(nc.Block())

        @block.sync
        def _(sp):
            for t_, d_ in zip((wq, wk, wv, wo), w_dram):
                sp.dma_start(t_[:], d_.rearrange("(c p) n -> p c n", p=P)).then_inc(loaded, 16)
            for t_, name in tables:
                sp.dma_start(t_[:], tab[name]).then_inc(loaded, 16)

            def store_halves(n):
                for g in range(G):
                    wait_alone(sp, st_ready[g], 32 * (forms + 1) * n)
                for j, (f, half) in enumerate(parts):
                    sp.wait_ge(lo_ready, NQK * n + j + 1)
                    for r, part in enumerate((hi, lo, hi)[:stores[j]]):
                        sp.dma_start(qk_dram[f][8 * half:8 * half + 8, r, :, :],
                                     part[j % NHL][:].bitcast(F32)).then_inc(hl_out[j % NHL], 16)

            def load_stack(n, r):
                g, n_ = r % G, n + r // G
                if g == 0:
                    for i in range(NHL):
                        wait_alone(sp, hl_out[i], 16 * stored(i, n_ + 1, 0))
                heads = slice(HG * g, HG * g + HG)
                wait_alone(sp, pv_done, ND * (G * n + r - G + 1))
                for d in range(2):
                    for f in range(forms):
                        sp.dma_start(qst[f][g][32 * d:32 * d + 32, :, :].bitcast(F32),
                                     qk_dram[f][heads, 0:2].rearrange("h r d t -> (r d) h t")
                                     ).then_inc(st_ready[g], 16)
                    sp.dma_start(kst[g][32 * d:32 * d + 32, :, :].bitcast(F32),
                                 qk_dram[forms][heads, d:d + 2].rearrange("h r d t -> (r d) h t")
                                 ).then_inc(st_ready[g], 16)

            def load_max(n, r):
                k, g = G * n + r, r % G
                wait_alone(sp, ml_ready, k + 1)
                wait(sp, m_in, 16 * NMI * k)
                sp.dma_start(m_dram, mhl[:].bitcast(F32)).then_inc(m_out, 16)
                sp.wait_ge(m_out, 16 * (k + 1))
                for f in range(forms):
                    for d in range(forms):
                        for r in range(2):
                            row = 96 + 4 * f + 2 * d + r
                            sp.dma_start(qst[f][g][row:row + 1, :, :].bitcast(F32),
                                         m_dram.rearrange("(h q) r t -> r h q t", q=TB)[r:r + 1]
                                         ).then_inc(m_in, 16)

            store_halves(0)
            for g in range(G):
                load_stack(0, g)
            load_max(0, 0)

            def round_(n, last):
                for g in range(G):
                    if not (last and g == G - 1):
                        load_max(n, g + 1)
                    if not last:
                        if g == 0:
                            store_halves(n + 1)
                        load_stack(n, g + G)

            with sp.Fori(0, B - 1) as n:
                round_(n, False)
            round_(B - 1, True)
            sp.wait_ge(m_in, 16 * NMI * G * B)

        @block.gpsimd
        def _(pool):
            nc.gpsimd.memset(mhalf[:], -0.5).then_inc(half_set, 1)
            nc.gpsimd.memset(v[:], 1.0).then_inc(v_set, 1)
            pool.wait_ge(v_set, 1)
            pool.wait_ge(half_set, 1)

            def roots(n):
                pool.wait_ge(var_ready, n + 1)
                nc.gpsimd.tensor_tensor(rstd[:], ve[:], mhalf[:], ALU.pow).then_inc(rstd_ready, 1)

            def place_v(n, g):
                wait_alone(pool, v_out, 2 * n + 2)
                wait_alone(pool, pv_done, ND * (G * (n - 1) + g + 1))
                nc.gpsimd.tensor_copy(v[:, :, 0:H * (HD + 1)].rearrange("p t (h x) -> p t h x", h=H)[:, :, HG * g:HG * g + HG, 0:HD],
                                      v_all[:, :, HG * HD * g:HG * HD * (g + 1)].rearrange("p t (h d) -> p t h d", h=HG)
                                      ).then_inc(v_ready, 1)

            def gather(q, i):
                for m in range(TOPK * i, TOPK * (i + 1)):
                    if m == 0:
                        wait_alone(pool, idx_ready, q + 1)
                    wait_alone(pool, y_added, NADD * q + m - NY + 1)
                    nc.gpsimd.indirect_dma_start(yg[m % NY][:], None, ys_dram,
                                                 bass.IndirectOffsetOnAxis(ap=idx[:, i, m % TOPK:m % TOPK + 1], axis=0)
                                                 ).then_inc(got[m % NY], 16)

            if chosen:
                for i in range(TB):
                    gather(0, i)
            roots(0)
            if chosen:
                for i in range(TB):
                    gather(1, i)
            for g in range(G - 1):
                place_v(0, g)

            def round_(n, more):
                roots(n + 1)
                for g in range(G):
                    if more and chosen:
                        gather(n + 2, g)
                    if g == 0:
                        place_v(n, G - 1)
                    else:
                        place_v(n + 1, g - 1)

            round_(0, True)
            with pool.Fori(1, B - 2) as n:
                round_(n, True)
            round_(B - 2, False)
            place_v(B - 1, G - 1)

        @block.tensor
        def _(pe):
            def transpose_x(ring, n):
                pe.wait_ge(xn_ready, n + 1)
                for c in range(DC):
                    bank = ring.take(pe, ("xT", c), ((xT_a, xT_v)[c], n + 1))
                    for i in range(TB):
                        mm = nc.tensor.transpose(bank[:, i * P:(i + 1) * P], xn[:, i, c * P:(c + 1) * P], ident[:])
                    mm.then_inc(xT_mm, 1)

            def project(ring, n, name):
                pe.wait_ge(xT_a, n + 1)
                pe.wait_ge(xT_v, n + 1)
                w = wq if name == "q" else wk
                for half in range(2):
                    if name == "k":
                        freed = (lo_ready, NQK * n + 2 * forms + half + 1)
                    elif decayed:
                        freed = (qf_ready, 2 * forms * n + forms * (half + 1))
                    else:
                        freed = (lo_ready, NQK * n + half + 1)
                    bank = ring.take(pe, (name, half), freed)
                    for c in range(DC):
                        mm = nc.tensor.matmul(bank[:, :], w[:, c, half * P:(half + 1) * P], xT[:, c, :],
                                              start=c == 0, stop=c == DC - 1)
                    mm.then_inc(qk_mm, 1)

            def project_v(ring, n):
                for j in range(2):
                    bank = ring.take(pe, ("v", j), (v_out, 2 * n + j + 1))
                    for i in range(2):
                        for c in range(DC):
                            mm = nc.tensor.matmul(bank[:, i * D:(i + 1) * D],
                                                  xT[:, c, (2 * j + i) * P:(2 * j + i + 1) * P], wv[:, c, :],
                                                  start=c == 0, stop=c == DC - 1)
                    mm.then_inc(v_mm, 1)

            def pass1(ring, n, r, i):
                g, h, qb = r % G, i // TB, i % TB
                if i == 0:
                    pe.wait_ge(st_ready[g], 32 * (forms + 1) * (n + r // G + 1))
                bank = ring.take(pe, ("p1", r, i), (p1_max, HG * TB * (G * n + r) + i + 1))
                cols = L if decayed else (qb + 1) * P
                nc.tensor.matmul(bank[:, 0:cols], qst[0][g][0:96, h, qb * P:(qb + 1) * P],
                                 kst[g][0:96, h, 0:cols], start=True, stop=True).then_inc(p1_mm, 1)

            def transpose_max(ring, n, r):
                pe.wait_ge(maxed, maxed_at(n, r))
                bank = ring.take(pe, ("mT", r), (ml_ready, G * n + r + 1))
                nc.tensor.transpose(bank[0:HG * TB, 0:P], mpost[r % 2][:].rearrange("p h q -> p (h q)"),
                                    ident[:]).then_inc(mT_mm, 1)

            def scores(n, g, d):
                kb, f = duos[d]
                q0, q1 = span(kb, f)
                if d == 0:
                    pe.wait_ge(m_in, 16 * NMI * (G * n + g + 1))
                for pair in range(2):
                    pe.wait_ge(p_ready, NP2 * n + UNITS * g + 2 * d + pair + 1)
                    for hh in range(2):
                        h = 2 * pair + hh
                        nc.tensor.matmul(sbank[pair][:, hh, q0:q1], kst[g][:, h, kb * P:(kb + 1) * P],
                                         qst[f][g][:, h, q0:q1], start=True, stop=False)
                        mm = nc.tensor.matmul(sbank[pair][:, hh, kb * P:(kb + 1) * P], identb[:],
                                              maskb[:, f, :], start=False, stop=True)
                    mm.then_inc(s_mm, 1)

            def weigh(n, r, d):
                kb, f = duos[d]
                q0, q1 = span(kb, f)
                k = G * n + r
                if d == 0:
                    pe.wait_ge(o_ready, k + 1)
                    pe.wait_ge(v_ready, k + 1 + (r % G < G - 1))
                pe.wait_ge(p_ready, UNITS * k + 2 * d + 2 + 2)
                for h in range(HG):
                    mm = nc.tensor.matmul(obank[32 * h:32 * h + 32, q0:q1], v[:, kb, (HG * (r % G) + h) * (HD + 1):(HG * (r % G) + h) * (HD + 1) + 32],
                                          pt[d % 2][h // 2][:, h % 2, q0:q1],
                                          start=d == 0, stop=d == ND - 1)
                mm.then_inc(pv_done, 1)

            def untranspose(ring, n, r):
                k = G * n + r
                pe.wait_ge(o_ready, k + 2)
                bank = ring.take(pe, ("oT", r), (on_ready, k + 1))
                for qb in range(TB):
                    mm = nc.tensor.transpose(bank[:, qb * P:(qb + 1) * P], oT[:, qb * P:(qb + 1) * P], ident[:])
                mm.then_inc(oT_mm, 1)

            def transpose_o(ring, n):
                pe.wait_ge(on_ready, G * (n + 1))
                for c in range(DC):
                    bank = ring.take(pe, ("onT", c), (onT_ready, 2 * n + c + 1))
                    for i in range(TB):
                        mm = nc.tensor.transpose(bank[:, i * P:(i + 1) * P], on[:, i, c * P:(c + 1) * P], ident[:])
                    mm.then_inc(onT_mm, 1)

            def project_o(ring, n):
                pe.wait_ge(onT_ready, 2 * n + 2)
                for j in range(2):
                    bank = ring.take(pe, ("y", j), (x_added, 2 * n + j + 2))
                    for i in range(2):
                        for c in range(DC):
                            mm = nc.tensor.matmul(bank[:, i * D:(i + 1) * D],
                                                  onT[:, c, (2 * j + i) * P:(2 * j + i + 1) * P], wo[:, c, :],
                                                  start=c == 0, stop=c == DC - 1)
                    mm.then_inc(y_mm, 1)

            def stage(ring, n, name, r):
                if name == "xT":
                    transpose_x(ring, n + 1)
                elif name in ("q", "k"):
                    project(ring, n + 1, name)
                elif name == "v":
                    project_v(ring, n + 1)
                elif name == "oT":
                    untranspose(ring, n, r)
                elif name == "onT":
                    transpose_o(ring, n - 1)
                elif name == "y":
                    project_o(ring, n - 1)

            pe.wait_ge(loaded, LOADED)
            for name, r in (("xT", 0), ("q", 0), ("k", 0), ("v", 0)):
                stage(ring_start, -1, name, r)
            pe.wait_ge(tabs, TABS)
            for i in range(HG * TB):
                pass1(ring_start, -1, 4, i)
            transpose_max(ring_start, -1, 4)
            for i in range(HG * TB):
                pass1(ring_start, -1, 5, i)

            def round_(n, first, last):
                ring = rings[first, last]
                for g in range(G):
                    for d in range(ND):
                        scores(n, g, d)
                        if g == d == 0:
                            pe.wait_ge(p1_max, NP1 * n + HG * TB * 2)
                            pe.wait_ge(on_ready, G * n - 1) if not first else pe.wait_ge(ml_ready, 1)
                        for r, i in tiles(g, d, last):
                            pass1(ring, n, r, i)
                        if moves_max(g, d, last):
                            transpose_max(ring, n, g + 1)
                        for name, r in stages(g, d, first, last):
                            stage(ring, n, name, r)
                        if d:
                            weigh(n, g, d - 1)
                        elif not (first and g == 0):
                            weigh(n, g - 1, ND - 1)

            round_(0, True, False)
            with pe.Fori(1, B - 1) as n:
                round_(n, False, False)
            round_(B - 1, False, True)
            weigh(B, -1, ND - 1)
            pe.wait_ge(p1_max, NP1 * B)
            pe.wait_ge(on_ready, G * B - 1)
            stage(ring_end, B, "oT", -1)
            stage(ring_end, B, "onT", 0)
            stage(ring_end, B, "y", 0)

        @block.scalar
        def _(act):
            nc.scalar.nop().then_inc(p_ready, 2)
            for g in range(G):
                for f in range(forms):
                    act.dma_start(qst[f][g][64:ROWS, :, :].bitcast(F32),
                                  tab["qrow_" + tag].unsqueeze(1).broadcast_to([ROWS - 64, HG, L])).then_inc(tabs, 16)
                first_row = 0 if decayed else 2
                act.dma_start(kst[g][64 + first_row:ROWS, :, :].bitcast(F32),
                              tab["krow_" + tag][first_row:].unsqueeze(1).broadcast_to([ROWS - 64 - first_row, HG, L])
                              ).then_inc(tabs, 16)
                if not decayed:
                    act.dma_start(kst[g][64:66, :, :].bitcast(F32),
                                  tab["alibi"][:, HG * g:HG * g + HG, :]).then_inc(tabs, 16)
            act.wait_ge(v_set, 1)

            def copy_x(ring, n):
                act.wait_ge(xT_mm, 2 * n + 1)
                nc.scalar.copy(xT[:, 0, :], ring["xT", 0][:, :]).then_inc(xT_a, 1)

            def high_halves(ring, n, name):
                for j, (f, half) in enumerate(parts):
                    if (f == forms) != (name == "k"):
                        continue
                    if j >= NHL:
                        act.wait_ge(hl_out[j % NHL], 16 * stored(j % NHL, n, j))
                    else:
                        wait(act, hl_out[j % NHL], 16 * stored(j % NHL, n, 0))
                    if decayed and f < forms:
                        act.wait_ge(qf_ready, 2 * forms * n + j + 1)
                        nc.scalar.copy(hi[j % NHL][:], qf[j % 2][:]).then_inc(hi_ready, 1)
                    else:
                        act.wait_ge(qk_mm, 4 * n + (2 if f == forms else 0) + half + 1)
                        nc.scalar.activation(hi[j % NHL][:], ring[name, half][:, :],
                                             ACT.Copy, scale=1.0 if f == forms else qscale).then_inc(hi_ready, 1)

            def copy_v(ring, n):
                for j in range(2):
                    act.wait_ge(v_mm, 2 * n + j + 1)
                    wait(act, v_ready, G * n)
                    nc.scalar.copy(v_all[:, 2 * j:2 * j + 2, :].rearrange("p t d -> p (t d)"),
                                   ring["v", j][:, :]).then_inc(v_out, 1)

            def split_max(ring, n, r):
                k = G * n + r
                act.wait_ge(mT_mm, k + 1)
                wait(act, m_out, 16 * k)
                nc.scalar.mul(mhl[:, 0, :], ring["mT", r][0:HG * TB, 0:P], -1.0).then_inc(mh_ready, 1)

            def exps(n, g, d):
                kb, f = duos[d]
                q0, q1 = span(kb, f)
                for pair in range(2):
                    act.wait_ge(s_mm, NP2 * n + UNITS * g + 2 * d + pair + 1)
                    nc.scalar.activation(pt[d % 2][pair][:, :, q0:q1], sbank[pair][:, :, q0:q1], ACT.Exp,
                                         scale=sfac[:, f, kb:kb + 1] if decayed else 1.0).then_inc(p_ready, 1)

            def copy_o(ring, n):
                for c in range(DC):
                    act.wait_ge(onT_mm, 2 * n + c + 1)
                    nc.scalar.copy(onT[:, c, :], ring["onT", c][:, :]).then_inc(onT_ready, 1)

            def stage(ring, n, name, r):
                if name == "xT":
                    copy_x(ring, n + 1)
                elif name in ("q", "k"):
                    high_halves(ring, n + 1, name)
                elif name == "v":
                    copy_v(ring, n + 1)
                elif name == "onT":
                    copy_o(ring, n - 1)

            for name, r in (("xT", 0), ("q", 0), ("k", 0), ("v", 0)):
                stage(ring_start, -1, name, r)
            split_max(ring_start, -1, 4)
            if decayed:
                act.wait_ge(loaded, LOADED)

            def round_(n, first, last):
                ring = rings[first, last]
                for g in range(G):
                    for d in range(ND):
                        exps(n, g, d)
                        if moves_max(g, d, last):
                            split_max(ring, n, g + 1)
                        for name, r in stages(g, d, first, last):
                            stage(ring, n, name, r)

            round_(0, True, False)
            with act.Fori(1, B - 1) as n:
                round_(n, False, False)
            round_(B - 1, False, True)
            stage(ring_end, B, "onT", 0)

        @block.vector
        def _(dve):
            nc.vector.nop().then_inc(o_ready, 1)
            nc.vector.nop().then_inc(x_added, 1)

            def rows(q):
                nc.vector.tensor_copy(idx[:], idx_all[:, bass.ds(q * TB, TB), :]).then_inc(idx_ready, 1)

            def add_chosen(q, m):
                i, k = m // TOPK, m % TOPK
                dve.wait_ge(got[m % NY], 16 * (NADD // NY * q + m // NY + 1))
                wait(dve, y_added, NADD * q + m)
                x = x_res[:, bass.ds(q * TB + i, 1), :].rearrange("p a d -> p (a d)")
                nc.vector.scalar_tensor_tensor(out=x, in0=yg[m % NY][:],
                                               scalar=w_all[:, bass.ds(q * TB + i, 1), k:k + 1].rearrange("p a k -> p (a k)"),
                                               in1=x, op0=ALU.mult, op1=ALU.add).then_inc(y_added, 1)

            def variances(n):
                if chosen:
                    dve.wait_ge(y_added, NADD * (n + 1))
                for i in range(TB):
                    st = nc.vector.bn_stats(stats[:, i, :], x_res[:, bass.ds(n * TB + i, 1), :].rearrange("p a d -> p (a d)"))
                st.then_inc(ln, 1)
                wait_alone(dve, ln, 2 * n + 1)
                for i in range(TB):
                    st = nc.vector.bn_aggr(mv[:, i, :], stats[:, i, :])
                st.then_inc(ln, 1)
                dve.wait_ge(ln, 2 * n + 2)
                nc.vector.tensor_scalar_add(ve[:], mv[:, :, 1], EPS).then_inc(var_ready, 1)

            def scale(n):
                dve.wait_ge(rstd_ready, n + 1)
                for i in range(TB):
                    st = nc.vector.tensor_scalar(xn[:, i, :], x_res[:, bass.ds(n * TB + i, 1), :].rearrange("p a d -> p (a d)"),
                                                 mv[:, i, 0:1], rstd[:, i:i + 1], ALU.subtract, ALU.mult)
                st.then_inc(xn_ready, 1)

            def copy_x(ring, n):
                dve.wait_ge(xT_mm, 2 * n + 2)
                nc.vector.tensor_copy(xT[:, 1, :], ring["xT", 1][:, :]).then_inc(xT_v, 1)

            def low(ring, n, j):
                f, half = parts[j]
                dve.wait_ge(hi_ready, NQK * n + j + 1)
                high = hi[j % NHL][:].bitcast(F32)
                if decayed and f < forms:
                    nc.vector.tensor_tensor(lo[j % NHL][:], qf[j % 2][:], high, ALU.subtract).then_inc(lo_ready, 1)
                else:
                    nc.vector.scalar_tensor_tensor(out=lo[j % NHL][:], in0=ring["k" if f == forms else "q", half][:, :],
                                                   scalar=1.0 if f == forms else qscale, in1=high,
                                                   op0=ALU.mult, op1=ALU.subtract).then_inc(lo_ready, 1)

            def low_halves(ring, n, name):
                if name == "k":
                    for j in range(2 * forms, NQK):
                        low(ring, n, j)
                elif not decayed:
                    for j in range(2 * forms):
                        low(ring, n, j)
                else:
                    for j in range(2 * forms):
                        f, half = parts[j]
                        dve.wait_ge(qk_mm, 4 * n + half + 1)
                        wait(dve, lo_ready, NQK * n + max(j - 1, 0))
                        nc.vector.tensor_tensor(qf[j % 2][:], ring["q", half][:, :], efac[:, f, :],
                                                ALU.mult).then_inc(qf_ready, 1)
                        dve.wait_ge(qf_ready, 2 * forms * n + j + 1)
                        if j:
                            low(ring, n, j - 1)
                    low(ring, n, 2 * forms - 1)

            def maximum(ring, n, r, i):
                wait_alone(dve, p1_mm, HG * TB * (G * n + r) + i + 1)
                h, qb = i // TB, i % TB
                bank = ring["p1", r, i]
                cols = L if decayed else (qb + 1) * P
                other = dwin[:, (TB - 1 - qb) * P:(TB - 1 - qb) * P + L] if decayed else cwin[:, L - cols:L]
                nc.vector.tensor_tensor_reduce(out=bank[:, 0:cols], in0=bank[:, 0:cols], in1=other, scale=1.0,
                                               scalar=LOW, op0=ALU.mult if decayed else ALU.add, op1=ALU.max,
                                               accum_out=mcol[r % 2][:, h, qb:qb + 1]).then_inc(p1_max, 1)
                if decayed and i == HG * TB - 1:
                    dve.wait_ge(p1_max, HG * TB * (G * n + r + 1))
                    nc.vector.tensor_tensor(mpost[0][:], mcol[r % 2][:], mfac[:].unsqueeze(1).broadcast_to([P, HG, TB]),
                                            ALU.mult).then_inc(m_ready, 1)

            def split_max(ring, n, r):
                dve.wait_ge(mh_ready, G * n + r + 1)
                nc.vector.scalar_tensor_tensor(out=mhl[:, 1, :], in0=ring["mT", r][0:HG * TB, 0:P], scalar=-1.0,
                                               in1=mhl[:, 0, :].bitcast(F32), op0=ALU.mult,
                                               op1=ALU.subtract).then_inc(ml_ready, 1)

            def copy_o(n, r):
                dve.wait_ge(pv_done, ND * (G * n + r + 1))
                nc.vector.tensor_copy(oT[:], obank[:, :]).then_inc(o_ready, 1)

            def normalise(ring, n, r):
                k = G * n + r
                dve.wait_ge(oT_mm, k + 1)
                o4 = ring["oT", r][:, :].rearrange("p (q h x) -> p q h x", q=TB, h=HG)
                nc.vector.reciprocal(rec[:], o4[:, :, :, HD]).then_inc(rec_ready, 1)
                dve.wait_ge(rec_ready, k + 1)
                heads = slice(HG * HD * (r % G), HG * HD * (r % G + 1))
                nc.vector.tensor_tensor(on[:, :, heads].rearrange("p q (h d) -> p q h d", h=HG),
                                        o4[:, :, :, 0:HD], rec[:].unsqueeze(3).broadcast_to([P, TB, HG, HD]),
                                        ALU.mult).then_inc(on_ready, 1)

            def add(ring, n):
                for j in range(2):
                    dve.wait_ge(y_mm, 2 * n + j + 1)
                    xr = x_res[:, bass.ds(n * TB + 2 * j, 2), :].rearrange("p a d -> p (a d)")
                    nc.vector.tensor_tensor(xr, ring["y", j][:, :], xr, ALU.add).then_inc(x_added, 1)

            def stage(ring, n, name, r):
                if name == "ln":
                    variances(n + 1)
                elif name == "scale":
                    scale(n + 1)
                elif name == "xT":
                    copy_x(ring, n + 1)
                elif name in ("q", "k"):
                    low_halves(ring, n + 1, name)
                elif name == "oT":
                    normalise(ring, n, r)
                elif name == "y":
                    add(ring, n - 1)

            if chosen:
                rows(0)
                for m in range(NADD):
                    add_chosen(0, m)
                rows(1)
            stage(ring_start, -1, "ln", 0)
            stage(ring_start, -1, "scale", 0)
            dve.wait_ge(loaded, LOADED)
            for name in ("xT", "q", "k"):
                stage(ring_start, -1, name, 0)
            if chosen:
                for m in range(NADD):
                    add_chosen(1, m)
            for i in range(HG * TB):
                maximum(ring_start, -1, 4, i)
            split_max(ring_start, -1, 4)
            for i in range(HG * TB):
                maximum(ring_start, -1, 5, i)

            def round_(n, first, last, more=False):
                ring = rings[first, last]
                for g in range(G):
                    for d in range(ND):
                        for r, i in tiles(g, d, last):
                            maximum(ring, n, r, i)
                        if moves_max(g, d, last):
                            split_max(ring, n, g + 1)
                        if d == 0 and not (first and g == 0):
                            copy_o(n, g - 1)
                        for name, r in stages(g, d, first, last):
                            stage(ring, n, name, r)
                        if more and chosen:
                            if g == d == 0:
                                rows(n + 2)
                            if d >= ND - TOPK:
                                add_chosen(n + 2, TOPK * g + d - (ND - TOPK))

            round_(0, True, False, more=True)
            with dve.Fori(1, B - 2) as n:
                round_(n, False, False, more=True)
            round_(B - 2, False, False)
            round_(B - 1, False, True)
            copy_o(B, -1)
            stage(ring_end, B, "oT", -1)
            stage(ring_end, B, "y", 0)


def route(nc, sem, tag, x_res, ident, gate_w, gate_b, tab, xs_dram, run, row_all, w_all,
          wgu, wd, gu_dram, dn_dram, wsg_dram, wsd_dram, zrow):
    with ExitStack() as ctx:
        def sb(name, shape, dt=F32):
            return ctx.enter_context(nc.sbuf_tensor(f"{name}_{tag}", shape, dt))

        def ps(name, shape):
            return ctx.enter_context(nc.psum_tensor(f"{name}_{tag}", shape, F32))

        def s(name):
            return sem(f"{name}_{tag}")

        gw = sb("gw", [P, DC, E])
        gb = sb("gb", [P, E])
        base = sb("base", [P, E])
        before_f, ones_f = sb("before_f", [P, P]), sb("ones_f", [P, P])
        before, ones = sb("before", [P, P], BF16), sb("ones", [P, P], BF16)
        stats, mv = sb("rstats", [P, TB, 6]), sb("rmv", [P, TB, 2])
        ve, rstd, mhalf = sb("rve", [P, TB]), sb("rrstd", [P, TB]), sb("rmhalf", [P, TB])
        xn = [sb(f"rxn{i}", [P, TB, D]) for i in range(2)]
        xT = sb("rxT", [P, DC, L])
        th = sb("rth", [P, TB, E])
        score = sb("score", [P, TB, E])
        vals, valr = sb("vals", [P, TB, E + 2]), sb("valr", [P, TB, E + 2])
        top, topr = sb("top", [P, TB, 8]), sb("topr", [P, TB, 8])
        gval, gvalr = sb("gval", [P, TB, NGROUP + 4]), sb("gvalr", [P, TB, NGROUP + 4])
        gtop, gtopr = sb("gtop", [P, TB, 8]), sb("gtopr", [P, TB, 8])
        gmask = sb("gmask", [P, TB, NGROUP])
        mask, maskb = sb("rmask", [P, TB, E]), sb("rmaskb", [P, TB, E], BF16)
        wsel = sb("wsel", [P, TB, E])
        wsum = sb("wsum", [P, TB])
        slot = sb("slot", [P, TB, E])
        stop_, same = sb("stop", [P, TB, 8]), sb("same", [P, TOPK, E])
        w6 = sb("w6", [P, TB, TOPK])
        idx = [sb(f"idx{i}", [P, TB, TOPK], U32) for i in range(2)]

        wsg, wsd = sb("wsg", [P, DC, 2 * FS]), sb("wsd", [P, FS // P, D])
        sth, sa = sb("sth", [P, L]), sb("sa", [P, L])
        shT = sb("shT", [P, FS // P, L])
        bank_g, bank_u = ps("rg", [P, L]), ps("ru", [P, L])
        bank_y = ps("ry", [P, 2, D])
        bank_x = [ps(f"rx{i}", [P, 512]) for i in range(2)]
        bank_l = ps("rl", [P, TB, E])
        bank_r = ps("rr", [P, TB + 1, E])

        loaded, cast = s("rloaded"), s("rcast")
        w_in = s("rw_in")
        half_set = s("rhalf")
        step = s("rstep")
        var_ready = s("rvar")
        rstd_ready = s("rrstd_ready")
        xn_ready = s("rxn_ready")
        xT_mm = s("rxT_mm")
        xT_ready = s("rxT_ready")
        l_mm = s("rl_mm")
        th_ready = s("rth_ready")
        mask_ready = s("rmask_ready")
        rank_mm = s("rrank_mm")
        idx_ready = s("ridx_ready")
        sent = [s(f"rsent{i}") for i in range(2)]
        sg_mm = s("rsg_mm")
        sth_ready = s("rsth")
        sa_ready, sh_ready = s("rsa"), s("rsh")
        sy_mm = s("rsy_mm")
        added = s("radded")

        NSTEP = 29

        block = ctx.enter_context(nc.Block())

        @block.sync
        def _(sp):
            sp.dma_start(gw[:], gate_w.rearrange("(c p) e -> p c e", p=P)).then_inc(loaded, 16)
            sp.dma_start(gb[:], gate_b.unsqueeze(0).broadcast_to([P, E])).then_inc(loaded, 16)
            sp.dma_start(base[:], tab["base"]).then_inc(loaded, 16)
            sp.dma_start(before_f[:], tab["before"]).then_inc(loaded, 16)
            sp.dma_start(wsg[:], wsg_dram.rearrange("(c p) n -> p c n", p=P)).then_inc(loaded, 16)
            sp.dma_start(wsd[:], wsd_dram.rearrange("(c p) n -> p c n", p=P)).then_inc(loaded, 16)
            sp.dma_start(wgu[:], gu_dram.rearrange("e (c p) n -> p (e c) n", p=P)).then_inc(w_in, 16)
            sp.dma_start(wd[:], dn_dram.rearrange("e p n -> p e n")).then_inc(w_in, 16)
            sp.wait_ge(w_in, 32)

        @block.gpsimd
        def _(pool):
            nc.gpsimd.memset(mhalf[:], -0.5).then_inc(half_set, 1)
            pool.wait_ge(half_set, 1)

            def scatter(n, p, tiles):
                wait_alone(pool, idx_ready, n + 1)
                for i in tiles:
                    for k in range(TOPK):
                        nc.gpsimd.indirect_dma_start(
                            xs_dram, bass.IndirectOffsetOnAxis(ap=idx[p][:, i, k:k + 1], axis=0),
                            xn[p][:, i, :], None).then_inc(sent[p], 16)

            def roots(n):
                pool.wait_ge(var_ready, n + 1)
                nc.gpsimd.tensor_tensor(rstd[:], ve[:], mhalf[:], ALU.pow).then_inc(rstd_ready, 1)

            roots(0)
            with pool.Fori(0, B // 2 - 1) as j:
                for p in range(2):
                    scatter(2 * j + p, p, range(1))
                    roots(2 * j + p + 1)
                    scatter(2 * j + p, p, range(1, TB))
            scatter(B - 2, 0, range(1))
            roots(B - 1)
            scatter(B - 2, 0, range(1, TB))
            scatter(B - 1, 1, range(TB))
            for p in range(2):
                pool.wait_ge(sent[p], 16 * TB * TOPK * (B // 2))

        @block.tensor
        def _(pe):
            pe.wait_ge(loaded, 96)
            pe.wait_ge(cast, 1)

            def shared_up(n, c):
                wait(pe, sh_ready, 2 * n + c)
                for bank, at in ((bank_g, c * P), (bank_u, FS + c * P)):
                    for k in range(DC):
                        mm = nc.tensor.matmul(bank[:, :], wsg[:, k, at:at + P], xT[:, k, :],
                                              start=k == 0, stop=k == DC - 1)
                mm.then_inc(sg_mm, 1)

            def shared_down(n):
                pe.wait_ge(sh_ready, 2 * n + 2)
                for j in range(2):
                    wait(pe, added, 2 * n + j)
                    for i in range(2):
                        for c in range(FS // P):
                            mm = nc.tensor.matmul(bank_y[:, i, :], shT[:, c, (2 * j + i) * P:(2 * j + i + 1) * P],
                                                  wsd[:, c, :], start=c == 0, stop=c == FS // P - 1)
                    mm.then_inc(sy_mm, 1)

            def logits(n, p):
                pe.wait_ge(xn_ready, n + 1)
                for c in range(DC):
                    for i in range(TB):
                        mm = nc.tensor.transpose(bank_x[c][:, i * P:(i + 1) * P], xn[p][:, i, c * P:(c + 1) * P],
                                                 ident[:])
                    mm.then_inc(xT_mm, 1)
                pe.wait_ge(xT_ready, 2 * n + 2)
                for i in range(TB):
                    for c in range(DC):
                        mm = nc.tensor.matmul(bank_l[:, i, :], xT[:, c, i * P:(i + 1) * P], gw[:, c, :],
                                              start=c == 0, stop=c == DC - 1)
                mm.then_inc(l_mm, 1)

            def sequence(n, p, last=False):
                shared_up(n, 0)
                pe.wait_ge(mask_ready, n + 1)
                for i in range(TB + 1):
                    for k in range(min(i + 1, TB)):
                        mm = nc.tensor.matmul(bank_r[:, i, :], (before if k == i else ones)[:], maskb[:, k, :],
                                              start=k == 0, stop=k == min(i, TB - 1))
                mm.then_inc(rank_mm, 1)
                shared_up(n, 1)
                if not last:
                    logits(n + 1, (p + 1) % 2)
                shared_down(n)

            logits(0, 0)
            sequence(0, 0)
            sequence(1, 1)
            with pe.Fori(1, B // 2 - 1) as j:
                for p in range(2):
                    sequence(2 * j + p, p)
            sequence(B - 2, 0)
            sequence(B - 1, 1, last=True)

        @block.scalar
        def _(act):
            def front(n):
                for c in range(DC):
                    act.wait_ge(xT_mm, 2 * n + c + 1)
                    nc.scalar.copy(xT[:, c, :], bank_x[c][:, :]).then_inc(xT_ready, 1)
                act.wait_ge(l_mm, n + 1)
                nc.scalar.activation(th[:], bank_l[:], ACT.Tanh, scale=0.5).then_inc(th_ready, 1)

            def squash(n):
                for c in range(FS // P):
                    act.wait_ge(sg_mm, 2 * n + c + 1)
                    nc.scalar.activation(sth[:], bank_g[:, :], ACT.Tanh, scale=0.5).then_inc(sth_ready, 1)

            front(0)
            with act.Fori(0, B - 1) as n:
                squash(n)
                front(n + 1)
            squash(B - 1)

        @block.vector
        def _(dve):
            dve.wait_ge(loaded, 96)
            nc.vector.memset(ones_f[:], 1.0)
            nc.vector.memset(zrow[:], 0.0)
            for marks in (vals, gval, gtopr, topr):
                nc.vector.memset(marks[:], LOW)
            nc.vector.tensor_copy(run[:], base[:])
            nc.vector.tensor_copy(before[:], before_f[:])
            nc.vector.memset(ones[:], 1.0).then_inc(cast, 1)
            dve.wait_ge(cast, 1)

            def layernorm(n, p, used):
                def x(i):
                    return x_res[:, bass.ds(n * TB + i, 1), :].rearrange("p a d -> p (a d)")
                for i in range(TB):
                    st = nc.vector.bn_stats(stats[:, i, :], x(i))
                at = tick(n)
                at(st)
                for i in range(TB):
                    st = nc.vector.bn_aggr(mv[:, i, :], stats[:, i, :])
                at(st)
                nc.vector.tensor_scalar_add(ve[:], mv[:, :, 1], EPS).then_inc(var_ready, 1)
                dve.wait_ge(rstd_ready, n + 1)
                wait(dve, sent[p], 16 * TB * TOPK * used)
                for i in range(TB):
                    st = nc.vector.tensor_scalar(xn[p][:, i, :], x(i), mv[:, i, 0:1], rstd[:, i:i + 1],
                                                 ALU.subtract, ALU.mult)
                st.then_inc(xn_ready, 1)

            class tick:

                def __init__(self, n, k=0):
                    self.n, self.k = n, k

                def __call__(self, ins):
                    self.k += 1
                    ins.then_inc(step, 1)
                    wait_alone(dve, step, NSTEP * self.n + self.k)

            def choose(n, at):
                dve.wait_ge(th_ready, n + 1)
                at(nc.vector.tensor_scalar(score[:], th[:], 0.5, 0.5, ALU.mult, ALU.add))
                biased = vals[:, :, 0:E]
                at(nc.vector.tensor_tensor(biased, score[:], gb[:].unsqueeze(1).broadcast_to([P, TB, E]), ALU.add))
                groups = biased.rearrange("p t (g e) -> p t g e", g=NGROUP)
                at(nc.vector.tensor_reduce(gval[:, :, 0:NGROUP], groups, AX.X, ALU.max))
                for i in range(TB):
                    st = nc.vector.max(gtop[:, i, :], gval[:, i, :])
                at(st)
                at(nc.vector.tensor_copy(gtopr[:, :, 0:TOPG], gtop[:, :, 0:TOPG]))
                for i in range(TB):
                    st = nc.vector.match_replace(gvalr[:, i, :], gtopr[:, i, :], gval[:, i, :], HIGH)
                at(st)
                at(nc.vector.tensor_scalar(gmask[:], gvalr[:, :, 0:NGROUP], HIGH, None, ALU.is_ge))
                at(nc.vector.tensor_tensor(groups, groups, gmask[:].unsqueeze(3).broadcast_to([P, TB, NGROUP, EG]),
                                           ALU.mult))
                at(nc.vector.tensor_scalar_add(biased, biased, 0.0))
                for i in range(TB):
                    st = nc.vector.max(top[:, i, :], vals[:, i, :])
                at(st)
                at(nc.vector.tensor_copy(topr[:, :, 0:TOPK], top[:, :, 0:TOPK]))
                for i in range(TB):
                    st = nc.vector.match_replace(valr[:, i, :], topr[:, i, :], vals[:, i, :], HIGH)
                at(st)
                nc.vector.tensor_scalar(maskb[:], valr[:, :, 0:E], HIGH, None, ALU.is_ge).then_inc(mask_ready, 1)
                at(nc.vector.tensor_scalar(mask[:], valr[:, :, 0:E], HIGH, None, ALU.is_ge))

            def place(n, p, at, used):
                at(nc.vector.tensor_tensor(wsel[:], mask[:], score[:], ALU.mult))
                at(nc.vector.tensor_reduce(wsum[:], wsel[:], AX.X, ALU.add))
                at(nc.vector.tensor_scalar_add(wsum[:], wsum[:], 1e-20))
                at(nc.vector.reciprocal(wsum[:], wsum[:]))
                at(nc.vector.tensor_scalar_mul(wsum[:], wsum[:], ROUTE_SCALE))
                at(nc.vector.tensor_tensor(wsel[:], wsel[:], wsum[:].unsqueeze(2).broadcast_to([P, TB, E]), ALU.mult))
                dve.wait_ge(rank_mm, n + 1)
                at(nc.vector.tensor_tensor(slot[:], bank_r[:, 0:TB, :], run[:].unsqueeze(1).broadcast_to([P, TB, E]),
                                           ALU.add))
                nc.vector.tensor_tensor(run[:], bank_r[:, TB, :], run[:], ALU.add)
                at(nc.vector.tensor_tensor(slot[:], slot[:], mask[:], ALU.mult))
                for i in range(TB):
                    st = nc.vector.max(stop_[:, i, :], slot[:, i, :])
                at(st)
                wait(dve, sent[p], 16 * TB * TOPK * used)
                nc.vector.tensor_scalar_add(row_all[:, bass.ds(n * TB, TB), :], stop_[:, :, 0:TOPK], -1.0)
                nc.vector.tensor_scalar_add(idx[p][:], stop_[:, :, 0:TOPK], -1.0).then_inc(idx_ready, 1)
                for i in range(TB):
                    for k in range(TOPK):
                        st = nc.vector.scalar_tensor_tensor(out=same[:, k, :], in0=slot[:, i, :],
                                                            scalar=stop_[:, i, k:k + 1], in1=wsel[:, i, :],
                                                            op0=ALU.is_equal, op1=ALU.mult,
                                                            accum_out=w6[:, i, k:k + 1])
                    at(st)
                at(nc.vector.tensor_copy(w_all[:, bass.ds(n * TB, TB), :], w6[:]))
                assert at.k == NSTEP, at.k

            def shared_inner(n, c):
                dve.wait_ge(sth_ready, 2 * n + c + 1)
                nc.vector.scalar_tensor_tensor(out=sa[:], in0=sth[:], scalar=1.0, in1=bank_g[:, :],
                                               op0=ALU.add, op1=ALU.mult).then_inc(sa_ready, 1)
                dve.wait_ge(sa_ready, 2 * n + c + 1)
                nc.vector.scalar_tensor_tensor(out=shT[:, c, :], in0=sa[:], scalar=0.5, in1=bank_u[:, :],
                                               op0=ALU.mult, op1=ALU.mult).then_inc(sh_ready, 1)

            def shared_add(n):
                for j in range(2):
                    dve.wait_ge(sy_mm, 2 * n + j + 1)
                    x = x_res[:, bass.ds(n * TB + 2 * j, 2), :]
                    nc.vector.tensor_tensor(x, bank_y[:], x, ALU.add).then_inc(added, 1)

            def sequence(n, p, used, last=False):
                at = tick(n, 2)
                choose(n, at)
                shared_inner(n, 0)
                place(n, p, at, used)
                shared_inner(n, 1)
                if not last:
                    layernorm(n + 1, (p + 1) % 2, used + p)
                shared_add(n)

            layernorm(0, 0, 0)
            sequence(0, 0, 0)
            sequence(1, 1, 0)
            with dve.Fori(1, B // 2 - 1) as j:
                for p in range(2):
                    sequence(2 * j + p, p, j)
            sequence(B - 2, 0, B // 2 - 1)
            sequence(B - 1, 1, B // 2 - 1, last=True)


def to_registers(nc, engine, values):
    return nc.values_load_multi_w_load_instructions(
        values, engines=[engine], skip_runtime_bounds_check_because="VectorE keeps the tables in their ranges")[1]


def experts(nc, sem, tag, ident, wgu, wd, tab, run, row_all, idx_all, xs_dram, ys_dram, zrow):
    U = 8
    NB = 4
    J = NSLOT // U
    TQ = 4
    TP = NSLOT // TQ
    LAG = 8
    assert NSLOT == TQ * TP and U % NB == 0 and LAG == U
    with ExitStack() as ctx:
        def sb(name, shape, dt=F32):
            return ctx.enter_context(nc.sbuf_tensor(f"{name}_{tag}", shape, dt))

        def ps(name, shape):
            return ctx.enter_context(nc.psum_tensor(f"{name}_{tag}", shape, F32))

        def s(name):
            return sem(f"{name}_{tag}")

        sidx, ebase = sb("sidx", [P, TQ]), sb("ebase", [P, E])
        padf, padu = sb("padf", [P, E]), sb("padu", [P, E], U32)
        cnt_i, nt_i = sb("cnt_i", [P, E], I32), sb("nt_i", [P, E], I32)
        nt, ct, one = sb("nt", [P, E]), sb("ct", [P, E]), sb("one", [P, E])
        le, ln = sb("le", [P, TQ, E]), sb("len", [P, TQ, E])
        ex, st0 = sb("ex", [P, TQ]), sb("st0", [P, TQ])
        cols = sb("cols", [P, 2, TQ])
        rows = sb("rows", [1, 2, NSLOT], U32)
        shift, moved = sb("shift", [P, E]), [sb(f"moved{i}", [P, T * TOPK]) for i in range(2)]
        acc = [sb(f"acc{i}", [P, T * TOPK]) for i in range(2)]
        xt = [sb(f"ext{i}", [P, D]) for i in range(NB)]
        xT = [sb(f"exT{i}", [P, DC, P]) for i in range(2)]
        th = [sb(f"eth{i}", [P, FI]) for i in range(2)]
        a = [sb(f"ea{i}", [P, FI]) for i in range(2)]
        h = [sb(f"eh{i}", [P, FI]) for i in range(2)]
        hT = [sb(f"ehT{i}", [P, P]) for i in range(2)]
        y = [sb(f"ey{i}", [P, D]) for i in range(NB)]
        bx = [ps(f"ebx{i}", [P, DC, P]) for i in range(2)]
        bg = [ps(f"ebg{i}", [P, 2 * FI]) for i in range(2)]
        bh = [ps(f"ebh{i}", [P, P]) for i in range(2)]
        by = [ps(f"eby{i}", [P, D]) for i in range(2)]

        loaded, zeroed = s("eloaded"), s("ezeroed")
        step = s("estep")
        pad_ready = s("epad_ready")
        padded = s("epadded")
        shift_ready = s("eshift")
        move = s("emove")
        cols_ready = s("ecols")
        rows_mm, rows_ready = s("erows_mm"), s("erows")
        x_in = [s(f"ex_in{i}") for i in range(NB)]
        y_out = [s(f"ey_out{i}") for i in range(NB)]
        xT_mm, xT_ready = s("exT_mm"), s("exT_ready")
        g_mm = s("eg_mm")
        th_ready = s("eth_ready")
        a_ready = s("ea_ready")
        h_ready = s("eh_ready")
        hT_mm, hT_ready = s("ehT_mm"), s("ehT_ready")
        y_mm, y_ready = s("ey_mm"), s("ey_ready")

        block = ctx.enter_context(nc.Block())

        @block.sync
        def _(sp):
            sp.dma_start(sidx[:], tab["sidx"]).then_inc(loaded, 16)
            sp.dma_start(ebase[:], tab["base"]).then_inc(loaded, 16)
            sp.dma_start(xs_dram[E * CAP:E * CAP + P, :], zrow[:]).then_inc(padded, 16)
            sp.wait_ge(pad_ready, 1)
            with sp.Fori(0, E // U) as j:
                for row in to_registers(nc, mybir.EngineType.SP, padu[0:1, bass.ds(j * U, U)]):
                    sp.dma_start(xs_dram[bass.ds(row, P), :], zrow[:]).then_inc(padded, 16)
            sp.wait_ge(padded, 16 * (E + 1))
            sp.wait_ge(rows_ready, 1)

            def load(s_, q, row):
                wait_alone(sp, xT_mm, s_ - NB + 1)
                sp.dma_start(xt[q % NB][:], xs_dram[bass.ds(row, P), :]).then_inc(x_in[q % NB], 16)

            def store(s_, q):
                wait_alone(sp, y_ready, s_ + 1)
                sp.dma_start(ys_dram[bass.ds(s_ * P, P), :], y[q % NB][:]).then_inc(y_out[q % NB], 16)

            def steps(j, first):
                row = to_registers(nc, mybir.EngineType.SP, rows[0:1, 1, bass.ds(j * U, U)])
                for q in range(U):
                    load(U * j + q, q, row[q])
                    if not first:
                        store(U * j + q - LAG, q)

            steps(0, True)
            with sp.Fori(1, J) as j:
                steps(j, False)
            for s_ in range(NSLOT - LAG, NSLOT):
                store(s_, s_)
            for b in range(NB):
                sp.wait_ge(y_out[b], 16 * (NSLOT // NB))

        @block.gpsimd
        def _(pool):
            pool.wait_ge(shift_ready, 1)
            rows_f = row_all[:].rearrange("p t k -> p (t k)")
            for e in range(1, E):
                nc.gpsimd.tensor_scalar(moved[e % 2][:], rows_f, float(e * CAP), shift[:, e - 1:e],
                                        ALU.is_ge, ALU.mult).then_inc(move, 1)
                pool.wait_ge(move, 2 * e - 1)
                nc.gpsimd.tensor_tensor(acc[e % 2][:], moved[e % 2][:], rows_f if e == 1 else acc[(e - 1) % 2][:],
                                        ALU.add).then_inc(move, 1)
                pool.wait_ge(move, 2 * e)
            nc.gpsimd.tensor_copy(idx_all[:].rearrange("p t k -> p (t k)"), acc[(E - 1) % 2][:]).then_inc(move, 1)
            pool.wait_ge(move, 2 * E - 1)

        @block.tensor
        def _(pe):
            pe.wait_ge(cols_ready, 1)
            for w in range(2):
                for q in range(TQ):
                    mm = nc.tensor.transpose(by[w][0:1, q * TP:(q + 1) * TP], cols[0:TP, w, q:q + 1], ident[0:TP, 0:TP])
            mm.then_inc(rows_mm, 1)
            pe.wait_ge(rows_ready, 1)

            def up_t(s_, q, j):
                pe.wait_ge(x_in[q % NB], 16 * (U // NB * j + q // NB + 1))
                wait(pe, xT_ready, s_ - 1)
                for c in range(DC):
                    mm = nc.tensor.transpose(bx[q % 2][:, c, :], xt[q % NB][:, c * P:(c + 1) * P], ident[:])
                mm.then_inc(xT_mm, 1)

            def up(s_, q, e):
                pe.wait_ge(xT_ready, s_ + 1)
                wait(pe, h_ready, s_ - 1)
                for c in range(DC):
                    mm = nc.tensor.matmul(bg[q % 2][:, :], xT[q % 2][:, c, :],
                                          wgu[:, bass.ds(e * DC + c, 1), :].rearrange("p a n -> p (a n)"),
                                          start=c == 0, stop=c == DC - 1)
                mm.then_inc(g_mm, 1)

            def down_t(s_, q):
                pe.wait_ge(h_ready, s_ + 1)
                wait(pe, hT_ready, s_ - 1)
                nc.tensor.transpose(bh[q % 2][:, :], h[q % 2][:], ident[:]).then_inc(hT_mm, 1)

            def down(s_, q, e):
                pe.wait_ge(hT_ready, s_ + 1)
                wait(pe, y_ready, s_ - 1)
                nc.tensor.matmul(by[q % 2][:, :], hT[q % 2][:],
                                 wd[:, bass.ds(e, 1), :].rearrange("p a n -> p (a n)"),
                                 start=True, stop=True).then_inc(y_mm, 1)

            def steps(j, first, last):
                back = 0 if first else 2
                es = to_registers(nc, mybir.EngineType.PE, rows[0:1, 0, bass.ds(j * U - back, U + back)])
                for q in range(U + 2 * last):
                    s_ = U * j + q
                    if q < U:
                        up(s_, q, es[q + back])
                    if not (first and q < 1) and q < U + 1:
                        down_t(s_ - 1, q - 1)
                    if not (first and q < 2):
                        down(s_ - 2, q - 2, es[q - 2 + back])
                    if not last or q < U - 2:
                        up_t(s_ + 2, q + 2, j)

            up_t(0, 0, 0)
            up_t(1, 1, 0)
            steps(0, True, False)
            with pe.Fori(1, J - 1) as j:
                steps(j, False, False)
            steps(J - 1, False, True)

        @block.scalar
        def _(act):
            act.wait_ge(rows_mm, 1)
            for w in range(2):
                cp = nc.scalar.copy(rows[0:1, w, :].rearrange("p (j q) -> p j q", q=TQ),
                                    by[w][0:1, 0:NSLOT].rearrange("p (q j) -> p j q", q=TQ))
            cp.then_inc(rows_ready, 1)

            def tokens(s_, q):
                act.wait_ge(xT_mm, s_ + 1)
                nc.scalar.copy(xT[q % 2][:], bx[q % 2][:]).then_inc(xT_ready, 1)

            def squash(s_, q):
                act.wait_ge(g_mm, s_ + 1)
                nc.scalar.activation(th[q % 2][:], bg[q % 2][:, 0:FI], ACT.Tanh, scale=0.5).then_inc(th_ready, 1)

            def output(s_, q, j):
                act.wait_ge(y_mm, s_ + 1)
                wait(act, y_out[q % NB], 16 * (U // NB * j + q // NB))
                nc.scalar.copy(y[q % NB][:], by[q % 2][:]).then_inc(y_ready, 1)

            def steps(j, first, last):
                for q in range(U + 2 * last):
                    s_ = U * j + q
                    if q < U:
                        squash(s_, q)
                    if not (first and q < 2):
                        output(s_ - 2, q - 2, j)
                    if not last or q < U - 2:
                        tokens(s_ + 2, q + 2)

            tokens(0, 0)
            tokens(1, 1)
            steps(0, True, False)
            steps(1, False, False)
            with act.Fori(2, J - 1) as j:
                steps(j, False, False)
            steps(J - 1, False, True)

        @block.vector
        def _(dve):
            k = [0]

            def done(ins):
                k[0] += 1
                ins.then_inc(step, 1)
                dve.wait_ge(step, k[0])

            dve.wait_ge(loaded, 32)
            done(nc.vector.tensor_scalar_add(padf[:], run[:], -1.0))
            nc.vector.tensor_copy(padu[:], padf[:]).then_inc(pad_ready, 1)
            nc.vector.memset(one[:], 1.0)
            done(nc.vector.tensor_tensor(nt[:], run[:], ebase[:], ALU.subtract))
            done(nc.vector.tensor_scalar_add(cnt_i[:], nt[:], float(P - 1)))
            done(nc.vector.tensor_single_scalar(nt_i[:], cnt_i[:], P.bit_length() - 1, ALU.arith_shift_right))
            done(nc.vector.tensor_copy(nt[:], nt_i[:]))
            done(nc.vector.tensor_tensor_scan(ct[:], one[:], nt[:], 0.0, ALU.mult, ALU.add))
            done(nc.vector.tensor_tensor(le[:], ct[:].unsqueeze(1).broadcast_to([P, TQ, E]),
                                         sidx[:].unsqueeze(2).broadcast_to([P, TQ, E]), ALU.is_le))
            done(nc.vector.tensor_tensor(ln[:], le[:], nt[:].unsqueeze(1).broadcast_to([P, TQ, E]), ALU.mult))
            nc.vector.tensor_reduce(ex[:], le[:], AX.X, ALU.add)
            done(nc.vector.tensor_reduce(st0[:], ln[:], AX.X, ALU.add))
            done(nc.vector.tensor_tensor(st0[:], sidx[:], st0[:], ALU.subtract))
            done(nc.vector.tensor_scalar_mul(st0[:], st0[:], float(P)))
            done(nc.vector.scalar_tensor_tensor(out=st0[:], in0=ex[:], scalar=float(CAP), in1=st0[:],
                                                op0=ALU.mult, op1=ALU.add))
            nc.vector.tensor_scalar_min(cols[:, 1, :], st0[:], float(E * CAP))
            nc.vector.tensor_scalar_min(cols[:, 0, :], ex[:], float(E - 1)).then_inc(cols_ready, 1)
            nc.vector.tensor_scalar(shift[:], nt[:], float(P), float(-CAP), ALU.mult, ALU.add).then_inc(shift_ready, 1)
            dve.wait_ge(rows_ready, 1)

            def inner(s_, q):
                dve.wait_ge(th_ready, s_ + 1)
                nc.vector.scalar_tensor_tensor(out=a[q % 2][:], in0=th[q % 2][:], scalar=1.0, in1=bg[q % 2][:, 0:FI],
                                               op0=ALU.add, op1=ALU.mult).then_inc(a_ready, 1)
                dve.wait_ge(a_ready, s_ + 1)
                nc.vector.scalar_tensor_tensor(out=h[q % 2][:], in0=a[q % 2][:], scalar=0.5,
                                               in1=bg[q % 2][:, FI:2 * FI], op0=ALU.mult,
                                               op1=ALU.mult).then_inc(h_ready, 1)

            def turned(s_, q):
                dve.wait_ge(hT_mm, s_ + 1)
                nc.vector.tensor_copy(hT[q % 2][:], bh[q % 2][:]).then_inc(hT_ready, 1)

            def steps(j, first):
                for q in range(U):
                    s_ = U * j + q
                    if not (first and q < 1):
                        turned(s_ - 1, q - 1)
                    inner(s_, q)

            steps(0, True)
            with dve.Fori(1, J) as j:
                steps(j, False)
            turned(NSLOT - 1, NSLOT - 1)


def combine(nc, sem, tag, x_res, ys_dram, idx_all, w_all, out_dram):
    NB = 2
    with ExitStack() as ctx:
        def sb(name, shape, dt=F32):
            return ctx.enter_context(nc.sbuf_tensor(f"{name}_{tag}", shape, dt))

        def s(name):
            return sem(f"{name}_{tag}")

        yg = [sb(f"cyg{i}", [P, TOPK, D]) for i in range(NB)]
        idx = [sb(f"cidx{i}", [P, TOPK], U32) for i in range(NB)]

        idx_ready = s("cidx_ready")
        got = [s(f"cgot{i}") for i in range(NB)]
        added = s("cadded")
        stored = s("cstored")

        block = ctx.enter_context(nc.Block())

        @block.sync
        def _(sp):
            with sp.Fori(0, T) as t:
                wait_alone(sp, added, TOPK * t + TOPK)
                sp.dma_start(out_dram[bass.ds(t * P, P), :],
                             x_res[:, bass.ds(t, 1), :].rearrange("p a d -> p (a d)")).then_inc(stored, 16)
            sp.wait_ge(stored, 16 * T)

        @block.gpsimd
        def _(pool):
            with pool.Fori(0, T // NB) as j:
                for p in range(NB):
                    wait_alone(pool, idx_ready, NB * j + p + 1)
                    for k in range(TOPK):
                        nc.gpsimd.indirect_dma_start(yg[p][:, k, :], None, ys_dram,
                                                     bass.IndirectOffsetOnAxis(ap=idx[p][:, k:k + 1], axis=0)
                                                     ).then_inc(got[p], 16)

        @block.vector
        def _(dve):
            def rows(t, p, j):
                nc.vector.tensor_copy(idx[p][:], idx_all[:, bass.ds(t, 1), :].rearrange("p a k -> p (a k)")
                                      ).then_inc(idx_ready, 1)

            def tile(t, p, j):
                x = x_res[:, bass.ds(t, 1), :].rearrange("p a d -> p (a d)")
                dve.wait_ge(got[p], 16 * TOPK * (j + 1))
                for k in range(TOPK):
                    wait(dve, added, TOPK * t + k)
                    nc.vector.scalar_tensor_tensor(out=x, in0=yg[p][:, k, :],
                                                   scalar=w_all[:, bass.ds(t, 1), k:k + 1].rearrange("p a k -> p (a k)"),
                                                   in1=x, op0=ALU.mult, op1=ALU.add).then_inc(added, 1)
                dve.wait_ge(added, TOPK * (t + 1))

            for p in range(NB):
                rows(p, p, 0)
            for p in range(NB):
                tile(p, p, 0)
                rows(p + NB, p, 1)
            with dve.Fori(1, T // NB - 1) as j:
                for p in range(NB):
                    tile(NB * j + p, p, j)
                    rows(NB * j + p + NB, p, j + 1)
            for p in range(NB):
                tile(T - NB + p, p, T // NB - 1)


def setup(nc, sem, x_dram, x_res, ident, identb, maskb, tab, wkT_dram, wvT_dram, wdown_dram, wup_dram, kv_dram,
          row_tables):
    DL = wdown_dram.shape[1]
    with ExitStack() as ctx:
        def sb(name, shape, dt=F32):
            return ctx.enter_context(nc.sbuf_tensor(f"{name}_0", shape, dt))

        def ps(name, shape):
            return ctx.enter_context(nc.psum_tensor(f"{name}_0", shape, F32))

        maskf = sb("maskf", [P, 2, P])
        wkT, wvT, wkvT = (sb(n, [P, DC, D]) for n in ("wkT", "wvT", "wkvT"))
        wdown, wup = sb("wdown", [P, DC, DL]), sb("wup", [DL, 2, D])
        foldT = sb("foldT", [DL, D])
        kv = sb("kv", [P, 2, DC, D])
        bank_f, bank_kv = ps("bank_f", [DL, D]), [ps(f"bank_kv{i}", [P, DC, D]) for i in range(2)]
        x_in, c_in, w_in = sem("x_in"), sem("c_in"), sem("w_in")
        summed = sem("summed")
        cast = sem("cast")
        f_mm, f_ready = sem("f_mm"), sem("f_ready")
        kv_mm, kv_ready = sem("kv_mm"), sem("kv_ready")
        kv_out = sem("kv_out")
        rows_out = sem("rows_out")

        block = ctx.enter_context(nc.Block())

        @block.sync
        def _(sp):
            sp.dma_start(x_res[:], x_dram.rearrange("b (t p) d -> p (b t) d", p=P)).then_inc(x_in, 16)
            sp.dma_start(ident[:], tab["ident"]).then_inc(c_in, 16)
            sp.dma_start(maskf[:], tab["mask"]).then_inc(c_in, 16)
            sp.dma_start(wkT[:], wkT_dram.rearrange("(c p) n -> p c n", p=P)).then_inc(w_in, 16)
            sp.dma_start(wvT[:], wvT_dram.rearrange("(c p) n -> p c n", p=P)).then_inc(w_in, 16)
            sp.dma_start(wdown[:], wdown_dram.rearrange("(c p) n -> p c n", p=P)).then_inc(w_in, 16)
            for i in range(2):
                sp.dma_start(wup[:, i, :], wup_dram[i]).then_inc(w_in, 16)
            for name, rows in row_tables.items():
                sp.dma_start(rows, tab[name]).then_inc(rows_out, 16)
            sp.wait_ge(kv_ready, 2)
            for i in range(2):
                sp.dma_start(kv_dram[i].rearrange("(c p) n -> p c n", p=P), kv[:, i, :, :]).then_inc(kv_out, 16)
            sp.wait_ge(kv_out, 32)
            sp.wait_ge(x_in, 16)
            sp.wait_ge(rows_out, 16 * len(row_tables))

        @block.vector
        def _(dve):
            dve.wait_ge(c_in, 32)
            nc.vector.tensor_copy(identb[:], ident[:])
            nc.vector.tensor_copy(maskb[:], maskf[:]).then_inc(cast, 1)
            dve.wait_ge(w_in, 80)
            nc.vector.tensor_tensor(wkvT[:], wkT[:], wvT[:], ALU.add).then_inc(summed, 1)
            dve.wait_ge(cast, 1)

        @block.tensor
        def _(pe):
            pe.wait_ge(summed, 1)
            for c in range(DC):
                mm = nc.tensor.matmul(bank_f[:, :], wdown[:, c, :], wkvT[:, c, :], start=c == 0, stop=c == DC - 1)
            mm.then_inc(f_mm, 1)
            pe.wait_ge(f_ready, 1)
            for i in range(2):
                for c in range(DC):
                    mm = nc.tensor.matmul(bank_kv[i][:, c, :], foldT[:, c * P:(c + 1) * P], wup[:, i, :],
                                          start=True, stop=True)
                mm.then_inc(kv_mm, 1)

        @block.scalar
        def _(act):
            act.wait_ge(f_mm, 1)
            nc.scalar.copy(foldT[:], bank_f[:, :]).then_inc(f_ready, 1)
            for i in range(2):
                act.wait_ge(kv_mm, i + 1)
                nc.scalar.copy(kv[:, i, :, :], bank_kv[i][:]).then_inc(kv_ready, 1)


@contextmanager
def phase(nc):
    sems = []

    def sem(name):
        sems.append(nc.alloc_semaphore(name=name))
        return sems[-1]

    yield sem
    nc.clear_and_free_semaphores(sems)
    nc.all_engine_barrier()


def hybrid_kernel(nc, ins, out):
    with ExitStack() as ctx:
        def sb(name, shape, dt=F32):
            return ctx.enter_context(nc.sbuf_tensor(name, shape, dt))

        def dram(name, shape):
            return nc.dram_tensor(name, shape, F32, kind="Internal").ap()

        x_res = sb("x_res", [P, T, D])
        ident = sb("ident", [P, P])
        identb = sb("identb", [P, P], BF16)
        maskb = sb("maskb", [P, 2, P], BF16)
        qk_dram = [dram(f"qk{i}", [H, 3, HD, L]) for i in range(3)]
        m_dram = dram("m", [HG * TB, 2, P])
        kv_dram = [dram(f"kv{i}", [D, D]) for i in range(2)]
        row_tables = {n: dram(n, ins[n].shape) for n in ("qrow_a", "krow_a", "qrow_b", "krow_b", "alibi")}
        xs_dram = dram("xs", [XROWS, D])
        ys_dram = dram("ys", [YROWS, D])

        with phase(nc) as sem:
            setup(nc, sem, ins["x"], x_res, ident, identb, maskb, ins, ins["wkT"], ins["wvT"], ins["wdown"],
                  [ins["wupk"], ins["wupv"]], kv_dram, row_tables)

        def ffn(tag, idx_all, w_all):
            with ExitStack() as own:
                def own_sb(name, shape, dt=F32):
                    return own.enter_context(nc.sbuf_tensor(f"{name}_{tag}", shape, dt))

                zrow, run, row_all = own_sb("zrow", [P, D]), own_sb("run", [P, E]), own_sb("row_all", [P, T, TOPK])
                wgu, wd = own_sb("wgu", [P, E * DC, 2 * FI]), own_sb("wd", [P, E, D])
                with phase(nc) as sem:
                    route(nc, sem, tag, x_res, ident, ins["gate"], ins["bias"], ins, xs_dram, run, row_all,
                          w_all, wgu, wd, ins["gu"], ins["dn"], ins["wsg"], ins["wsd"], zrow)
                with phase(nc) as sem:
                    experts(nc, sem, tag, ident, wgu, wd, ins, run, row_all, idx_all, xs_dram, ys_dram, zrow)

        tables = {**ins, **row_tables}
        with phase(nc) as sem:
            attention(nc, sem, False, x_res, ident, identb, maskb, [ins[n] for n in ("a_wq", "a_wk", "a_wv", "a_wo")],
                      tables, [qk_dram[0], qk_dram[2]], m_dram)
        with nc.sbuf_tensor("idx_all", [P, T, TOPK], U32) as idx_all, nc.sbuf_tensor("w_all", [P, T, TOPK], F32) as w_all:
            ffn("1", idx_all, w_all)
            with phase(nc) as sem:
                attention(nc, sem, True, x_res, ident, identb, maskb,
                          [ins["b_wq"], kv_dram[0], kv_dram[1], ins["b_wo"]],
                          tables, qk_dram, m_dram, (ys_dram, idx_all, w_all))
            ffn("2", idx_all, w_all)
            with phase(nc) as sem:
                combine(nc, sem, "2", x_res, ys_dram, idx_all, w_all, out.rearrange("b l d -> (b l) d"))


def split12(a):
    high = (a.astype(np.float32).view(np.uint32) & np.uint32(0xFFFFF000)).view(np.float32)
    return high, (a - high).astype(np.float32)


def constants():
    j, p = np.arange(L), np.arange(P)
    mid = L / 2
    slope = (2.0 ** (-8.0 / H)) ** (np.arange(H) + 1)
    t = {"ident": np.eye(P), "alibi": np.stack(split12(slope[:, None] * (j[None, :] - mid)))}
    for name, rows in (("qrow_a", 34), ("krow_a", 34), ("qrow_b", 40), ("krow_b", 40)):
        t[name] = np.zeros((rows, L))
    t["qrow_a"][0:2] = 1.0
    t["krow_a"][32:34] = 1.0
    for f, sign in ((0, -1.0), (1, 1.0)):
        high, low = split12(np.exp(sign * LDECAY * (j - mid)))
        t["krow_b"][32 + 4 * f:36 + 4 * f] = [high, low, low, high]
    t["cwin"] = np.zeros((P, L))
    t["cwin"][:, L - P:] = np.where(p[None, :] <= p[:, None], 0.0, NEG)
    t["efac"] = np.broadcast_to(np.stack([np.exp(-LDECAY * (j - mid)), np.exp(LDECAY * (j - mid))]) / 16.0, (P, 2, L))
    t["dwin"] = np.exp(-LDECAY * np.abs(p[:, None] - (np.arange(7 * P) - 3 * P)[None, :]))
    at = p[:, None] + P * np.arange(TB)[None, :] - mid
    t["sfac"] = np.stack([np.exp(LDECAY * at), np.exp(-LDECAY * at)], 1)
    t["mfac"] = np.exp(LDECAY * at)
    t["mask"] = np.stack([np.where(p[None, :] >= p[:, None], 0.0, NEG), np.where(p[None, :] < p[:, None], 0.0, NEG)], 1)
    t["base"] = np.broadcast_to(np.arange(E) * CAP + 1.0, (P, E))
    t["before"] = p[:, None] < p[None, :]
    t["sidx"] = 4.0 * p[:, None] + np.arange(4)[None, :]
    return {k: np.ascontiguousarray(a, np.float32) for k, a in t.items()}


def kernel(**inputs):
    import concourse.bacc as bacc
    from concourse.bass_utils import run_bass_kernel_spmd

    def turned(a, *axes):
        return np.ascontiguousarray(np.transpose(a, axes))

    i = {k: np.asarray(a) for k, a in inputs.items()}
    arrays = {
        "x": i["L0_attn_a_x"],
        "a_wq": i["L0_attn_a_q_w"], "a_wk": i["L0_attn_a_k_w"], "a_wv": i["L0_attn_a_v_w"], "a_wo": i["L0_attn_a_o_w"],
        "b_wq": i["L0_attn_b_W_q"], "b_wo": i["L0_attn_b_W_o"],
        "wkT": turned(i["L0_attn_b_W_k"], 1, 0), "wvT": turned(i["L0_attn_b_W_v"], 1, 0),
        "wdown": i["L0_attn_b_W_down_kv"], "wupk": i["L0_attn_b_W_up_k"], "wupv": i["L0_attn_b_W_up_v"],
        "gate": turned(i["L0_ffn_gate_weight"], 1, 0), "bias": i["L0_ffn_e_score_correction_bias"],
        "gu": turned(i["L0_ffn_experts_gate_up"], 0, 2, 1), "dn": turned(i["L0_ffn_experts_down"], 0, 2, 1),
        "wsg": np.concatenate([turned(i["L0_ffn_shared_gate_w"], 1, 0), turned(i["L0_ffn_shared_up_w"], 1, 0)], 1),
        "wsd": turned(i["L0_ffn_shared_down_w"], 1, 0),
        **constants(),
    }
    nc = bacc.Bacc("TRN2", target_bir_lowering=False, num_devices=1)
    ins = {k: nc.dram_tensor(f"in_{k}", a.shape, mybir.dt.from_np(a.dtype), kind="ExternalInput").ap()
           for k, a in arrays.items()}
    out = nc.dram_tensor("out", (B, L, D), F32, kind="ExternalOutput").ap()
    hybrid_kernel(nc, ins, out)
    r = run_bass_kernel_spmd(nc, [{f"in_{k}": np.ascontiguousarray(a) for k, a in arrays.items()}], core_ids=[0])
    return r.results[0]["out"]
```

```python
from contextlib import ExitStack, contextmanager

import numpy as np

import concourse.bass as bass
from concourse import mybir

F32 = mybir.dt.float32
F32R = mybir.dt.float32r
BF16 = mybir.dt.bfloat16
I32 = mybir.dt.int32
U32 = mybir.dt.uint32
ALU = mybir.AluOpType
ACT = mybir.ActivationFunctionType
AX = mybir.AxisListType

P = 128
B, L, D = 8, 512, 256
T = B * L // P
TB = L // P
DC = D // P
H, HD = 16, 16
G, HG = 4, 4
E, FI = 32, 128
FS = 2 * FI
TOPK, NGROUP, TOPG = 6, 8, 4
EG = E // NGROUP
ROUTE_SCALE = 2.5
LDECAY = 0.01
EPS = 1e-5
NEG = -1e30
LOW, HIGH = -3e38, 3e38
CAP = T * P + P
NSLOT = T * TOPK + E
XROWS = E * CAP + P
YROWS = NSLOT * P


def wait(eng, sem, value):
    if isinstance(value, int) and value <= 0:
        return
    eng.wait_ge(sem, value)


def wait_alone(eng, sem, value):
    if isinstance(value, int) and value <= 0:
        return
    eng.wait_ge(sem, value)
    eng.nop(nofuse=True)


class Ring:

    def __init__(self, banks, plan):
        self.banks, self.plan = banks, plan
        self.at, self.held = 0, [None] * len(banks)

    def __getitem__(self, key):
        return self.banks[self.plan.index(key) % len(self.banks)]

    def take(self, pe, key, freed):
        assert self.plan[self.at] == key, (self.plan[self.at], key)
        i = self.at % len(self.banks)
        if self.held[i] is not None:
            pe.wait_ge(*self.held[i])
        self.held[i] = freed
        self.at += 1
        return self.banks[i]


def attention(nc, sem, decayed, x_res, ident, identb, maskb, w_dram, tab, qk_dram, m_dram,
              chosen=None, begin=None):
    tag = "b" if decayed else "a"
    forms = 2 if decayed else 1
    qscale = 1.0 / 16.0 if decayed else 1.0 / 4.0
    NQK = 2 * (forms + 1)
    NHL = 3 if decayed else 4
    UNITS = 2 * TB * forms
    ROWS = 104 if decayed else 98
    NP1 = H * TB
    NP2 = G * UNITS
    duos = [(kb, f) for kb in range(TB) for f in range(forms)]
    ND = len(duos)
    NMI = 2 * forms * forms

    parts = ([(f, half) for half in range(2) for f in range(forms)] + [(forms, half) for half in range(2)])
    stores = [3 if f == forms else 2 for f, _ in parts]

    def stored(buf, n, j):
        every = sum(c for i, c in enumerate(stores) if i % NHL == buf)
        return every * n + sum(c for i, c in enumerate(stores[:j]) if i % NHL == buf)

    def span(kb, f):
        return (kb * P, L) if f == 0 else (0, (kb + 1) * P)

    QUARTER = ND // 4

    def stages(g, d, first, last):
        if d % QUARTER:
            return []
        before, now, after = {
            (0, 0): ([], [], [("ln", 0)]),
            (0, 1): ([("oT", -1)], [], [("scale", 0)]),
            (0, 2): ([], [], [("xT", 0)]),
            (0, 3): ([], [], [("q", 0)] if decayed else [("q", 0), ("q", 1)]),
            (1, 0): ([("onT", 0)], [], [("q", 1)] if decayed else [("k", 0), ("k", 1)]),
            (1, 1): ([], [("oT", 0)], [("k", 0), ("k", 1)] if decayed else []),
            (1, 2): ([("y", 0)], [], []),
            (1, 3): ([], [], [("v", 0)]),
            (2, 1): ([], [("oT", 1)], []),
            (3, 1): ([], [("oT", 2)], []),
        }.get((g, d // QUARTER), ([], [], []))
        return before * (not first) + now + after * (not last)

    def tiles(g, d, last):
        each = HG * TB // ND
        return [(g + 2, i) for i in range(d * each, d * each + each) if not (last and g + 2 >= G)]

    def moves_max(g, d, last):
        return d == 0 and not (last and g == G - 1)

    def banks_of(stage, r):
        if stage in ("ln", "scale"):
            return []
        return [(stage, r)] if stage in ("oT", "q", "k") else [(stage, i) for i in range(2)]

    def plan_round(first, last):
        plan = []
        for g in range(G):
            for d in range(ND):
                plan += [("p1", r, i) for r, i in tiles(g, d, last)]
                if moves_max(g, d, last):
                    plan.append(("mT", g + 1))
                for stage, r in stages(g, d, first, last):
                    plan += banks_of(stage, r)
        return plan

    start = [("xT", 0), ("q", 0), ("q", 1), ("k", 0), ("k", 1), ("v", 0)]
    plan_start = ([k for stage, r in start for k in banks_of(stage, r)]
                  + [("p1", 4, i) for i in range(HG * TB)] + [("mT", 4)] + [("p1", 5, i) for i in range(HG * TB)])
    plan_end = [("oT", -1), ("onT", 0), ("onT", 1), ("y", 0), ("y", 1)]

    with ExitStack() as ctx:
        def sb(name, shape, dt=F32):
            return ctx.enter_context(nc.sbuf_tensor(f"{name}_{tag}", shape, dt))

        def ps(name, shape):
            return ctx.enter_context(nc.psum_tensor(f"{name}_{tag}", shape, F32))

        def s(name):
            return sem(f"{name}_{tag}")

        wq, wk, wv, wo = (sb(n, [P, DC, D]) for n in ("wq", "wk", "wv", "wo"))
        qst = [[sb(f"qst{f}_{g}", [ROWS, HG, L], F32R) for g in range(G)] for f in range(forms)]
        kst = [sb(f"kst{g}", [ROWS, HG, L], F32R) for g in range(G)]
        xn_onT = sb("xn_onT", [P, TB * D])
        xn = xn_onT[:].rearrange("p (t d) -> p t d", t=TB)
        onT = xn_onT[:].rearrange("p (c l) -> p c l", c=DC)
        xT = sb("xT", [P, DC, L])
        hi = [sb(f"hi{i}", [P, L], F32R) for i in range(NHL)]
        lo = [sb(f"lo{i}", [P, L], F32R) for i in range(NHL)]
        zero = sb("zero", [P, 1])
        v_all = sb("v_all", [P, TB, D])
        v = sb("v", [P, TB, H * (HD + 1) + 32 - (HD + 1)])
        pt = [[sb(f"pt{i}{j}", [P, 2, L]) for j in range(2)] for i in range(2)]
        oT = sb("oT", [P, L])
        on = sb("on", [P, TB, D])
        mcol = [sb(f"mcol{i}", [P, HG, TB]) for i in range(2)]
        mhl = sb("mhl", [HG * TB, 2, P], F32R)
        rec = sb("rec", [P, TB, HG])
        stats = sb("stats", [P, TB, 6])
        mv = sb("mv", [P, TB, 2])
        ve = sb("ve", [P, TB])
        rstd = sb("rstd", [P, TB])
        mhalf = sb("mhalf", [P, TB])
        if decayed:
            qf = [sb(f"qf{i}", [P, L]) for i in range(2)]
            efac = sb("efac", [P, 2, L])
            dwin = sb("dwin", [P, 7 * P])
            sfac = sb("sfac", [P, 2, TB])
            mfac = sb("mfac", [P, TB])
            mpost = [sb("mpost", [P, HG, TB])] * 2
        else:
            cwin = sb("cwin", [P, L])
            mpost = mcol

        rbank = [ps(f"r{i}", [P, 512]) for i in range(3)]
        sbank = [ps(f"s{i}", [P, 2, 512]) for i in range(2)]
        obank = ps("o", [P, 512])
        ring_start, ring_end = Ring(rbank, plan_start), Ring(rbank, plan_end)
        rings = {(first, last): Ring(rbank, plan_round(first, last))
                 for first, last in ((True, False), (False, False), (False, True))}

        loaded = s("loaded")
        fill_set = s("fill_set")
        q_filled = s("q_filled")
        k_filled = s("k_filled")
        tabs = s("tabs")
        half_set = s("half_set")
        v_set = s("v_set")
        ln = s("ln")
        var_ready = s("var_ready")
        rstd_ready = s("rstd_ready")
        xn_ready = s("xn_ready")
        xT_mm = s("xT_mm")
        xT_a, xT_v = s("xT_a"), s("xT_v")
        qk_mm = s("qk_mm")
        qf_ready = s("qf_ready")
        hi_ready = s("hi_ready")
        lo_ready = s("lo_ready")
        hl_out = [s(f"hl_out{i}") for i in range(NHL)]
        st_ready = [s(f"st_ready{g}") for g in range(G)]
        v_mm = s("v_mm")
        v_out = s("v_out")
        v_ready = s("v_ready")
        p1_mm = s("p1_mm")
        p1_max = s("p1_max")
        m_ready = s("m_ready")
        mT_mm = s("mT_mm")
        mh_ready = s("mh_ready")
        ml_ready = s("ml_ready")
        m_out = s("m_out")
        m_in = s("m_in")
        s_mm = s("s_mm")
        p_ready = s("p_ready")
        pv_done = s("pv_done")
        o_ready = s("o_ready")
        oT_mm = s("oT_mm")
        rec_ready = s("rec_ready")
        on_ready = s("on_ready")
        onT_mm = s("onT_mm")
        onT_ready = s("onT_ready")
        y_mm = s("y_mm")
        x_added = s("x_added")
        maxed = m_ready if decayed else p1_max
        if chosen:
            ys_dram, idx_all, w_all = chosen
            NY = 4
            yg = [sb(f"yg{i}", [P, D]) for i in range(NY)]
            idx = sb("cidx", [P, TB, TOPK], U32)
            idx_ready = s("cidx_ready")
            got = [s(f"cgot{i}") for i in range(NY)]
            y_added = s("cadded")
        NADD = TB * TOPK
        if begin:
            DL = begin["wdown"].shape[1]
            maskf = sb("maskf", [P, 2, P])
            wkT, wvT, wkvT = (sb(n, [P, DC, D]) for n in ("wkT", "wvT", "wkvT"))
            wdown, wup = sb("wdown", [P, DC, DL]), sb("wup", [DL, 2, D])
            foldT = sb("foldT", [DL, D])
            kv = sb("kv", [P, 2, DC, D])
            x_in = [s(f"x_in{i}") for i in range(2)]
            c_in = s("c_in")
            cast = s("cast")
            w_in = s("w_in")
            summed = s("summed")
            f_mm, f_ready = s("f_mm"), s("f_ready")
            kv_mm, kv_ready = s("kv_mm"), s("kv_ready")
            kv_out = s("kv_out")
            rows_out = s("rows_out")

        def maxed_at(n, g):
            return G * n + g + 1 if decayed else NP1 * n + HG * TB * (g + 1)

        tables = [(efac, "efac"), (dwin, "dwin"), (sfac, "sfac"), (mfac, "mfac")] if decayed else [(cwin, "cwin")]
        LOADED = 16 * (4 + len(tables))
        TABS = 16 * G * (1 if decayed else 3)

        block = ctx.enter_context(nc.Block())

        @block.sync
        def _(sp):
            if begin:
                xs = begin["x"].rearrange("b (t p) d -> p (b t) d", p=P)
                sp.dma_start(x_res[:, 0:TB, :], xs[:, 0:TB, :]).then_inc(x_in[0], 16)
                sp.dma_start(ident[:], begin["ident"]).then_inc(c_in, 16)
                sp.dma_start(maskf[:], begin["mask"]).then_inc(c_in, 16)
                for name in tab["scratch"]:
                    sp.dma_start(tab[name], begin[name]).then_inc(rows_out, 16)
            for t_, d_ in zip((wq, wk, wv, wo), w_dram):
                sp.dma_start(t_[:], d_.rearrange("(c p) n -> p c n", p=P)).then_inc(loaded, 16)
            for t_, name in tables:
                sp.dma_start(t_[:], tab[name]).then_inc(loaded, 16)
            if begin:
                sp.dma_start(x_res[:, TB:, :], xs[:, TB:, :]).then_inc(x_in[1], 16)
                for t_, name in ((wkT, "wkT"), (wvT, "wvT"), (wdown, "wdown")):
                    sp.dma_start(t_[:], begin[name].rearrange("(c p) n -> p c n", p=P)).then_inc(w_in, 16)
                for i, name in enumerate(("wupk", "wupv")):
                    sp.dma_start(wup[:, i, :], begin[name]).then_inc(w_in, 16)
            for g in range(G):
                if decayed:
                    sp.dma_start(kst[g][96:ROWS, :, :].bitcast(F32),
                                 tab["krow"].unsqueeze(1).broadcast_to([ROWS - 96, HG, L])).then_inc(tabs, 16)
                else:
                    if g == 0:
                        sp.wait_ge(q_filled, G)
                        sp.wait_ge(k_filled, 1)
                        sp.wait_ge(rows_out, 16 * len(tab["scratch"]))
                    sp.dma_start(kst[g][64:66, :, :].bitcast(F32),
                                 tab["alibi"][:, HG * g:HG * g + HG, :]).then_inc(tabs, 16)
                    for stack, row in ((qst[0][g], 64), (kst[g], 96)):
                        sp.dma_start(stack[row:row + 2, :, :].bitcast(F32),
                                     tab["ones"].unsqueeze(1).broadcast_to([2, HG, L])).then_inc(tabs, 16)

            def store_halves(n, j0, j1):
                if j0 == 0:
                    for g in range(G):
                        wait_alone(sp, st_ready[g], 32 * (forms + 1) * n)
                for j in range(j0, j1):
                    f, half = parts[j]
                    sp.wait_ge(lo_ready, NQK * n + j + 1)
                    for r, part in enumerate((hi, lo, hi)[:stores[j]]):
                        sp.dma_start(qk_dram[f][8 * half:8 * half + 8, r, :, :],
                                     part[j % NHL][:].bitcast(F32)).then_inc(hl_out[j % NHL], 16)

            def load_stack(n, r):
                g, n_ = r % G, n + r // G
                if g == 0:
                    for i in range(NHL):
                        wait_alone(sp, hl_out[i], 16 * stored(i, n_ + 1, 0))
                heads = slice(HG * g, HG * g + HG)
                wait_alone(sp, pv_done, ND * (G * n + r - G + 1))
                for d in range(2):
                    for f in range(forms):
                        sp.dma_start(qst[f][g][32 * d:32 * d + 32, :, :].bitcast(F32),
                                     qk_dram[f][heads, 0:2].rearrange("h r d t -> (r d) h t")
                                     ).then_inc(st_ready[g], 16)
                    sp.dma_start(kst[g][32 * d:32 * d + 32, :, :].bitcast(F32),
                                 qk_dram[forms][heads, d:d + 2].rearrange("h r d t -> (r d) h t")
                                 ).then_inc(st_ready[g], 16)

            def load_max(n, r):
                k, g = G * n + r, r % G
                wait_alone(sp, ml_ready, k + 1)
                wait(sp, m_in, 16 * NMI * k)
                sp.dma_start(m_dram, mhl[:].bitcast(F32)).then_inc(m_out, 16)
                sp.wait_ge(m_out, 16 * (k + 1))
                for f in range(forms):
                    for d in range(forms):
                        for r in range(2):
                            row = 96 + 4 * f + 2 * d + r
                            sp.dma_start(qst[f][g][row:row + 1, :, :].bitcast(F32),
                                         m_dram.rearrange("(h q) r t -> r h q t", q=TB)[r:r + 1]
                                         ).then_inc(m_in, 16)

            store_halves(0, 0, NQK)
            for g in range(G):
                load_stack(0, g)
            load_max(0, 0)

            def round_(n, first, last):
                load_max(n, 1)
                if not first:
                    load_stack(n, 3)
                if not last:
                    store_halves(n + 1, 0, 2 * forms)
                load_max(n, 2)
                if not last:
                    store_halves(n + 1, 2 * forms, NQK)
                    load_stack(n, 4)
                load_max(n, 3)
                if not last:
                    load_stack(n, 5)
                    load_max(n, 4)
                    load_stack(n, 6)

            round_(0, True, False)
            with sp.Fori(1, B - 1) as n:
                round_(n, False, False)
            round_(B - 1, False, True)
            sp.wait_ge(m_in, 16 * NMI * G * B)
            if begin:
                sp.wait_ge(kv_ready, 2)
                for i in range(2):
                    sp.dma_start(tab["kv"][i].rearrange("(c p) n -> p c n", p=P), kv[:, i, :, :]).then_inc(kv_out, 16)
                sp.wait_ge(kv_out, 32)

        @block.gpsimd
        def _(pool):
            nc.gpsimd.memset(mhalf[:], -0.5).then_inc(half_set, 1)
            nc.gpsimd.memset(v[:], 1.0).then_inc(v_set, 1)
            pool.wait_ge(v_set, 1)
            pool.wait_ge(half_set, 1)

            def roots(n):
                pool.wait_ge(var_ready, n + 1)
                nc.gpsimd.tensor_tensor(rstd[:], ve[:], mhalf[:], ALU.pow).then_inc(rstd_ready, 1)

            def place_v(n, g):
                wait_alone(pool, v_out, 2 * n + 2)
                wait_alone(pool, pv_done, ND * (G * (n - 1) + g + 1))
                v_heads = v[:, :, 0:H * (HD + 1)].rearrange("p t (h x) -> p t h x", h=H)
                nc.gpsimd.tensor_copy(v_heads[:, :, HG * g:HG * g + HG, 0:HD],
                                      v_all[:, :, HG * HD * g:HG * HD * (g + 1)].rearrange("p t (h d) -> p t h d", h=HG)
                                      ).then_inc(v_ready, 1)

            def gather(q, i):
                for m in range(TOPK * i, TOPK * (i + 1)):
                    if m == 0:
                        wait_alone(pool, idx_ready, q + 1)
                    wait_alone(pool, y_added, NADD * q + m - NY + 1)
                    nc.gpsimd.indirect_dma_start(yg[m % NY][:], None, ys_dram,
                                                 bass.IndirectOffsetOnAxis(ap=idx[:, i, m % TOPK:m % TOPK + 1], axis=0)
                                                 ).then_inc(got[m % NY], 16)

            if chosen:
                for i in range(TB):
                    gather(0, i)
            roots(0)
            if chosen:
                for i in range(TB):
                    gather(1, i)
            for g in range(G - 1):
                place_v(0, g)

            def round_(n, more):
                roots(n + 1)
                for g in range(G):
                    if more and chosen:
                        gather(n + 2, g)
                    if g == 0:
                        place_v(n, G - 1)
                    else:
                        place_v(n + 1, g - 1)

            round_(0, True)
            with pool.Fori(1, B - 2) as n:
                round_(n, True)
            round_(B - 2, False)
            place_v(B - 1, G - 1)

        @block.tensor
        def _(pe):
            def transpose_x(ring, n):
                pe.wait_ge(xn_ready, n + 1)
                for c in range(DC):
                    bank = ring.take(pe, ("xT", c), ((xT_a, xT_v)[c], n + 1))
                    for i in range(TB):
                        mm = nc.tensor.transpose(bank[:, i * P:(i + 1) * P], xn[:, i, c * P:(c + 1) * P], ident[:])
                    mm.then_inc(xT_mm, 1)

            def project(ring, n, name, half):
                pe.wait_ge(xT_a, n + 1)
                pe.wait_ge(xT_v, n + 1)
                w = wq if name == "q" else wk
                if name == "k":
                    freed = (lo_ready, NQK * n + 2 * forms + half + 1)
                elif decayed:
                    freed = (qf_ready, 2 * forms * n + forms * (half + 1))
                else:
                    freed = (lo_ready, NQK * n + half + 1)
                bank = ring.take(pe, (name, half), freed)
                for c in range(DC):
                    mm = nc.tensor.matmul(bank[:, :], w[:, c, half * P:(half + 1) * P], xT[:, c, :],
                                          start=c == 0, stop=c == DC - 1)
                mm.then_inc(qk_mm, 1)

            def project_v(ring, n):
                for j in range(2):
                    bank = ring.take(pe, ("v", j), (v_out, 2 * n + j + 1))
                    for i in range(2):
                        for c in range(DC):
                            mm = nc.tensor.matmul(bank[:, i * D:(i + 1) * D],
                                                  xT[:, c, (2 * j + i) * P:(2 * j + i + 1) * P], wv[:, c, :],
                                                  start=c == 0, stop=c == DC - 1)
                    mm.then_inc(v_mm, 1)

            def pass1(ring, n, r, i):
                g, h, qb = r % G, i // TB, i % TB
                if i == 0:
                    pe.wait_ge(st_ready[g], 32 * (forms + 1) * (n + r // G + 1))
                bank = ring.take(pe, ("p1", r, i), (p1_max, HG * TB * (G * n + r) + i + 1))
                cols = L if decayed else (qb + 1) * P
                nc.tensor.matmul(bank[:, 0:cols], qst[0][g][0:96, h, qb * P:(qb + 1) * P],
                                 kst[g][0:96, h, 0:cols], start=True, stop=True).then_inc(p1_mm, 1)

            def transpose_max(ring, n, r):
                pe.wait_ge(maxed, maxed_at(n, r))
                bank = ring.take(pe, ("mT", r), (ml_ready, G * n + r + 1))
                nc.tensor.transpose(bank[0:HG * TB, 0:P], mpost[r % 2][:].rearrange("p h q -> p (h q)"),
                                    ident[:]).then_inc(mT_mm, 1)

            def scores(n, g, d):
                kb, f = duos[d]
                q0, q1 = span(kb, f)
                if d == 0:
                    pe.wait_ge(m_in, 16 * NMI * (G * n + g + 1))
                for pair in range(2):
                    pe.wait_ge(p_ready, NP2 * n + UNITS * g + 2 * d + pair + 1)
                    for hh in range(2):
                        h = 2 * pair + hh
                        nc.tensor.matmul(sbank[pair][:, hh, q0:q1], kst[g][:, h, kb * P:(kb + 1) * P],
                                         qst[f][g][:, h, q0:q1], start=True, stop=False)
                    for hh in range(2):
                        mm = nc.tensor.matmul(sbank[pair][:, hh, kb * P:(kb + 1) * P], identb[:],
                                              maskb[:, f, :], start=False, stop=True)
                    mm.then_inc(s_mm, 1)

            def weigh(n, r, d):
                kb, f = duos[d]
                q0, q1 = span(kb, f)
                k = G * n + r
                if d == 0:
                    pe.wait_ge(o_ready, k + 1)
                    pe.wait_ge(v_ready, k + 1 + (r % G < G - 1))
                pe.wait_ge(p_ready, UNITS * k + 2 * d + 2 + 2)
                for h in range(HG):
                    at = (HG * (r % G) + h) * (HD + 1)
                    mm = nc.tensor.matmul(obank[32 * h:32 * h + 32, q0:q1], v[:, kb, at:at + 32],
                                          pt[d % 2][h // 2][:, h % 2, q0:q1],
                                          start=d == 0, stop=d == ND - 1)
                mm.then_inc(pv_done, 1)

            def untranspose(ring, n, r):
                k = G * n + r
                pe.wait_ge(o_ready, k + 2)
                bank = ring.take(pe, ("oT", r), (on_ready, k + 1))
                for qb in range(TB):
                    mm = nc.tensor.transpose(bank[:, qb * P:(qb + 1) * P], oT[:, qb * P:(qb + 1) * P], ident[:])
                mm.then_inc(oT_mm, 1)

            def transpose_o(ring, n):
                pe.wait_ge(on_ready, G * (n + 1))
                for c in range(DC):
                    bank = ring.take(pe, ("onT", c), (onT_ready, 2 * n + c + 1))
                    for i in range(TB):
                        mm = nc.tensor.transpose(bank[:, i * P:(i + 1) * P], on[:, i, c * P:(c + 1) * P], ident[:])
                    mm.then_inc(onT_mm, 1)

            def project_o(ring, n):
                pe.wait_ge(onT_ready, 2 * n + 2)
                for j in range(2):
                    bank = ring.take(pe, ("y", j), (x_added, 2 * n + j + 2))
                    for i in range(2):
                        for c in range(DC):
                            mm = nc.tensor.matmul(bank[:, i * D:(i + 1) * D],
                                                  onT[:, c, (2 * j + i) * P:(2 * j + i + 1) * P], wo[:, c, :],
                                                  start=c == 0, stop=c == DC - 1)
                    mm.then_inc(y_mm, 1)

            def stage(ring, n, name, r):
                if name == "xT":
                    transpose_x(ring, n + 1)
                elif name in ("q", "k"):
                    project(ring, n + 1, name, r)
                elif name == "v":
                    project_v(ring, n + 1)
                elif name == "oT":
                    untranspose(ring, n, r)
                elif name == "onT":
                    transpose_o(ring, n - 1)
                elif name == "y":
                    project_o(ring, n - 1)

            if begin:
                pe.wait_ge(c_in, 32)
                pe.wait_ge(cast, 1)
            pe.wait_ge(loaded, LOADED)
            for name, r in start:
                stage(ring_start, -1, name, r)
            if begin:
                pe.wait_ge(summed, 1)
                for c in range(DC):
                    mm = nc.tensor.matmul(obank[0:DL, 0:D], wdown[:, c, :], wkvT[:, c, :],
                                          start=c == 0, stop=c == DC - 1)
                mm.then_inc(f_mm, 1)
                pe.wait_ge(f_ready, 1)
                for i in range(2):
                    for c in range(DC):
                        mm = nc.tensor.matmul(sbank[i][:, 0, c * D:(c + 1) * D], foldT[:, c * P:(c + 1) * P],
                                              wup[:, i, :], start=True, stop=True)
                    mm.then_inc(kv_mm, 1)
            pe.wait_ge(q_filled, G * forms)
            pe.wait_ge(k_filled, 1)
            pe.wait_ge(tabs, TABS)
            for i in range(HG * TB):
                pass1(ring_start, -1, 4, i)
            transpose_max(ring_start, -1, 4)
            for i in range(HG * TB):
                pass1(ring_start, -1, 5, i)

            def round_(n, first, last):
                ring = rings[first, last]
                for g in range(G):
                    for d in range(ND):
                        scores(n, g, d)
                        if g == d == 0:
                            pe.wait_ge(p1_max, NP1 * n + HG * TB * 2)
                            pe.wait_ge(on_ready, G * n - 1) if not first else pe.wait_ge(ml_ready, 1)
                        for r, i in tiles(g, d, last):
                            pass1(ring, n, r, i)
                        if moves_max(g, d, last):
                            transpose_max(ring, n, g + 1)
                        for name, r in stages(g, d, first, last):
                            stage(ring, n, name, r)
                        if d:
                            weigh(n, g, d - 1)
                        elif not (first and g == 0):
                            weigh(n, g - 1, ND - 1)

            if begin:
                pe.wait_ge(kv_ready, 2)
            round_(0, True, False)
            with pe.Fori(1, B - 1) as n:
                round_(n, False, False)
            round_(B - 1, False, True)
            weigh(B, -1, ND - 1)
            pe.wait_ge(p1_max, NP1 * B)
            pe.wait_ge(on_ready, G * B - 1)
            stage(ring_end, B, "oT", -1)
            stage(ring_end, B, "onT", 0)
            stage(ring_end, B, "y", 0)

        @block.scalar
        def _(act):
            nc.scalar.nop().then_inc(p_ready, 2)
            act.wait_ge(fill_set, 1)

            for g in range(G):
                for f in range(forms):
                    nc.scalar.copy(qst[f][g][64:ROWS, :, :].rearrange("p h t -> p (h t)"),
                                   zero[64:ROWS, :].broadcast_to([ROWS - 64, HG * L])).then_inc(q_filled, 1)
            act.wait_ge(v_set, 1)

            def copy_x(ring, n):
                act.wait_ge(xT_mm, 2 * n + 1)
                nc.scalar.copy(xT[:, 0, :], ring["xT", 0][:, :]).then_inc(xT_a, 1)

            def high_halves(ring, n, name, r):
                for j, (f, half) in enumerate(parts):
                    if (f == forms) != (name == "k") or half != r:
                        continue
                    if j >= NHL:
                        act.wait_ge(hl_out[j % NHL], 16 * stored(j % NHL, n, j))
                    else:
                        wait(act, hl_out[j % NHL], 16 * stored(j % NHL, n, 0))
                    if decayed and f < forms:
                        act.wait_ge(qf_ready, 2 * forms * n + j + 1)
                        nc.scalar.copy(hi[j % NHL][:], qf[j % 2][:]).then_inc(hi_ready, 1)
                    else:
                        act.wait_ge(qk_mm, 4 * n + (2 if f == forms else 0) + half + 1)
                        nc.scalar.activation(hi[j % NHL][:], ring[name, half][:, :],
                                             ACT.Copy, scale=1.0 if f == forms else qscale).then_inc(hi_ready, 1)

            def copy_v(ring, n):
                for j in range(2):
                    act.wait_ge(v_mm, 2 * n + j + 1)
                    wait(act, v_ready, G * n)
                    nc.scalar.copy(v_all[:, 2 * j:2 * j + 2, :].rearrange("p t d -> p (t d)"),
                                   ring["v", j][:, :]).then_inc(v_out, 1)

            def split_max(ring, n, r):
                k = G * n + r
                act.wait_ge(mT_mm, k + 1)
                wait(act, m_out, 16 * k)
                nc.scalar.mul(mhl[:, 0, :], ring["mT", r][0:HG * TB, 0:P], -1.0).then_inc(mh_ready, 1)

            def exps(n, g, d):
                kb, f = duos[d]
                q0, q1 = span(kb, f)
                for pair in range(2):
                    act.wait_ge(s_mm, NP2 * n + UNITS * g + 2 * d + pair + 1)
                    nc.scalar.activation(pt[d % 2][pair][:, :, q0:q1], sbank[pair][:, :, q0:q1], ACT.Exp,
                                         scale=sfac[:, f, kb:kb + 1] if decayed else 1.0).then_inc(p_ready, 1)

            def copy_o(ring, n):
                for c in range(DC):
                    act.wait_ge(onT_mm, 2 * n + c + 1)
                    nc.scalar.copy(onT[:, c, :], ring["onT", c][:, :]).then_inc(onT_ready, 1)

            def stage(ring, n, name, r):
                if name == "xT":
                    copy_x(ring, n + 1)
                elif name in ("q", "k"):
                    high_halves(ring, n + 1, name, r)
                elif name == "v":
                    copy_v(ring, n + 1)
                elif name == "onT":
                    copy_o(ring, n - 1)

            for name, r in start:
                stage(ring_start, -1, name, r)
            if begin:
                act.wait_ge(f_mm, 1)
                nc.scalar.copy(foldT[:], obank[0:DL, 0:D]).then_inc(f_ready, 1)
                for i in range(2):
                    act.wait_ge(kv_mm, i + 1)
                    nc.scalar.copy(kv[:, i, :, :].rearrange("p c n -> p (c n)"),
                                   sbank[i][:, 0, :]).then_inc(kv_ready, 1)
            split_max(ring_start, -1, 4)
            if decayed:
                act.wait_ge(loaded, LOADED)

            def round_(n, first, last):
                ring = rings[first, last]
                for g in range(G):
                    for d in range(ND):
                        exps(n, g, d)
                        if moves_max(g, d, last):
                            split_max(ring, n, g + 1)
                        for name, r in stages(g, d, first, last):
                            stage(ring, n, name, r)

            round_(0, True, False)
            with act.Fori(1, B - 1) as n:
                round_(n, False, False)
            round_(B - 1, False, True)
            stage(ring_end, B, "onT", 0)

        @block.vector
        def _(dve):
            def rows(q):
                nc.vector.tensor_copy(idx[:], idx_all[:, bass.ds(q * TB, TB), :]).then_inc(idx_ready, 1)

            def x_tile(t):
                return x_res[:, bass.ds(t, 1), :].rearrange("p a d -> p (a d)")

            def add_chosen(q, m):
                i, k = m // TOPK, m % TOPK
                dve.wait_ge(got[m % NY], 16 * (NADD // NY * q + m // NY + 1))
                wait(dve, y_added, NADD * q + m)
                x = x_tile(q * TB + i)
                weight = w_all[:, bass.ds(q * TB + i, 1), k:k + 1].rearrange("p a k -> p (a k)")
                nc.vector.scalar_tensor_tensor(out=x, in0=yg[m % NY][:], scalar=weight, in1=x,
                                               op0=ALU.mult, op1=ALU.add).then_inc(y_added, 1)

            def variances(n):
                if chosen:
                    dve.wait_ge(y_added, NADD * (n + 1))
                for i in range(TB):
                    st = nc.vector.bn_stats(stats[:, i, :], x_tile(n * TB + i))
                st.then_inc(ln, 1)
                wait_alone(dve, ln, 2 * n + 1)
                for i in range(TB):
                    st = nc.vector.bn_aggr(mv[:, i, :], stats[:, i, :])
                st.then_inc(ln, 1)
                dve.wait_ge(ln, 2 * n + 2)
                nc.vector.tensor_scalar_add(ve[:], mv[:, :, 1], EPS).then_inc(var_ready, 1)

            def scale(n):
                dve.wait_ge(rstd_ready, n + 1)
                for i in range(TB):
                    st = nc.vector.tensor_scalar(xn[:, i, :], x_tile(n * TB + i),
                                                 mv[:, i, 0:1], rstd[:, i:i + 1], ALU.subtract, ALU.mult)
                st.then_inc(xn_ready, 1)

            def copy_x(ring, n):
                dve.wait_ge(xT_mm, 2 * n + 2)
                nc.vector.tensor_copy(xT[:, 1, :], ring["xT", 1][:, :]).then_inc(xT_v, 1)

            def low(ring, n, j):
                f, half = parts[j]
                dve.wait_ge(hi_ready, NQK * n + j + 1)
                high = hi[j % NHL][:].bitcast(F32)
                if decayed and f < forms:
                    nc.vector.tensor_tensor(lo[j % NHL][:], qf[j % 2][:], high, ALU.subtract).then_inc(lo_ready, 1)
                else:
                    nc.vector.scalar_tensor_tensor(out=lo[j % NHL][:], in0=ring["k" if f == forms else "q", half][:, :],
                                                   scalar=1.0 if f == forms else qscale, in1=high,
                                                   op0=ALU.mult, op1=ALU.subtract).then_inc(lo_ready, 1)

            def low_halves(ring, n, name, half):
                if name == "k":
                    low(ring, n, 2 * forms + half)
                elif not decayed:
                    low(ring, n, half)
                else:
                    wait(dve, lo_ready, NQK * n + forms * half)
                    dve.wait_ge(qk_mm, 4 * n + half + 1)
                    for j in range(forms * half, forms * half + forms):
                        nc.vector.tensor_tensor(qf[j % 2][:], ring["q", half][:, :], efac[:, parts[j][0], :],
                                                ALU.mult).then_inc(qf_ready, 1)
                    for j in range(forms * half, forms * half + forms):
                        low(ring, n, j)

            def maximum(ring, n, r, i):
                wait_alone(dve, p1_mm, HG * TB * (G * n + r) + i + 1)
                h, qb = i // TB, i % TB
                bank = ring["p1", r, i]
                cols = L if decayed else (qb + 1) * P
                other = dwin[:, (TB - 1 - qb) * P:(TB - 1 - qb) * P + L] if decayed else cwin[:, L - cols:L]
                nc.vector.tensor_tensor_reduce(out=bank[:, 0:cols], in0=bank[:, 0:cols], in1=other, scale=1.0,
                                               scalar=LOW, op0=ALU.mult if decayed else ALU.add, op1=ALU.max,
                                               accum_out=mcol[r % 2][:, h, qb:qb + 1]).then_inc(p1_max, 1)
                if decayed and i == HG * TB - 1:
                    dve.wait_ge(p1_max, HG * TB * (G * n + r + 1))
                    nc.vector.tensor_tensor(mpost[0][:], mcol[r % 2][:], mfac[:].unsqueeze(1).broadcast_to([P, HG, TB]),
                                            ALU.mult).then_inc(m_ready, 1)

            def split_max(ring, n, r):
                dve.wait_ge(mh_ready, G * n + r + 1)
                nc.vector.scalar_tensor_tensor(out=mhl[:, 1, :], in0=ring["mT", r][0:HG * TB, 0:P], scalar=-1.0,
                                               in1=mhl[:, 0, :].bitcast(F32), op0=ALU.mult,
                                               op1=ALU.subtract).then_inc(ml_ready, 1)

            def copy_o(n, r):
                dve.wait_ge(pv_done, ND * (G * n + r + 1))
                nc.vector.tensor_copy(oT[:], obank[:, :]).then_inc(o_ready, 1)

            def normalise(ring, n, r):
                k = G * n + r
                dve.wait_ge(oT_mm, k + 1)
                o4 = ring["oT", r][:, :].rearrange("p (q h x) -> p q h x", q=TB, h=HG)
                nc.vector.reciprocal(rec[:], o4[:, :, :, HD]).then_inc(rec_ready, 1)
                dve.wait_ge(rec_ready, k + 1)
                heads = slice(HG * HD * (r % G), HG * HD * (r % G + 1))
                nc.vector.tensor_tensor(on[:, :, heads].rearrange("p q (h d) -> p q h d", h=HG),
                                        o4[:, :, :, 0:HD], rec[:].unsqueeze(3).broadcast_to([P, TB, HG, HD]),
                                        ALU.mult).then_inc(on_ready, 1)

            def add(ring, n):
                for j in range(2):
                    dve.wait_ge(y_mm, 2 * n + j + 1)
                    xr = x_res[:, bass.ds(n * TB + 2 * j, 2), :].rearrange("p a d -> p (a d)")
                    nc.vector.tensor_tensor(xr, ring["y", j][:, :], xr, ALU.add).then_inc(x_added, 1)

            def stage(ring, n, name, r):
                if name == "ln":
                    variances(n + 1)
                elif name == "scale":
                    scale(n + 1)
                elif name == "xT":
                    copy_x(ring, n + 1)
                elif name in ("q", "k"):
                    low_halves(ring, n + 1, name, r)
                elif name == "oT":
                    normalise(ring, n, r)
                elif name == "y":
                    add(ring, n - 1)

            if chosen:
                rows(0)
            nc.vector.memset(zero[:], 0.0).then_inc(fill_set, 1)
            for g in range(G):
                ms = nc.vector.memset(kst[g][64:96, :, :].bitcast(F32), 0.0)
            ms.then_inc(k_filled, 1)
            if begin:
                dve.wait_ge(c_in, 32)
                nc.vector.tensor_copy(identb[:], ident[:])
                nc.vector.tensor_copy(maskb[:], maskf[:]).then_inc(cast, 1)
                dve.wait_ge(x_in[0], 16)
            nc.vector.nop().then_inc(o_ready, 1)
            nc.vector.nop().then_inc(x_added, 1)

            if chosen:
                for m in range(NADD):
                    add_chosen(0, m)
                rows(1)
            stage(ring_start, -1, "ln", 0)
            stage(ring_start, -1, "scale", 0)
            dve.wait_ge(loaded, LOADED)
            for name, r in start:
                stage(ring_start, -1, name, r)
            if begin:
                dve.wait_ge(w_in, 80)
                nc.vector.tensor_tensor(wkvT[:], wkT[:], wvT[:], ALU.add).then_inc(summed, 1)
                dve.wait_ge(x_in[1], 16)
            for i in range(HG * TB):
                maximum(ring_start, -1, 4, i)
            split_max(ring_start, -1, 4)
            if chosen:
                for m in range(NADD):
                    add_chosen(1, m)
            for i in range(HG * TB):
                maximum(ring_start, -1, 5, i)

            def round_(n, first, last, more=False):
                ring = rings[first, last]
                for g in range(G):
                    for d in range(ND):
                        for r, i in tiles(g, d, last):
                            maximum(ring, n, r, i)
                        if moves_max(g, d, last):
                            split_max(ring, n, g + 1)
                        if d == 0 and not (first and g == 0):
                            copy_o(n, g - 1)
                        for name, r in stages(g, d, first, last):
                            stage(ring, n, name, r)
                        if more and chosen:
                            if g == d == 0:
                                rows(n + 2)
                            if d >= ND - TOPK:
                                add_chosen(n + 2, TOPK * g + d - (ND - TOPK))

            round_(0, True, False, more=True)
            with dve.Fori(1, B - 2) as n:
                round_(n, False, False, more=True)
            round_(B - 2, False, False)
            round_(B - 1, False, True)
            copy_o(B, -1)
            stage(ring_end, B, "oT", -1)
            stage(ring_end, B, "y", 0)


def to_registers(nc, engine, values):
    return nc.values_load_multi_w_load_instructions(
        values, engines=[engine], skip_runtime_bounds_check_because="VectorE keeps the tables in their ranges")[1]


TQ = 4
TP = NSLOT // TQ
WE = DC * 2 * FI + D


def route(nc, sem, tag, x_res, ident, gate_w, gate_b, tab, xs_dram, run, row_all, w_all,
          w_exp, gu_dram, dn_dram, wsg_dram, wsd_dram, zrow, rows, shift):
    with ExitStack() as ctx:
        def sb(name, shape, dt=F32):
            return ctx.enter_context(nc.sbuf_tensor(f"{name}_{tag}", shape, dt))

        def ps(name, shape):
            return ctx.enter_context(nc.psum_tensor(f"{name}_{tag}", shape, F32))

        def s(name):
            return sem(f"{name}_{tag}")

        gw = sb("gw", [P, DC, E])
        gb = sb("gb", [P, E])
        base = sb("base", [P, E])
        before_f, ones_f = sb("before_f", [P, P]), sb("ones_f", [P, P])
        before, ones = sb("before", [P, P], BF16), sb("ones", [P, P], BF16)
        stats, mv = sb("rstats", [P, TB, 6]), sb("rmv", [P, TB, 2])
        ve, rstd, mhalf = sb("rve", [P, TB]), sb("rrstd", [P, TB]), sb("rmhalf", [P, TB])
        xn = [sb(f"rxn{i}", [P, TB, D]) for i in range(2)]
        xT = sb("rxT", [P, DC, L])
        th = sb("rth", [P, TB, E])
        score = sb("score", [P, TB, E])
        vals, valr = sb("vals", [P, TB, E + 2]), sb("valr", [P, TB, E + 2])
        top, topr = sb("top", [P, TB, 8]), sb("topr", [P, TB, 8])
        gval, gvalr = sb("gval", [P, TB, NGROUP + 4]), sb("gvalr", [P, TB, NGROUP + 4])
        gtop, gtopr = sb("gtop", [P, TB, 8]), sb("gtopr", [P, TB, 8])
        gmask = sb("gmask", [P, TB, NGROUP])
        mask, maskb = sb("rmask", [P, TB, E]), sb("rmaskb", [P, TB, E], BF16)
        wsel = sb("wsel", [P, TB, E])
        wsum = sb("wsum", [P, TB])
        slot = sb("slot", [P, TB, E])
        slot6, same = sb("slot6", [P, TB, 8]), sb("same", [P, TOPK, E])
        w6 = sb("w6", [P, TB, TOPK])
        idx = [sb(f"idx{i}", [P, TB, TOPK], U32) for i in range(2)]

        sidx = sb("sidx", [P, TQ])
        padf, padu = sb("padf", [P, E]), sb("padu", [P, E], U32)
        cnt_i, nt_i = sb("cnt_i", [P, E], I32), sb("nt_i", [P, E], I32)
        nt, ct, one = sb("nt", [P, E]), sb("ct", [P, E]), sb("one", [P, E])
        le, lt = sb("le", [P, TQ, E]), sb("len", [P, TQ, E])
        ex, st0 = sb("ex", [P, TQ]), sb("st0", [P, TQ])
        cols = sb("cols", [P, 2, TQ])
        wsg, wsd = sb("wsg", [P, DC, 2 * FS]), sb("wsd", [P, FS // P, D])
        sth, sa = sb("sth", [P, L]), sb("sa", [P, L])
        shT = sb("shT", [P, FS // P, L])
        bank_g, bank_u = ps("rg", [P, L]), ps("ru", [P, L])
        bank_y = [ps(f"ry{i}", [P, 2, D]) for i in range(2)]
        bank_x = [ps(f"rx{i}", [P, 512]) for i in range(2)]
        bank_l = ps("rl", [P, TB, E])
        bank_r = ps("rr", [P, TB + 1, E])

        loaded, cast = s("rloaded"), s("rcast")
        w_in = s("rw_in")
        half_set = s("rhalf")
        step = s("rstep")
        var_ready = s("rvar")
        rstd_ready = s("rrstd_ready")
        xn_ready = s("rxn_ready")
        xT_mm = s("rxT_mm")
        xT_ready = s("rxT_ready")
        l_mm = s("rl_mm")
        th_ready = s("rth_ready")
        mask_ready = s("rmask_ready")
        rank_mm = s("rrank_mm")
        idx_ready = s("ridx_ready")
        sent = [s(f"rsent{i}") for i in range(2)]
        sg_mm = s("rsg_mm")
        sth_ready = s("rsth")
        sa_ready, sh_ready = s("rsa"), s("rsh")
        sy_mm = s("rsy_mm")
        added = s("radded")

        ln = s("rln")
        table_step = s("etable")
        pad_ready = s("epad_ready")
        padded = s("epadded")
        cols_ready = s("ecols")
        rows_mm, rows_ready = s("erows_mm"), s("erows")
        NSTEP = 27

        block = ctx.enter_context(nc.Block())

        @block.sync
        def _(sp):
            sp.dma_start(gw[:], gate_w.rearrange("(c p) e -> p c e", p=P)).then_inc(loaded, 16)
            sp.dma_start(gb[:], gate_b.unsqueeze(0).broadcast_to([P, E])).then_inc(loaded, 16)
            sp.dma_start(base[:], tab["base"]).then_inc(loaded, 16)
            sp.dma_start(before_f[:], tab["before"]).then_inc(loaded, 16)
            sp.dma_start(wsg[:], wsg_dram.rearrange("(c p) n -> p c n", p=P)).then_inc(loaded, 16)
            sp.dma_start(wsd[:], wsd_dram.rearrange("(c p) n -> p c n", p=P)).then_inc(loaded, 16)
            sp.dma_start(sidx[:], tab["sidx"]).then_inc(loaded, 16)
            w_of = w_exp[:].rearrange("p (e n) -> p e n", e=E)
            for c in range(DC):
                sp.dma_start(w_of[:, :, c * 2 * FI:(c + 1) * 2 * FI],
                             gu_dram[:, c * P:(c + 1) * P, :].rearrange("e p n -> p e n")).then_inc(w_in, 16)
            sp.dma_start(w_of[:, :, DC * 2 * FI:], dn_dram.rearrange("e p n -> p e n")).then_inc(w_in, 16)
            sp.wait_ge(cast, 1)
            sp.dma_start(xs_dram[E * CAP:E * CAP + P, :], zrow[:]).then_inc(padded, 16)
            sp.wait_ge(pad_ready, 1)
            with sp.Fori(0, E // 8) as j:
                for row in to_registers(nc, mybir.EngineType.SP, padu[0:1, bass.ds(j * 8, 8)]):
                    sp.dma_start(xs_dram[bass.ds(row, P), :], zrow[:]).then_inc(padded, 16)
            sp.wait_ge(padded, 16 * (E + 1))
            sp.wait_ge(w_in, 16 * (DC + 1))

        @block.gpsimd
        def _(pool):
            nc.gpsimd.memset(mhalf[:], -0.5).then_inc(half_set, 1)
            pool.wait_ge(half_set, 1)

            def scatter(n, p, roots_between=True):
                wait_alone(pool, idx_ready, n + 1)
                for i in range(TB):
                    for k in range(TOPK):
                        nc.gpsimd.indirect_dma_start(
                            xs_dram, bass.IndirectOffsetOnAxis(ap=idx[p][:, i, k:k + 1], axis=0),
                            xn[p][:, i, :], None).then_inc(sent[p], 16)
                        if i == 0 and k == 1 and roots_between:
                            roots(n + 1)

            def roots(n):
                pool.wait_ge(var_ready, n + 1)
                nc.gpsimd.tensor_tensor(rstd[:], ve[:], mhalf[:], ALU.pow).then_inc(rstd_ready, 1)

            roots(0)
            with pool.Fori(0, B // 2 - 1) as j:
                for p in range(2):
                    scatter(2 * j + p, p)
            scatter(B - 2, 0)
            scatter(B - 1, 1, roots_between=False)
            for p in range(2):
                pool.wait_ge(sent[p], 16 * TB * TOPK * (B // 2))

        @block.tensor
        def _(pe):
            pe.wait_ge(loaded, 112)
            pe.wait_ge(cast, 1)

            def shared_up(n, c):
                wait(pe, sh_ready, 2 * n + c)
                for bank, at in ((bank_g, c * P), (bank_u, FS + c * P)):
                    for k in range(DC):
                        mm = nc.tensor.matmul(bank[:, :], wsg[:, k, at:at + P], xT[:, k, :],
                                              start=k == 0, stop=k == DC - 1)
                mm.then_inc(sg_mm, 1)

            def shared_down(n):
                pe.wait_ge(sh_ready, 2 * n + 2)
                for j in range(2):
                    wait(pe, added, 2 * n + j - 1)
                    for i in range(2):
                        for c in range(FS // P):
                            mm = nc.tensor.matmul(bank_y[j][:, i, :], shT[:, c, (2 * j + i) * P:(2 * j + i + 1) * P],
                                                  wsd[:, c, :], start=c == 0, stop=c == FS // P - 1)
                    mm.then_inc(sy_mm, 1)

            def logits(n, p):
                pe.wait_ge(xn_ready, n + 1)
                for c in range(DC):
                    for i in range(TB):
                        mm = nc.tensor.transpose(bank_x[c][:, i * P:(i + 1) * P], xn[p][:, i, c * P:(c + 1) * P],
                                                 ident[:])
                    mm.then_inc(xT_mm, 1)
                pe.wait_ge(xT_ready, 2 * n + 2)
                for i in range(TB):
                    for c in range(DC):
                        mm = nc.tensor.matmul(bank_l[:, i, :], xT[:, c, i * P:(i + 1) * P], gw[:, c, :],
                                              start=c == 0, stop=c == DC - 1)
                mm.then_inc(l_mm, 1)

            def sequence(n, p, last=False):
                shared_up(n, 0)
                pe.wait_ge(mask_ready, n + 1)
                for i in range(TB + 1):
                    for k in range(min(i + 1, TB)):
                        mm = nc.tensor.matmul(bank_r[:, i, :], (before if k == i else ones)[:], maskb[:, k, :],
                                              start=k == 0, stop=k == min(i, TB - 1))
                mm.then_inc(rank_mm, 1)
                shared_up(n, 1)
                if not last:
                    logits(n + 1, (p + 1) % 2)
                shared_down(n)

            logits(0, 0)
            sequence(0, 0)
            sequence(1, 1)
            with pe.Fori(1, B // 2 - 1) as j:
                for p in range(2):
                    sequence(2 * j + p, p)
            sequence(B - 2, 0)
            sequence(B - 1, 1, last=True)
            pe.wait_ge(cols_ready, 1)
            for w in range(2):
                for q in range(TQ):
                    mm = nc.tensor.transpose(bank_x[w][0:1, q * TP:(q + 1) * TP], cols[0:TP, w, q:q + 1],
                                             ident[0:TP, 0:TP])
            mm.then_inc(rows_mm, 1)

        @block.scalar
        def _(act):
            def front(n):
                for c in range(DC):
                    act.wait_ge(xT_mm, 2 * n + c + 1)
                    nc.scalar.copy(xT[:, c, :], bank_x[c][:, :]).then_inc(xT_ready, 1)
                act.wait_ge(l_mm, n + 1)
                nc.scalar.activation(th[:], bank_l[:], ACT.Tanh, scale=0.5).then_inc(th_ready, 1)

            def squash(n):
                for c in range(FS // P):
                    act.wait_ge(sg_mm, 2 * n + c + 1)
                    nc.scalar.activation(sth[:], bank_g[:, :], ACT.Tanh, scale=0.5).then_inc(sth_ready, 1)

            front(0)
            with act.Fori(0, B - 1) as n:
                squash(n)
                front(n + 1)
            squash(B - 1)
            act.wait_ge(rows_mm, 1)
            for w in range(2):
                cp = nc.scalar.copy(rows[0:1, w, :].rearrange("p (j q) -> p j q", q=TQ),
                                    bank_x[w][0:1, 0:NSLOT].rearrange("p (q j) -> p j q", q=TQ))
            cp.then_inc(rows_ready, 1)

        @block.vector
        def _(dve):
            def x(n, i):
                return x_res[:, bass.ds(n * TB + i, 1), :].rearrange("p a d -> p (a d)")

            def variances(n):
                for i in range(TB):
                    st = nc.vector.bn_stats(stats[:, i, :], x(n, i))
                st.then_inc(ln, 1)
                wait_alone(dve, ln, 2 * n + 1)
                for i in range(TB):
                    st = nc.vector.bn_aggr(mv[:, i, :], stats[:, i, :])
                st.then_inc(ln, 1)
                dve.wait_ge(ln, 2 * n + 2)
                nc.vector.tensor_scalar_add(ve[:], mv[:, :, 1], EPS).then_inc(var_ready, 1)

            def scale(n, p, used):
                dve.wait_ge(rstd_ready, n + 1)
                wait(dve, sent[p], 16 * TB * TOPK * used)
                for i in range(TB):
                    st = nc.vector.tensor_scalar(xn[p][:, i, :], x(n, i), mv[:, i, 0:1], rstd[:, i:i + 1],
                                                 ALU.subtract, ALU.mult)
                st.then_inc(xn_ready, 1)

            class tick:

                def __init__(self, n):
                    self.n, self.k = n, 0

                def __call__(self, ins):
                    self.k += 1
                    ins.then_inc(step, 1)
                    wait_alone(dve, step, NSTEP * self.n + self.k)

            def choose(n, at):
                dve.wait_ge(th_ready, n + 1)
                at(nc.vector.tensor_scalar(score[:], th[:], 0.5, 0.5, ALU.mult, ALU.add))
                biased = vals[:, :, 0:E]
                at(nc.vector.tensor_tensor(biased, score[:], gb[:].unsqueeze(1).broadcast_to([P, TB, E]), ALU.add))
                groups = biased.rearrange("p t (g e) -> p t g e", g=NGROUP)
                at(nc.vector.tensor_reduce(gval[:, :, 0:NGROUP], groups, AX.X, ALU.max))
                for i in range(TB):
                    st = nc.vector.max(gtop[:, i, :], gval[:, i, :])
                at(st)
                at(nc.vector.tensor_copy(gtopr[:, :, 0:TOPG], gtop[:, :, 0:TOPG]))
                for i in range(TB):
                    st = nc.vector.match_replace(gvalr[:, i, :], gtopr[:, i, :], gval[:, i, :], HIGH)
                at(st)
                at(nc.vector.tensor_scalar(gmask[:], gvalr[:, :, 0:NGROUP], HIGH, None, ALU.is_ge))
                at(nc.vector.tensor_tensor(groups, groups, gmask[:].unsqueeze(3).broadcast_to([P, TB, NGROUP, EG]),
                                           ALU.mult))
                at(nc.vector.tensor_scalar_add(biased, biased, 0.0))
                for i in range(TB):
                    st = nc.vector.max(top[:, i, :], vals[:, i, :])
                at(st)
                at(nc.vector.tensor_copy(topr[:, :, 0:TOPK], top[:, :, 0:TOPK]))
                for i in range(TB):
                    st = nc.vector.match_replace(valr[:, i, :], topr[:, i, :], vals[:, i, :], HIGH)
                at(st)
                nc.vector.tensor_scalar(maskb[:], valr[:, :, 0:E], HIGH, None, ALU.is_ge).then_inc(mask_ready, 1)
                at(nc.vector.tensor_scalar(mask[:], valr[:, :, 0:E], HIGH, None, ALU.is_ge))

            def place(n, p, at, used):
                at(nc.vector.tensor_tensor(wsel[:], mask[:], score[:], ALU.mult))
                at(nc.vector.tensor_reduce(wsum[:], wsel[:], AX.X, ALU.add))
                at(nc.vector.tensor_scalar_add(wsum[:], wsum[:], 1e-20))
                at(nc.vector.reciprocal(wsum[:], wsum[:]))
                at(nc.vector.tensor_scalar_mul(wsum[:], wsum[:], ROUTE_SCALE))
                at(nc.vector.tensor_tensor(wsel[:], wsel[:], wsum[:].unsqueeze(2).broadcast_to([P, TB, E]), ALU.mult))
                dve.wait_ge(rank_mm, n + 1)
                at(nc.vector.tensor_tensor(slot[:], bank_r[:, 0:TB, :], run[:].unsqueeze(1).broadcast_to([P, TB, E]),
                                           ALU.add))
                nc.vector.tensor_tensor(run[:], bank_r[:, TB, :], run[:], ALU.add)
                at(nc.vector.tensor_tensor(slot[:], slot[:], mask[:], ALU.mult))
                for i in range(TB):
                    st = nc.vector.max(slot6[:, i, :], slot[:, i, :])
                at(st)
                wait(dve, sent[p], 16 * TB * TOPK * used)
                nc.vector.tensor_scalar_add(row_all[:, bass.ds(n * TB, TB), :], slot6[:, :, 0:TOPK], -1.0)
                nc.vector.tensor_scalar_add(idx[p][:], slot6[:, :, 0:TOPK], -1.0).then_inc(idx_ready, 1)

            def weights(n, at, tiles):
                for i in tiles:
                    for k in range(TOPK):
                        st = nc.vector.scalar_tensor_tensor(out=same[:, k, :], in0=slot[:, i, :],
                                                            scalar=slot6[:, i, k:k + 1], in1=wsel[:, i, :],
                                                            op0=ALU.is_equal, op1=ALU.mult,
                                                            accum_out=w6[:, i, k:k + 1])
                    at(st)
                if tiles[-1] == TB - 1:
                    at(nc.vector.tensor_copy(w_all[:, bass.ds(n * TB, TB), :], w6[:]))
                    assert at.k == NSTEP, at.k

            def shared_inner(n, c):
                dve.wait_ge(sth_ready, 2 * n + c + 1)
                nc.vector.scalar_tensor_tensor(out=sa[:], in0=sth[:], scalar=1.0, in1=bank_g[:, :],
                                               op0=ALU.add, op1=ALU.mult).then_inc(sa_ready, 1)
                dve.wait_ge(sa_ready, 2 * n + c + 1)
                nc.vector.scalar_tensor_tensor(out=shT[:, c, :], in0=sa[:], scalar=0.5, in1=bank_u[:, :],
                                               op0=ALU.mult, op1=ALU.mult).then_inc(sh_ready, 1)

            def shared_add(n):
                for j in range(2):
                    dve.wait_ge(sy_mm, 2 * n + j + 1)
                    x = x_res[:, bass.ds(n * TB + 2 * j, 2), :]
                    nc.vector.tensor_tensor(x, bank_y[j][:], x, ALU.add).then_inc(added, 1)

            def step_tables():
                k = [0]
                def done(ins):
                    k[0] += 1
                    ins.then_inc(table_step, 1)
                    dve.wait_ge(table_step, k[0])

                done(nc.vector.tensor_scalar_add(padf[:], run[:], -1.0))
                nc.vector.tensor_copy(padu[:], padf[:]).then_inc(pad_ready, 1)
                nc.vector.memset(one[:], 1.0)
                done(nc.vector.tensor_tensor(nt[:], run[:], base[:], ALU.subtract))
                done(nc.vector.tensor_scalar_add(cnt_i[:], nt[:], float(P - 1)))
                done(nc.vector.tensor_single_scalar(nt_i[:], cnt_i[:], P.bit_length() - 1, ALU.arith_shift_right))
                done(nc.vector.tensor_copy(nt[:], nt_i[:]))
                done(nc.vector.tensor_tensor_scan(ct[:], one[:], nt[:], 0.0, ALU.mult, ALU.add))
                done(nc.vector.tensor_tensor(le[:], ct[:].unsqueeze(1).broadcast_to([P, TQ, E]),
                                             sidx[:].unsqueeze(2).broadcast_to([P, TQ, E]), ALU.is_le))
                done(nc.vector.tensor_tensor(lt[:], le[:], nt[:].unsqueeze(1).broadcast_to([P, TQ, E]), ALU.mult))
                nc.vector.tensor_reduce(ex[:], le[:], AX.X, ALU.add)
                done(nc.vector.tensor_reduce(st0[:], lt[:], AX.X, ALU.add))
                done(nc.vector.tensor_tensor(st0[:], sidx[:], st0[:], ALU.subtract))
                done(nc.vector.tensor_scalar_mul(st0[:], st0[:], float(P)))
                done(nc.vector.scalar_tensor_tensor(out=st0[:], in0=ex[:], scalar=float(CAP), in1=st0[:],
                                                    op0=ALU.mult, op1=ALU.add))
                nc.vector.tensor_scalar_min(cols[:, 1, :], st0[:], float(E * CAP))
                nc.vector.tensor_scalar(cols[:, 0, :], ex[:], float(E - 1), float(WE), ALU.min,
                                        ALU.mult).then_inc(cols_ready, 1)
                nc.vector.tensor_scalar(shift[:], nt[:], float(P), float(-CAP), ALU.mult, ALU.add)

            def sequence(n, p, used, first=False, last=False):
                at = tick(n)
                choose(n, at)
                if not first:
                    shared_add(n - 1)
                shared_inner(n, 0)
                place(n, p, at, used)
                if not last:
                    variances(n + 1)
                weights(n, at, range(TB // 2))
                if not last:
                    scale(n + 1, (p + 1) % 2, used + p)
                weights(n, at, range(TB // 2, TB))
                shared_inner(n, 1)

            variances(0)
            dve.wait_ge(loaded, 112)
            nc.vector.memset(ones_f[:], 1.0)
            nc.vector.memset(zrow[:], 0.0)
            for marks in (vals, gval, gtopr, topr):
                nc.vector.memset(marks[:], LOW)
            nc.vector.tensor_copy(run[:], base[:])
            nc.vector.tensor_copy(before[:], before_f[:])
            nc.vector.memset(ones[:], 1.0).then_inc(cast, 1)
            dve.wait_ge(cast, 1)
            scale(0, 0, 0)
            sequence(0, 0, 0, first=True)
            sequence(1, 1, 0)
            with dve.Fori(1, B // 2 - 1) as j:
                for p in range(2):
                    sequence(2 * j + p, p, j)
            sequence(B - 2, 0, B // 2 - 1)
            sequence(B - 1, 1, B // 2 - 1, last=True)
            step_tables()
            shared_add(B - 1)
            dve.wait_ge(rows_ready, 1)


def experts(nc, sem, tag, ident, w_exp, rows, shift, row_all, idx_all, xs_dram, ys_dram):
    U = 28
    NB = 4
    J = NSLOT // U
    LAG = 8
    assert U % NB == 0 and LAG % NB == 0 and LAG <= U
    with ExitStack() as ctx:
        def sb(name, shape, dt=F32):
            return ctx.enter_context(nc.sbuf_tensor(f"{name}_{tag}", shape, dt))

        def ps(name, shape):
            return ctx.enter_context(nc.psum_tensor(f"{name}_{tag}", shape, F32))

        def s(name):
            return sem(f"{name}_{tag}")

        moved = [sb(f"moved{i}", [P, T * TOPK]) for i in range(2)]
        acc = [sb(f"acc{i}", [P, T * TOPK]) for i in range(2)]
        xt = [sb(f"ext{i}", [P, D]) for i in range(NB)]
        xT = [sb(f"exT{i}", [P, DC, P]) for i in range(2)]
        th = [sb(f"eth{i}", [P, FI]) for i in range(2)]
        a = [sb(f"ea{i}", [P, FI]) for i in range(2)]
        h = [sb(f"eh{i}", [P, FI]) for i in range(2)]
        hT = [sb(f"ehT{i}", [P, P]) for i in range(2)]
        y = [sb(f"ey{i}", [P, D]) for i in range(NB)]
        bx = [ps(f"ebx{i}", [P, DC, P]) for i in range(2)]
        bg = [ps(f"ebg{i}", [P, 2 * FI]) for i in range(2)]
        bh = [ps(f"ebh{i}", [P, P]) for i in range(2)]
        by = [ps(f"eby{i}", [P, D]) for i in range(2)]

        move = s("emove")
        x_in = [s(f"ex_in{i}") for i in range(NB)]
        y_out = [s(f"ey_out{i}") for i in range(NB)]
        xT_mm, xT_ready = s("exT_mm"), s("exT_ready")
        g_mm = s("eg_mm")
        th_ready = s("eth_ready")
        a_ready = s("ea_ready")
        h_ready = s("eh_ready")
        hT_mm, hT_ready = s("ehT_mm"), s("ehT_ready")
        y_mm, y_ready = s("ey_mm"), s("ey_ready")

        block = ctx.enter_context(nc.Block())

        @block.sync
        def _(sp):
            def load(s_, q, row):
                wait_alone(sp, xT_mm, s_ - NB + 1)
                sp.dma_start(xt[q % NB][:], xs_dram[bass.ds(row, P), :]).then_inc(x_in[q % NB], 16)

            def store(s_, q):
                wait_alone(sp, y_ready, s_ + 1)
                sp.dma_start(ys_dram[bass.ds(s_ * P, P), :], y[q % NB][:]).then_inc(y_out[q % NB], 16)

            def steps(j, first):
                row = to_registers(nc, mybir.EngineType.SP, rows[0:1, 1, bass.ds(j * U, U)])
                for q in range(U):
                    load(U * j + q, q, row[q])
                    if not first or q >= LAG:
                        store(U * j + q - LAG, q)

            steps(0, True)
            with sp.Fori(1, J) as j:
                steps(j, False)
            for s_ in range(NSLOT - LAG, NSLOT):
                store(s_, s_)
            for b in range(NB):
                sp.wait_ge(y_out[b], 16 * (NSLOT // NB))

        @block.gpsimd
        def _(pool):
            rows_f = row_all[:].rearrange("p t k -> p (t k)")
            for e in range(1, E):
                nc.gpsimd.tensor_scalar(moved[e % 2][:], rows_f, float(e * CAP), shift[:, e - 1:e],
                                        ALU.is_ge, ALU.mult).then_inc(move, 1)
                pool.wait_ge(move, 2 * e - 1)
                nc.gpsimd.tensor_tensor(acc[e % 2][:], moved[e % 2][:], rows_f if e == 1 else acc[(e - 1) % 2][:],
                                        ALU.add).then_inc(move, 1)
                pool.wait_ge(move, 2 * e)
            nc.gpsimd.tensor_copy(idx_all[:].rearrange("p t k -> p (t k)"), acc[(E - 1) % 2][:]).then_inc(move, 1)
            pool.wait_ge(move, 2 * E - 1)

        @block.tensor
        def _(pe):
            def up_t(s_, q, j):
                pe.wait_ge(x_in[q % NB], 16 * (U // NB * j + q // NB + 1))
                for c in range(DC):
                    mm = nc.tensor.transpose(bx[q % 2][:, c, :], xt[q % NB][:, c * P:(c + 1) * P], ident[:])
                mm.then_inc(xT_mm, 1)

            def up(s_, q, w):
                pe.wait_ge(xT_ready, s_ + 1)
                for c in range(DC):
                    mm = nc.tensor.matmul(bg[q % 2][:, :], xT[q % 2][:, c, :],
                                          w_exp[:, bass.ds(w + c * 2 * FI, 2 * FI)],
                                          start=c == 0, stop=c == DC - 1)
                mm.then_inc(g_mm, 1)

            def down_t(s_, q):
                pe.wait_ge(h_ready, s_ + 1)
                nc.tensor.transpose(bh[q % 2][:, :], h[q % 2][:], ident[:]).then_inc(hT_mm, 1)

            def down(s_, q, w):
                pe.wait_ge(hT_ready, s_ + 1)
                wait(pe, y_ready, s_ - 1)
                nc.tensor.matmul(by[q % 2][:, :], hT[q % 2][:],
                                 w_exp[:, bass.ds(w + DC * 2 * FI, D)],
                                 start=True, stop=True).then_inc(y_mm, 1)

            def steps(j, first, last):
                back = 0 if first else 2
                ws = to_registers(nc, mybir.EngineType.PE, rows[0:1, 0, bass.ds(j * U - back, U + back)])
                for q in range(U + 2 * last):
                    s_ = U * j + q
                    if q < U:
                        up(s_, q, ws[q + back])
                    if not (first and q < 1) and q < U + 1:
                        down_t(s_ - 1, q - 1)
                    if not last or q < U - 2:
                        up_t(s_ + 2, q + 2, j)
                    if not (first and q < 2):
                        down(s_ - 2, q - 2, ws[q - 2 + back])

            up_t(0, 0, 0)
            up_t(1, 1, 0)
            steps(0, True, False)
            with pe.Fori(1, J - 1) as j:
                steps(j, False, False)
            steps(J - 1, False, True)

        @block.scalar
        def _(act):
            def tokens(s_, q):
                act.wait_ge(xT_mm, s_ + 1)
                nc.scalar.copy(xT[q % 2][:], bx[q % 2][:]).then_inc(xT_ready, 1)

            def squash(s_, q):
                act.wait_ge(g_mm, s_ + 1)
                nc.scalar.activation(th[q % 2][:], bg[q % 2][:, 0:FI], ACT.Tanh, scale=0.5).then_inc(th_ready, 1)

            def output(s_, q, j):
                act.wait_ge(y_mm, s_ + 1)
                wait(act, y_out[q % NB], 16 * (U // NB * j + q // NB))
                nc.scalar.copy(y[q % NB][:], by[q % 2][:]).then_inc(y_ready, 1)

            def steps(j, first, last):
                for q in range(U + 2 * last):
                    s_ = U * j + q
                    if q < U:
                        squash(s_, q)
                    if not last or q < U - 2:
                        tokens(s_ + 2, q + 2)
                    if not (first and q < 2):
                        output(s_ - 2, q - 2, j)

            tokens(0, 0)
            tokens(1, 1)
            steps(0, True, False)
            steps(1, False, False)
            with act.Fori(2, J - 1) as j:
                steps(j, False, False)
            steps(J - 1, False, True)

        @block.vector
        def _(dve):
            def inner(s_, q):
                dve.wait_ge(th_ready, s_ + 1)
                nc.vector.scalar_tensor_tensor(out=a[q % 2][:], in0=th[q % 2][:], scalar=1.0, in1=bg[q % 2][:, 0:FI],
                                               op0=ALU.add, op1=ALU.mult).then_inc(a_ready, 1)
                dve.wait_ge(a_ready, s_ + 1)
                nc.vector.scalar_tensor_tensor(out=h[q % 2][:], in0=a[q % 2][:], scalar=0.5,
                                               in1=bg[q % 2][:, FI:2 * FI], op0=ALU.mult,
                                               op1=ALU.mult).then_inc(h_ready, 1)

            def turned(s_, q):
                dve.wait_ge(hT_mm, s_ + 1)
                nc.vector.tensor_copy(hT[q % 2][:], bh[q % 2][:]).then_inc(hT_ready, 1)

            def steps(j, first):
                for q in range(U):
                    s_ = U * j + q
                    if not (first and q < 1):
                        turned(s_ - 1, q - 1)
                    inner(s_, q)

            steps(0, True)
            with dve.Fori(1, J) as j:
                steps(j, False)
            turned(NSLOT - 1, NSLOT - 1)


def combine(nc, sem, tag, x_res, ys_dram, idx_all, w_all, out_dram):
    NB = 2
    with ExitStack() as ctx:
        def sb(name, shape, dt=F32):
            return ctx.enter_context(nc.sbuf_tensor(f"{name}_{tag}", shape, dt))

        def s(name):
            return sem(f"{name}_{tag}")

        yg = [sb(f"cyg{i}", [P, TOPK, D]) for i in range(NB)]
        idx = [sb(f"cidx{i}", [P, TOPK], U32) for i in range(NB)]

        idx_ready = s("cidx_ready")
        got = [s(f"cgot{i}") for i in range(NB)]
        added = s("cadded")
        stored = s("cstored")

        block = ctx.enter_context(nc.Block())

        @block.sync
        def _(sp):
            with sp.Fori(0, T) as t:
                wait_alone(sp, added, TOPK * t + TOPK)
                sp.dma_start(out_dram[bass.ds(t * P, P), :],
                             x_res[:, bass.ds(t, 1), :].rearrange("p a d -> p (a d)")).then_inc(stored, 16)
            sp.wait_ge(stored, 16 * T)

        @block.gpsimd
        def _(pool):
            with pool.Fori(0, T // NB) as j:
                for p in range(NB):
                    wait_alone(pool, idx_ready, NB * j + p + 1)
                    for k in range(TOPK):
                        nc.gpsimd.indirect_dma_start(yg[p][:, k, :], None, ys_dram,
                                                     bass.IndirectOffsetOnAxis(ap=idx[p][:, k:k + 1], axis=0)
                                                     ).then_inc(got[p], 16)

        @block.vector
        def _(dve):
            def rows(t, p, j):
                nc.vector.tensor_copy(idx[p][:], idx_all[:, bass.ds(t, 1), :].rearrange("p a k -> p (a k)")
                                      ).then_inc(idx_ready, 1)

            def tile(t, p, j):
                x = x_res[:, bass.ds(t, 1), :].rearrange("p a d -> p (a d)")
                dve.wait_ge(got[p], 16 * TOPK * (j + 1))
                for k in range(TOPK):
                    wait(dve, added, TOPK * t + k)
                    weight = w_all[:, bass.ds(t, 1), k:k + 1].rearrange("p a k -> p (a k)")
                    nc.vector.scalar_tensor_tensor(out=x, in0=yg[p][:, k, :], scalar=weight, in1=x,
                                                   op0=ALU.mult, op1=ALU.add).then_inc(added, 1)
                dve.wait_ge(added, TOPK * (t + 1))

            for p in range(NB):
                rows(p, p, 0)
            for p in range(NB):
                tile(p, p, 0)
                rows(p + NB, p, 1)
            with dve.Fori(1, T // NB - 1) as j:
                for p in range(NB):
                    tile(NB * j + p, p, j)
                    rows(NB * j + p + NB, p, j + 1)
            for p in range(NB):
                tile(T - NB + p, p, T // NB - 1)


@contextmanager
def phase(nc):
    sems = []

    def sem(name):
        sems.append(nc.alloc_semaphore(name=name))
        return sems[-1]

    yield sem
    nc.clear_and_free_semaphores(sems)
    nc.all_engine_barrier()


def hybrid_kernel(nc, ins, out):
    with ExitStack() as ctx:
        def sb(name, shape, dt=F32):
            return ctx.enter_context(nc.sbuf_tensor(name, shape, dt))

        def dram(name, shape):
            return nc.dram_tensor(name, shape, F32, kind="Internal").ap()

        x_res = sb("x_res", [P, T, D])
        ident = sb("ident", [P, P])
        identb = sb("identb", [P, P], BF16)
        maskb = sb("maskb", [P, 2, P], BF16)
        qk_dram = [dram(f"qk{i}", [H, 3, HD, L]) for i in range(3)]
        m_dram = dram("m", [HG * TB, 2, P])
        kv_dram = [dram(f"kv{i}", [D, D]) for i in range(2)]
        scratch = {n: dram(n, ins[n].shape) for n in ("krow", "alibi", "ones")}
        xs_dram = dram("xs", [XROWS, D])
        ys_dram = dram("ys", [YROWS, D])

        def ffn(tag, idx_all, w_all):
            with ExitStack() as own:
                def own_sb(name, shape, dt=F32):
                    return own.enter_context(nc.sbuf_tensor(f"{name}_{tag}", shape, dt))

                zrow, run, row_all = own_sb("zrow", [P, D]), own_sb("run", [P, E]), own_sb("row_all", [P, T, TOPK])
                rows, shift = own_sb("rows", [1, 2, NSLOT], U32), own_sb("shift", [P, E])
                w_exp = own_sb("w_exp", [P, E * WE])
                with phase(nc) as sem:
                    route(nc, sem, tag, x_res, ident, ins["gate"], ins["bias"], ins, xs_dram, run, row_all,
                          w_all, w_exp, ins["gu"], ins["dn"], ins["wsg"], ins["wsd"], zrow, rows, shift)
                with phase(nc) as sem:
                    experts(nc, sem, tag, ident, w_exp, rows, shift, row_all, idx_all, xs_dram, ys_dram)

        tables = {**ins, **scratch, "scratch": list(scratch), "kv": kv_dram}
        with phase(nc) as sem:
            attention(nc, sem, False, x_res, ident, identb, maskb, [ins[n] for n in ("a_wq", "a_wk", "a_wv", "a_wo")],
                      tables, [qk_dram[0], qk_dram[2]], m_dram, begin=ins)
        with ExitStack() as chosen:
            idx_all = chosen.enter_context(nc.sbuf_tensor("idx_all", [P, T, TOPK], U32))
            w_all = chosen.enter_context(nc.sbuf_tensor("w_all", [P, T, TOPK], F32))
            ffn("1", idx_all, w_all)
            with phase(nc) as sem:
                attention(nc, sem, True, x_res, ident, identb, maskb,
                          [ins["b_wq"], kv_dram[0], kv_dram[1], ins["b_wo"]],
                          tables, qk_dram, m_dram, (ys_dram, idx_all, w_all))
            ffn("2", idx_all, w_all)
            with phase(nc) as sem:
                combine(nc, sem, "2", x_res, ys_dram, idx_all, w_all, out.rearrange("b l d -> (b l) d"))


def split12(a):
    high = (a.astype(np.float32).view(np.uint32) & np.uint32(0xFFFFF000)).view(np.float32)
    return high, (a - high).astype(np.float32)


def constants():
    j, p = np.arange(L), np.arange(P)
    mid = L / 2
    slope = (2.0 ** (-8.0 / H)) ** (np.arange(H) + 1)
    t = {"ident": np.eye(P), "alibi": np.stack(split12(slope[:, None] * (j[None, :] - mid)))}
    t["krow"], t["ones"] = np.zeros((8, L)), np.ones((2, L))
    for f, sign in ((0, -1.0), (1, 1.0)):
        high, low = split12(np.exp(sign * LDECAY * (j - mid)))
        t["krow"][4 * f:4 * f + 4] = [high, low, low, high]
    t["cwin"] = np.zeros((P, L))
    t["cwin"][:, L - P:] = np.where(p[None, :] <= p[:, None], 0.0, NEG)
    t["efac"] = np.broadcast_to(np.stack([np.exp(-LDECAY * (j - mid)), np.exp(LDECAY * (j - mid))]) / 16.0, (P, 2, L))
    t["dwin"] = np.exp(-LDECAY * np.abs(p[:, None] - (np.arange(7 * P) - 3 * P)[None, :]))
    at = p[:, None] + P * np.arange(TB)[None, :] - mid
    t["sfac"] = np.stack([np.exp(LDECAY * at), np.exp(-LDECAY * at)], 1)
    t["mfac"] = np.exp(LDECAY * at)
    t["mask"] = np.stack([np.where(p[None, :] >= p[:, None], 0.0, NEG), np.where(p[None, :] < p[:, None], 0.0, NEG)], 1)
    t["base"] = np.broadcast_to(np.arange(E) * CAP + 1.0, (P, E))
    t["before"] = p[:, None] < p[None, :]
    t["sidx"] = TQ * p[:, None] + np.arange(TQ)[None, :]
    return {k: np.ascontiguousarray(a, np.float32) for k, a in t.items()}


def kernel(**inputs):
    import concourse.bacc as bacc
    from concourse.bass_utils import run_bass_kernel_spmd

    def turned(a, *axes):
        return np.ascontiguousarray(np.transpose(a, axes))

    i = {k: np.asarray(a) for k, a in inputs.items()}
    arrays = {
        "x": i["L0_attn_a_x"],
        "a_wq": i["L0_attn_a_q_w"], "a_wk": i["L0_attn_a_k_w"], "a_wv": i["L0_attn_a_v_w"], "a_wo": i["L0_attn_a_o_w"],
        "b_wq": i["L0_attn_b_W_q"], "b_wo": i["L0_attn_b_W_o"],
        "wkT": turned(i["L0_attn_b_W_k"], 1, 0), "wvT": turned(i["L0_attn_b_W_v"], 1, 0),
        "wdown": i["L0_attn_b_W_down_kv"], "wupk": i["L0_attn_b_W_up_k"], "wupv": i["L0_attn_b_W_up_v"],
        "gate": turned(i["L0_ffn_gate_weight"], 1, 0), "bias": i["L0_ffn_e_score_correction_bias"],
        "gu": turned(i["L0_ffn_experts_gate_up"], 0, 2, 1), "dn": turned(i["L0_ffn_experts_down"], 0, 2, 1),
        "wsg": np.concatenate([turned(i["L0_ffn_shared_gate_w"], 1, 0), turned(i["L0_ffn_shared_up_w"], 1, 0)], 1),
        "wsd": turned(i["L0_ffn_shared_down_w"], 1, 0),
        **constants(),
    }
    nc = bacc.Bacc("TRN2", target_bir_lowering=False, num_devices=1)
    ins = {k: nc.dram_tensor(f"in_{k}", a.shape, mybir.dt.from_np(a.dtype), kind="ExternalInput").ap()
           for k, a in arrays.items()}
    out = nc.dram_tensor("out", (B, L, D), F32, kind="ExternalOutput").ap()
    hybrid_kernel(nc, ins, out)
    r = run_bass_kernel_spmd(nc, [{f"in_{k}": np.ascontiguousarray(a) for k, a in arrays.items()}], core_ids=[0])
    return r.results[0]["out"]
```
